# Optimizing a Trainium2 kernel written in Bass

```python
import numpy as np
import jax
import jax.numpy as jnp

def _softmax(x, axis=-1):
    return jax.nn.softmax(x, axis=axis)

def _gelu(x):
    return jax.nn.gelu(x, approximate=True)

def _silu(x):
    return jax.nn.silu(x)

def _sigmoid(x):
    return jax.nn.sigmoid(x)

def _layernorm(x, axis=-1, eps=1e-05):
    m = jnp.mean(x, axis=axis, keepdims=True)
    v = jnp.var(x, axis=axis, keepdims=True)
    return (x - m) / jnp.sqrt(v + eps)

def _scatter_add(tgt, idx, src, axis=0):
    return tgt.at[idx].add(src)

def _segment_sum(src, seg, n):
    return jax.ops.segment_sum(src, seg, n)
kernel_name = 'mk_flamingo_gated_d2_seqx_r8_65da0b'

def setup_inputs(seed: int=0):
    np.random.seed(seed)
    _w = jnp.asarray

    def _rec_inputs():
        import jax
        import jax.numpy as jnp
        _rk = jax.random.key(seed)
        x = -0.0005207 + 1.001 * jax.random.normal(jax.random.fold_in(_rk, 1), (32, 64, 256), jnp.float32)
        _lenS = 64 - jax.random.randint(jax.random.fold_in(_rk, 7), (32,), 0, max(1, 64 // 4) + 1, jnp.int32)
        _lenS2 = 64 - jax.random.randint(jax.random.fold_in(_rk, 8), (32,), 0, max(1, 64 // 4) + 1, jnp.int32)
        _ctx_2048P = jax.random.normal(jax.random.fold_in(_rk, 11), (32, 16, 256), jnp.float32)
        _ctx_2048c = jax.random.dirichlet(jax.random.fold_in(_rk, 511), 0.3 * jnp.ones((16,), jnp.float32), (32, 64))
        _ctx_2048t = jnp.einsum('bsk,bkd->bsd', _ctx_2048c, _ctx_2048P)
        _ctx_2048t = _ctx_2048t * jax.lax.rsqrt(jnp.mean(jnp.square(_ctx_2048t)) + 1e-12) * 0.953939
        ctx_2048 = -0.000514642 + 1.00011 * (_ctx_2048t + 0.3 * jax.random.normal(jax.random.fold_in(_rk, 611), (32, 64, 256), jnp.float32))
        _validS = jnp.arange(64)[None, :] < _lenS[:, None]
        _validS2 = jnp.arange(64)[None, :] < _lenS2[:, None]
        _causal = jnp.tril(jnp.ones((64, 64), dtype=bool))
        mask_Bx2048x2048_ff0 = jnp.where(jnp.ones((32, 256, 256), dtype=bool), 0.0, -1000000000.0).astype(jnp.float32)
        mask_BxS2_bk0 = jnp.logical_not(jnp.broadcast_to(_validS2[:, :], (32, 64)))
        _g = jax.random.normal(jax.random.fold_in(_rk, 9001), (2, 2), jnp.float32)
        _g = jnp.sign(_g) * jnp.maximum(jnp.abs(_g), 1.0) + (_g == 0) * 1.0
        g_xattn = _g[0]
        g_ffn = _g[1]
        return (x, ctx_2048, mask_Bx2048x2048_ff0, mask_BxS2_bk0, g_xattn, g_ffn)
    x, ctx_2048, mask_Bx2048x2048_ff0, mask_BxS2_bk0, g_xattn, g_ffn = _rec_inputs()

    def _L0_xattn_setup():
        import jax, jax.numpy as jnp
        import numpy as np
        import math
        D_MODEL = 64
        NUM_HEAD = 8
        D_HEAD = D_MODEL // NUM_HEAD

        def _proj_heads(x, W, b):
            y = jnp.einsum('oc,bcl->bol', W, x) + b[None, :, None]
            B, C, L = y.shape
            return y.reshape(B, NUM_HEAD, D_HEAD, L).transpose(0, 1, 3, 2)
        key = jax.random.key(seed)
        ks = jax.random.split(key, 8)
        B, C, N, M = (2, D_MODEL, 256, 256)
        s = 1.0 / math.sqrt(C)
        return {'input_q': jax.random.normal(ks[0], (B, C, N), dtype=jnp.float32), 'input_k': jax.random.normal(ks[1], (B, C, M), dtype=jnp.float32), 'input_v': jax.random.normal(ks[2], (B, C, M), dtype=jnp.float32), 'key_masks': jnp.zeros((B, N, M), dtype=jnp.float32), 'Wq': jax.random.normal(ks[3], (C, C), dtype=jnp.float32) * s, 'bq': jnp.zeros((C,), dtype=jnp.float32), 'Wk': jax.random.normal(ks[4], (C, C), dtype=jnp.float32) * s, 'bk': jnp.zeros((C,), dtype=jnp.float32), 'Wv': jax.random.normal(ks[5], (C, C), dtype=jnp.float32) * s, 'bv': jnp.zeros((C,), dtype=jnp.float32)}
    _L0_xattn_all = _L0_xattn_setup()
    _L0_xattn_in = {k: v for k, v in _L0_xattn_all.items() if k in ('Wq', 'bq', 'Wk', 'bk', 'Wv', 'bv')}
    del _L0_xattn_all

    def _L0_ffn_setup():
        import jax, jax.numpy as jnp
        import numpy as np
        TOP_P = 0.9
        S, B, H, I, E = (256, 4, 256, 512, 8)

        def _top_p_weights(probs, top_p):
            order = jnp.argsort(-probs, axis=-1)
            sp = jnp.take_along_axis(probs, order, axis=-1)
            cum = jnp.cumsum(sp, axis=-1)
            exceed = cum > top_p
            first_idx = jnp.argmax(exceed, axis=-1)
            first = jnp.arange(probs.shape[-1])[None, :] == first_idx[:, None]
            keep = ~exceed | first
            kept = jnp.where(keep, sp, 0.0)
            t_idx = jnp.arange(probs.shape[0])[:, None]
            return jnp.zeros_like(probs).at[t_idx, order].set(kept)
        key = jax.random.key(seed)
        ks = jax.random.split(key, 5)
        scale = 0.02
        return {'hidden_states': jax.random.normal(ks[0], (S, B, H), dtype=jnp.float32), 'router_w': jax.random.normal(ks[1], (E, H), dtype=jnp.float32) * scale, 'gate_w': jax.random.normal(ks[2], (E, I, H), dtype=jnp.float32) * scale, 'up_w': jax.random.normal(ks[3], (E, I, H), dtype=jnp.float32) * scale, 'down_w': jax.random.normal(ks[4], (E, H, I), dtype=jnp.float32) * scale}
    _L0_ffn_all = _L0_ffn_setup()
    _L0_ffn_in = {k: v for k, v in _L0_ffn_all.items() if k in ('router_w', 'gate_w', 'up_w', 'down_w')}
    del _L0_ffn_all

    def _L1_xattn_setup():
        import jax, jax.numpy as jnp
        import numpy as np
        key = jax.random.key(seed)
        k1, k2, k3 = jax.random.split(key, 3)
        B, S, D, M = (8, 256, 256, 128)
        hidden_states = jax.random.normal(k1, (B, S, D), dtype=jnp.float32)
        memory_tokens = jax.random.normal(k2, (B, M, D), dtype=jnp.float32)
        memory_mask = jax.random.randint(k3, (B, M), 0, 2).astype(jnp.bool_)
        return {'hidden_states': hidden_states, 'memory_tokens': memory_tokens, 'memory_mask': memory_mask}
    _L1_xattn_all = _L1_xattn_setup()
    _L1_xattn_in = {k: v for k, v in _L1_xattn_all.items() if k in ()}
    del _L1_xattn_all

    def _L1_ffn_setup():
        import jax, jax.numpy as jnp
        import numpy as np
        NUM_EXPERTS = 4
        key = jax.random.key(seed)
        k1, k2, k3 = jax.random.split(key, 3)
        B, N, H = (8, 256, 256)
        E = NUM_EXPERTS
        I = H * 4 // E
        x = jax.random.normal(k1, (B, N, H), dtype=jnp.float32)
        gate_up_proj = jax.random.normal(k2, (E, H, 2 * I), dtype=jnp.float32) * 0.02
        down_proj = jax.random.normal(k3, (E, I, H), dtype=jnp.float32) * 0.02
        return {'x': x, 'gate_up_proj': gate_up_proj, 'down_proj': down_proj}
    _L1_ffn_all = _L1_ffn_setup()
    _L1_ffn_in = {k: v for k, v in _L1_ffn_all.items() if k in ('gate_up_proj', 'down_proj')}
    del _L1_ffn_all
    return {'x': x, 'ctx_2048': ctx_2048, 'mask_Bx2048x2048_ff0': mask_Bx2048x2048_ff0, 'mask_BxS2_bk0': mask_BxS2_bk0, 'g_xattn': g_xattn, 'g_ffn': g_ffn, 'L0_xattn_Wq': _L0_xattn_in['Wq'], 'L0_xattn_bq': _L0_xattn_in['bq'], 'L0_xattn_Wk': _L0_xattn_in['Wk'], 'L0_xattn_bk': _L0_xattn_in['bk'], 'L0_xattn_Wv': _L0_xattn_in['Wv'], 'L0_xattn_bv': _L0_xattn_in['bv'], 'L0_ffn_router_w': _L0_ffn_in['router_w'], 'L0_ffn_gate_w': _L0_ffn_in['gate_w'], 'L0_ffn_up_w': _L0_ffn_in['up_w'], 'L0_ffn_down_w': _L0_ffn_in['down_w'], 'L1_ffn_gate_up_proj': _L1_ffn_in['gate_up_proj'], 'L1_ffn_down_proj': _L1_ffn_in['down_proj']}

def reference(x, ctx_2048, mask_Bx2048x2048_ff0, mask_BxS2_bk0, g_xattn, g_ffn, L0_xattn_Wq, L0_xattn_bq, L0_xattn_Wk, L0_xattn_bk, L0_xattn_Wv, L0_xattn_bv, L0_ffn_router_w, L0_ffn_gate_w, L0_ffn_up_w, L0_ffn_down_w, L1_ffn_gate_up_proj, L1_ffn_down_proj):
    import jax
    import jax.numpy as jnp

    def _L0_xattn_ref(input_q, input_k, input_v, key_masks, Wq, bq, Wk, bk, Wv, bv):
        import jax, jax.numpy as jnp
        import numpy as np
        import math
        D_MODEL = 64
        NUM_HEAD = 8
        D_HEAD = D_MODEL // NUM_HEAD

        def _proj_heads(x, W, b):
            y = jnp.einsum('oc,bcl->bol', W, x) + b[None, :, None]
            B, C, L = y.shape
            return y.reshape(B, NUM_HEAD, D_HEAD, L).transpose(0, 1, 3, 2)
        q = _proj_heads(input_q, Wq, bq)
        k = _proj_heads(input_k, Wk, bk)
        v = _proj_heads(input_v, Wv, bv)
        scores = jnp.einsum('bhnd,bhmd->bhnm', q, k) / math.sqrt(D_HEAD)
        scores = scores + key_masks[:, None, :, :]
        attn = jax.nn.softmax(scores, axis=-1)
        out = jnp.einsum('bhnm,bhmd->bhnd', attn, v)
        B, H, N, Dh = out.shape
        return out.transpose(0, 1, 3, 2).reshape(B, D_MODEL, N)

    def _L0_ffn_ref(hidden_states, router_w, gate_w, up_w, down_w):
        import jax, jax.numpy as jnp
        import numpy as np
        TOP_P = 0.9
        S, B, H, I, E = (256, 4, 256, 512, 8)

        def _top_p_weights(probs, top_p):
            order = jnp.argsort(-probs, axis=-1)
            sp = jnp.take_along_axis(probs, order, axis=-1)
            cum = jnp.cumsum(sp, axis=-1)
            exceed = cum > top_p
            first_idx = jnp.argmax(exceed, axis=-1)
            first = jnp.arange(probs.shape[-1])[None, :] == first_idx[:, None]
            keep = ~exceed | first
            kept = jnp.where(keep, sp, 0.0)
            t_idx = jnp.arange(probs.shape[0])[:, None]
            return jnp.zeros_like(probs).at[t_idx, order].set(kept)
        s, b, h = hidden_states.shape
        x = hidden_states.reshape(-1, h)
        probs = jax.nn.softmax(x @ router_w.T, axis=-1)
        w = _top_p_weights(probs, TOP_P)
        out = jnp.zeros_like(x)
        n_exp = router_w.shape[0]
        for e in range(n_exp):
            g = jax.nn.silu(x @ gate_w[e].T)
            u = x @ up_w[e].T
            y = g * u @ down_w[e].T
            out = out + y * w[:, e:e + 1]
        return out.reshape(s, b, h)

    def _L1_xattn_ref(hidden_states, memory_tokens, memory_mask):
        import jax, jax.numpy as jnp
        import numpy as np
        B, S, D = hidden_states.shape
        scale = 1.0 / jnp.sqrt(jnp.asarray(D, hidden_states.dtype))
        scores = jnp.einsum('bsd,bmd->bsm', hidden_states, memory_tokens) * scale
        neg_inf = jnp.asarray(-1e+30, scores.dtype)
        scores = jnp.where(memory_mask[:, None, :], scores, neg_inf)
        attn = jax.nn.softmax(scores, axis=-1)
        readout = jnp.einsum('bsm,bmd->bsd', attn, memory_tokens)
        valid_b = jnp.any(memory_mask, axis=-1)
        out = jnp.where(valid_b[:, None, None], readout, jnp.zeros_like(readout))
        return out

    def _L1_ffn_ref(x, gate_up_proj, down_proj):
        import jax, jax.numpy as jnp
        import numpy as np
        NUM_EXPERTS = 4
        B, N, H = x.shape
        E, _, two_I = gate_up_proj.shape
        I = two_I // 2
        G = N // E
        x4 = x.reshape(B, G, E, H)
        gu = jnp.einsum('bgeh,ehd->bged', x4, gate_up_proj)
        gate, up = (gu[..., :I], gu[..., I:])
        inter = jax.nn.silu(gate) * up
        out = jnp.einsum('bgei,eih->bgeh', inter, down_proj)
        return out.reshape(B, N, H)
    x = x + jnp.tanh(g_xattn[0]) * _L0_xattn_ref(_layernorm(x, axis=-1), ctx_2048, ctx_2048, mask_Bx2048x2048_ff0, L0_xattn_Wq, L0_xattn_bq, L0_xattn_Wk, L0_xattn_bk, L0_xattn_Wv, L0_xattn_bv)
    x = x + jnp.tanh(g_ffn[0]) * _L0_ffn_ref(_layernorm(x, axis=-1), L0_ffn_router_w, L0_ffn_gate_w, L0_ffn_up_w, L0_ffn_down_w)
    x = x + jnp.tanh(g_xattn[1]) * _L1_xattn_ref(_layernorm(x, axis=-1), ctx_2048, mask_BxS2_bk0)
    x = x + jnp.tanh(g_ffn[1]) * _L1_ffn_ref(_layernorm(x, axis=-1), L1_ffn_gate_up_proj, L1_ffn_down_proj)
    return x

_drawn_inputs = setup_inputs


def setup_inputs(seed=0):
    import zlib

    import numpy as np

    out = dict(_drawn_inputs(seed))
    spreads = {'g_ffn': (-1.0, 0.6),
     'L0_xattn_bq': (0.0, 0.384),
     'L0_xattn_bk': (0.0, 2.0),
     'L0_xattn_bv': (0.0, 0.8)}
    factors = {'L0_ffn_router_w': 8.0,
     'L0_ffn_gate_w': 8.0,
     'L0_ffn_up_w': 8.0,
     'L0_ffn_down_w': 8.0,
     'L1_ffn_gate_up_proj': 4.885,
     'L1_ffn_down_proj': 4.89}
    for name, (base, spread) in spreads.items():
        noise = np.random.default_rng([zlib.crc32(name.encode()), seed]).standard_normal(out[name].shape)
        drawn = base * np.exp(spread * noise) if base else spread * noise
        out[name] = jnp.asarray(drawn.astype(out[name].dtype))
    for name, factor in factors.items():
        out[name] = (out[name] * factor).astype(out[name].dtype)
    return out
```

```python
from contextlib import ExitStack

import concourse.bass as bass
from concourse import mybir

F32 = mybir.dt.float32
BF16 = mybir.dt.bfloat16
F16 = mybir.dt.float16
U8 = mybir.dt.uint8
ALU = mybir.AluOpType
ACT = mybir.ActivationFunctionType
AX = mybir.AxisListType

B, S, D = 32, 64, 256
P = 128
NPAIR = B * S // P
H, DH = 8, 8
NE, NI = 8, 512
NE1, NI1 = 4, 256
ROUNDS = B // 4
TILE = 512
KT = D // P
IB = NI // P
IB1 = NI1 // P
UNITS = 4 * IB
VC = 3 * DH + 1
SROW = 7 * DH
EPS = 1e-5
ROUND_STEPS = 50
LATE_STEPS = 15
W_SCALE = 64.0
X_SCALE = 256.0
G_UNSCALE = 1.0 / (W_SCALE * X_SCALE)
LN_P_SCALE = 12 * 0.6931471805599453
LOW = -3.0e38


class Steps:

    def __init__(self, eng, sem, met):
        self.eng, self.sem, self.met, self.n, self.base = eng, sem, met, 0, 0

    def at(self, base):
        self.base, self.n = base, 0

    def apart(self):
        self.eng.sem_inc(self.met, 1)

    def link(self, instruction):
        self.n += 1
        instruction.then_inc(self.sem, 1)
        self.eng.wait_ge(self.sem, self.base + self.n)


def build(nc, A, out):
    ctx = ExitStack()

    def sb(name, shape, dt):
        return ctx.enter_context(nc.sbuf_tensor(name, shape, dt))

    def sem(name):
        return ctx.enter_context(nc.semaphore(name))

    x_d = A["x"].rearrange("(p b) s d -> (b s) p d", b=2)
    ctx_d = A["ctx_2048"].rearrange("(p b) s d -> p (b s) d", b=2)
    mask_d = A["mask_Bx2048x2048_ff0"].rearrange("b (t n) m -> b n t m", t=2)
    out_d = out.rearrange("(p b) s d -> p (b s) d", b=2)
    part_d = nc.dram_tensor("part_scratch", (2, 2, 3, P, D), BF16, kind="Internal").ap()
    tokw_d = nc.dram_tensor("tokw_scratch", (2, NE, TILE), F32, kind="Internal").ap()

    with ctx:
        ident = sb("ident", [P, P], F32)
        ident_b = sb("ident_b", [P, P], BF16)
        minus_half = sb("minus_half", [P, NPAIR], F32)
        gates = sb("gates", [P, 4], F32)
        gate_in = sb("gate_in", [P, 4], F32)
        x_res = sb("x_res", [P, NPAIR, D], F32)
        stats = sb("stats", [P, 6], F32)
        mean_var = sb("mean_var", [P, NPAIR, 2], F32)
        rstd = sb("rstd", [P, NPAIR], F32)
        mv2 = sb("mv2", [P, 2], F32)
        ve2 = sb("ve2", [P, 1], F32)
        rstd2 = sb("rstd2", [P, 1], F32)
        xn = sb("xn", [P, D], F32)
        th = sb("th", [P, TILE], F32)
        ga = sb("ga", [P, TILE], F32)
        uw = sb("uw", [P, TILE], F32)
        h32 = sb("h32", [P, TILE], F32)
        hp_hi = sb("hp_hi", [P, 2, TILE], F16)
        hp_lo = sb("hp_lo", [P, 2, TILE], F16)
        yT = sb("yT", [P, 2, TILE], F32)

        psG = ctx.enter_context(nc.psum_tensor("psG", [P, 512], F32))
        psU = ctx.enter_context(nc.psum_tensor("psU", [P, 512], F32))
        psY = ctx.enter_context(nc.psum_tensor("psY", [P, 2, 512], F32))
        ps1 = ctx.enter_context(nc.psum_tensor("ps1", [P, 2, 256], F32))
        ps2 = ctx.enter_context(nc.psum_tensor("ps2", [P, 512], F32))
        psV = ctx.enter_context(nc.psum_tensor("psV", [P, 512], F32))
        psM = ctx.enter_context(nc.psum_tensor("psM", [P, 512], F32))

        lnscale = sb("lnscale", [P, 1], F32)

        names = """x_loaded small_loaded stage0_loaded stage1_loaded stage2_loaded
            ctx0_loaded ctx1_loaded mask0_loaded mask1_loaded parts_stored stack_loaded
            max_rows_loaded tokw_stored wb0_loaded wb1_loaded out_stored consts_ready stage_zeroed exp_bias_set
            gates_ready v_copied x1_done lg_done y_added sc_read x3_done d_upT wst_T router_T wgrp_T w_hi w_split bias_ready
            ln_in pow_done xn_ready qk_projected v_projected qk_copied qk_split v_split
            maskT_ready maskT_copied scores1_done max_done max_split maxT_ready maxT_copied
            scores2_done masked_done exp_done phi_done plo_done pv_done pv_evac on_ready onT_ready
            xn2_ready xn2T_ready xt_hi xt_split router_done logits_done route_exp w_ready
            wT_ready wrow_ready gate_ready up_ready tanh_done gate_used up_used h_mul h_hi h_split
            down_done y_evac yT_T dve_step dve_apart pe_apart sp_apart
            d_loaded dw_hi dw_split xt3_done ctxT_done sc_done sc_masked c_exp pT_ready pT_done
            read_done xn4T xn4_hi xn4_split cx_loaded d_gate d_up d_tanh d_mul d_hi d_split d_down d_yevac
            d_yT d_out xn3_ready xn3T cxT mask_m_loaded mask_m_ready xn4_ready""".split()
        s = {n: sem(n) for n in names}

        early = ExitStack()

        def eb(name, shape, dt):
            return early.enter_context(nc.sbuf_tensor(name, shape, dt))

        w_gu = eb("w_gu", [P, 2, NE, 2, KT, NI], F16)
        w_dn = eb("w_dn", [P, 2, NE, IB, D], F16)
        w_rt = eb("w_rt", [P, KT, 2 * NE], F16)
        xT = eb("xT", [P, 2, 2, KT, TILE], F16)
        wb = eb("wb", [P, 2, TILE], F32)
        wrow = eb("wrow", [NE, P], F32)
        w_bd = eb("w_bd", [P, 3, P], F32)
        bias_qk = eb("bias_qk", [P, 2], F32)
        bias_qs = eb("bias_qs", [P, 1], F32)
        bias_v = eb("bias_v", [P, P], F32)
        tri = eb("tri", [P, NE, NE], F32)
        ctx_in = eb("ctx_in", [P, 2, D], F32)
        qk32 = eb("qk32", [P, 2, D], F32)
        rem = eb("rem", [P, 2, D], F32)
        parts = eb("parts", [P, 2, 3, D], BF16)
        v_parts = eb("v_parts", [P, 2, 2, 2 * H, VC], BF16)
        mask_in = eb("mask_in", [P, 2, 2, 256], F32)
        maskT = eb("maskT", [P, 2, 2, 256], F32)
        q_stack = eb("q_stack", [P, 2, 2, 2, 4, D], BF16)
        k_stack = eb("k_stack", [P, 2, 2, 4, D], BF16)
        zero_rows = eb("zero_rows", [3, D], BF16)
        row_max = eb("row_max", [P, 16], F32)
        max_rem = eb("max_rem", [P, 16], F32)
        max_parts = eb("max_parts", [P, 2, 3, 8], BF16)
        max_rows = eb("max_rows", [48, P], BF16)
        p32 = eb("p32", [P, 2, 512], F32)
        p_hi = eb("p_hi", [P, 2, 2, 512], F16)
        p_lo = eb("p_lo", [P, 2, 2, 512], F16)
        o_sum = eb("o_sum", [P, 2, H, DH], F32)
        o_rec = eb("o_rec", [P, 2, H], F32)
        on = eb("on", [P, 2, P], F32)
        lg = eb("lg", [P, NE], F32)
        lmax = eb("lmax", [P, 1], F32)
        pe_ = eb("probs", [P, NE], F32)
        lsum = eb("lsum", [P, 1], F32)
        gt = eb("gt", [P, NE, NE], F32)
        ge = eb("ge", [P, NE, NE], F32)
        excl = eb("excl", [P, NE], F32)
        keep = eb("keep", [P, NE], F32)
        tokw = eb("tokw", [P, NE], F32)
        stage_w = maskT[:, :, :, :].rearrange("p a b n -> p (a b n)")[:, 0:3 * P].rearrange("p (w c) -> p w c", w=3)
        stage = [yT[:, :, :].rearrange("p a b -> p (a b)"),
                 p32[:, :, :].rearrange("p a b -> p (a b)"),
                 mask_in[:, :, :, :].rearrange("p a b c -> p (a b c)")]
        rt_in = xn[0:NE, :]
        early.close()

        late = ExitStack()

        def lb(name, shape, dt):
            return late.enter_context(nc.sbuf_tensor(name, shape, dt))

        d_gu = lb("d_gu", [P, 2, NE1, KT, 2 * NI1], F16)
        d_dn = lb("d_dn", [P, 2, NE1, IB1, D], F16)
        d_st = lb("d_st", [P, 2, 1536], F32)
        bd = lb("bd", [P, P], F32)
        m_u8 = lb("m_u8", [P, NPAIR, P], U8)
        mm = lb("mm", [P, 2, P], F32)
        neg = lb("neg", [P, 2, P], F32)
        sc = lb("sc", [P, 2, P], F32)
        pc = lb("pc", [P, 2, P], F32)
        pT = lb("pT", [P, 2, P], F32)
        ctx2 = lb("ctx2", [P, 2, D], F32)
        ctxT = lb("ctxT", [P, 2, KT, P], F32)
        x3T = lb("x3T", [P, 2, KT, P], F32)
        xn3 = lb("xn3", [P, 2, D], F32)
        cstat = lb("cstat", [P, 2, 6], F32)
        cmv = lb("cmv", [P, 2, 2], F32)
        cve = lb("cve", [P, 2], F32)
        crs = lb("crs", [P, 2], F32)
        cmax = lb("cmax", [P, 2], F32)
        csum = lb("csum", [P, 2], F32)
        valid = lb("valid", [P, 2], F32)
        cr = lb("cr", [P, 2], F32)
        x4T = lb("x4T", [P, 2, KT, NE1, 64], F16)
        dy_gate = lb("dy_gate", [P, 1], F32)
        xo = lb("xo", [P, 2, D], F32)
        late.close()

        block = ctx.enter_context(nc.Block())

        w_in = [A["L0_xattn_Wq"], A["L0_xattn_Wk"], A["L0_xattn_Wv"]]
        b_in = [A["L0_xattn_bq"], A["L0_xattn_bk"]]
        N_SMALL = 2 * 8 * 2 + 2 * 2 + 1 + 2
        STACK_DMAS = 2 * 7

        @block.sync
        def _(sp):
            sp.sem_inc(s["tokw_stored"], 16)
            sp.sem_inc(s["out_stored"], 16)
            sp.dma_start(x_res[:, 0:8, :], x_d[:, 0:8, :]).then_inc(s["x_loaded"], 16)
            sp.dma_start(x_res[:, 8:16, :], x_d[:, 8:16, :]).then_inc(s["x_loaded"], 16)
            sp.dma_start(ctx_in[:, 0, :], ctx_d[0]).then_inc(s["ctx0_loaded"], 16)
            sp.wait_ge(s["stage_zeroed"], 3)
            for w in range(2):
                for b2 in range(2):
                    for hp in range(4):
                        r0 = b2 * 4 + hp
                        sp.dma_start(stage_w[r0:r0 + 121:8, w, 64 * b2:64 * b2 + 64],
                                     w_in[w][16 * hp:16 * hp + 16, :]).then_inc(s["small_loaded"], 16)
                        sp.dma_start(bias_qk[r0:r0 + 121:8, w:w + 1],
                                     b_in[w][16 * hp:16 * hp + 16].rearrange("(a b) -> a b", b=1)
                                     ).then_inc(s["small_loaded"], 16)
            for b2 in range(2):
                sp.dma_start(stage_w[64 * b2:64 * b2 + 64, 2, 64 * b2:64 * b2 + 64],
                             w_in[2]).then_inc(s["small_loaded"], 16)
                sp.dma_start(bias_v[:, 64 * b2:64 * b2 + 64],
                             A["L0_xattn_bv"].rearrange("(a n) -> a n", a=1).broadcast_to([P, 64])
                             ).then_inc(s["small_loaded"], 16)
            sp.dma_start(rt_in, A["L0_ffn_router_w"]).then_inc(s["small_loaded"], 16)
            for n, g in ((0, "g_xattn"), (2, "g_ffn")):
                sp.dma_start(gate_in[:, n:n + 2],
                             A[g].rearrange("(a n) -> a n", a=1).broadcast_to([P, 2])
                             ).then_inc(s["small_loaded"], 16)

            with sp.Fori(0, NE) as e:
                sp.wait_ge(s["wgrp_T"], 1 + 6 * e)
                sp.dma_start(stage[0].rearrange("p (t h) -> p t h", t=IB),
                             A["L0_ffn_gate_w"][e].rearrange("(t p) h -> p t h", p=P)
                             ).then_inc(s["stage0_loaded"], 16)
                sp.dma_start(stage[1].rearrange("p (t h) -> p t h", t=IB),
                             A["L0_ffn_up_w"][e].rearrange("(t p) h -> p t h", p=P)
                             ).then_inc(s["stage1_loaded"], 16)
                sp.dma_start(stage[2].rearrange("p (t i) -> p t i", t=2),
                             A["L0_ffn_down_w"][e].rearrange("(t p) i -> p t i", p=P)
                             ).then_inc(s["stage2_loaded"], 16)

            def load_mask(b, slot):
                sp.dma_start(mask_in[:, slot, :, :], mask_d[b]).then_inc(s[f"mask{slot}_loaded"], 16)

            def stack_pair(par, n):
                sp.wait_ge(s["qk_split"], n + 1)
                sp.dma_start(part_d[par].rearrange("w c r n -> r w c n"),
                             parts[:, :, :, :]).then_inc(s["parts_stored"], 16)
                sp.wait_ge(s["parts_stored"], 16 * (n + 1))
                for hh in range(2):
                    lo, hi = 64 * hh, 64 * hh + 64
                    src = [[part_d[par, w, c].rearrange("(g d r) n -> g d (r n)", g=2, d=DH)[hh]
                            for c in range(3)] for w in range(2)]
                    for i in range(2):
                        sp.dma_start(
                            q_stack[lo + 24 * i:lo + 24 * i + 24, par, hh, :, :, :].rearrange("r b h n -> r (b h n)"),
                            src[0][i].unsqueeze(1).broadcast_to([DH, 3, 2048])
                        ).then_inc(s["stack_loaded"], 16)
                        sp.dma_start(
                            k_stack[lo + 24 * i:lo + 24 * i + 24, par, :, :, :].rearrange("r b h n -> r (b h n)"),
                            part_d[par, 1].rearrange("c (g d r) n -> g d c (r n)", g=2, d=DH)[hh]
                        ).then_inc(s["stack_loaded"], 16)
                    sp.dma_start(q_stack[lo + 48:lo + 56, par, hh, :, :, :].rearrange("r b h n -> r (b h n)"),
                                 src[0][2]).then_inc(s["stack_loaded"], 16)
                    sp.dma_start(k_stack[lo + 48:lo + 56, par, :, :, :].rearrange("r b h n -> r (b h n)"),
                                 src[1][0]).then_inc(s["stack_loaded"], 16)
                    sp.dma_start(q_stack[lo + 56:lo + 59, par, hh, :, :, :].rearrange("r b h n -> r (b h) n"),
                                 zero_rows[:, :].unsqueeze(1).broadcast_to([3, 8, D])).then_inc(s["stack_loaded"], 16)

            def load_max_rows(c, n):
                par, b2 = c // 2, c % 2
                sp.wait_ge(s["maxT_copied"], n + 1)
                for hh in range(2):
                    sp.dma_start(q_stack[64 * hh + 56:64 * hh + 59, par, hh, b2, :, :].rearrange("r h n -> r (h n)"),
                                 max_rows[24 * hh:24 * hh + 24, :]).then_inc(s["max_rows_loaded"], 16)
                sp.wait_ge(s["max_rows_loaded"], 32 * (n + 1))
                sp.sem_inc(s["sp_apart"], 1)

            def attention_loads(a, c):
                par, b2 = c // 2, c % 2
                n = 4 * a + c
                if b2 == 0:
                    pair = 2 * a + par
                    sp.wait_ge(s["v_projected"], pair + 1)
                    sp.dma_start(ctx_in[:, par, :], ctx_d[(pair + 2) % NPAIR]).then_inc(s[f"ctx{par}_loaded"], 16)
                    sp.wait_ge(s["scores2_done"], 1 + 8 * n)
                    stack_pair(1 - par, pair + 1)
                sp.wait_ge(s["max_done"], 16 * n + 16)
                sp.sem_inc(s["sp_apart"], 1)
                sp.wait_ge(s["maskT_ready"], n + 1)
                load_mask((n + 2) % B, c % 2)
                load_max_rows((c + 1) % 4, n + 1)

            def store_token_weights(a, u):
                sp.wait_ge(s["wrow_ready"], 2 * a + u + 1)
                sp.dma_start(tokw_d[(a // 2) % 2, :, bass.ds((a % 2) * 256 + u * P, P)],
                             wrow[:, :]).then_inc(s["tokw_stored"], 16)
                sp.wait_ge(s["tokw_stored"], 16 + 16 * (2 * a + u + 1))
                sp.sem_inc(s["sp_apart"], 1)

            def load_expert_weights(gb, k):
                sp.wait_ge(s["up_used"], 1 + 16 * gb + 4 * k)
                sp.dma_start(wb[:, k % 2, :],
                             tokw_d[(gb // 2) % 2, (gb % 2) * 4 + k].rearrange("(q t) -> q t", q=1).broadcast_to([P, TILE])
                             ).then_inc(s[f"wb{k % 2}_loaded"], 16)

            sp.wait_ge(s["w_split"], 2 + 6 * NE)
            sp.dma_start(ctx_in[:, 1, :], ctx_d[1]).then_inc(s["ctx1_loaded"], 16)
            load_mask(0, 0)
            load_mask(1, 1)
            stack_pair(0, 0)
            load_max_rows(0, 0)

            with sp.Fori(0, 2) as a:
                for c in range(4):
                    attention_loads(a, c)
                    if c % 2 == 1:
                        store_token_weights(a, c // 2)
            with sp.Fori(2, ROUNDS) as a:
                for c in range(4):
                    load_expert_weights(a - 2, c)
                    attention_loads(a, c)
                    if c % 2 == 1:
                        store_token_weights(a, c // 2)
            with sp.Fori(ROUNDS - 2, ROUNDS) as gb:
                for c in range(4):
                    load_expert_weights(gb, c)

            sp.wait_ge(s["yT_T"], 4 * ROUNDS)
            sp.wait_ge(s["down_done"], 2 + UNITS * ROUNDS)
            sp.dma_start(m_u8[:, :, :],
                         A["mask_BxS2_bk0"].rearrange("(q p b) s -> q p (b s)", q=1, b=2).broadcast_to([P, NPAIR, P])
                         ).then_inc(s["mask_m_loaded"], 16)
            for e in range(NE1):
                sp.wait_ge(s["dw_split"], 4 * max(0, e - 1))
                sp.dma_start(d_st[:, e % 2, 0:1024].rearrange("p (t i) -> p t i", t=KT),
                             A["L1_ffn_gate_up_proj"][e].rearrange("(t p) i -> p t i", p=P)
                             ).then_inc(s["d_loaded"], 16)
                sp.dma_start(d_st[:, e % 2, 1024:1536].rearrange("p (t h) -> p t h", t=IB1),
                             A["L1_ffn_down_proj"][e].rearrange("(t p) h -> p t h", p=P)
                             ).then_inc(s["d_loaded"], 16)
                sp.wait_ge(s["d_loaded"], 32 * (e + 1))
            with sp.Fori(0, ROUNDS) as j:
                for u in range(2):
                    sp.wait_ge(s["read_done"], 1 + 2 * j)
                    sp.dma_start(ctx2[:, u, :], ctx_d[2 * j + u]).then_inc(s["cx_loaded"], 16)
                for u in range(2):
                    sp.wait_ge(s["d_out"], 2 * j + u + 1)
                    sp.dma_start(out_d[2 * j + u], xo[:, u, :]).then_inc(s["out_stored"], 16)
                sp.wait_ge(s["out_stored"], 16 + 32 * (j + 1))
                sp.sem_inc(s["sp_apart"], 1)
            sp.wait_ge(s["out_stored"], 16 + 16 * NPAIR)

        @block.gpsimd
        def _(pool):
            pool.sem_inc(s["plo_done"], 2)
            pool.sem_inc(s["h_mul"], 1)
            pool.memset(stage_w[:, :, :], 0.0).then_inc(s["stage_zeroed"], 1)
            pool.memset(zero_rows[:, :], 0.0).then_inc(s["stage_zeroed"], 1)
            pool.memset(ident[:, :], 0.0).then_inc(s["stage_zeroed"], 1)
            pool.wait_ge(s["stage_zeroed"], 3)
            pool.affine_select(out=ident[:, :], in_=ident[:, :], compare_op=ALU.not_equal, fill=1.0,
                               base=0, pattern=[[-1, P]], channel_multiplier=1).then_inc(s["consts_ready"], 1)
            pool.wait_ge(s["consts_ready"], 1)
            pool.tensor_copy(ident_b[:, :], ident[:, :]).then_inc(s["consts_ready"], 1)
            pool.memset(tri[:, :, :], 1.0).then_inc(s["consts_ready"], 1)
            pool.wait_ge(s["consts_ready"], 3)
            pool.affine_select(out=tri[:, :, :], in_=tri[:, :, :], compare_op=ALU.is_gt, fill=0.0,
                               base=0, pattern=[[1, NE], [-1, NE]], channel_multiplier=0).then_inc(s["consts_ready"], 1)
            pool.memset(minus_half[:, :], -0.5).then_inc(s["consts_ready"], 1)
            pool.memset(k_stack[:, :, :, :, :], 1.0).then_inc(s["consts_ready"], 1)
            pool.memset(q_stack[:, :, :, :, :, :], 0.0).then_inc(s["consts_ready"], 1)
            pool.memset(v_parts[:, :, :, :, :], 1.0).then_inc(s["consts_ready"], 1)
            pool.wait_ge(s["consts_ready"], 5)
            pool.wait_ge(s["ln_in"], 1)
            pool.tensor_tensor(rstd[:, :], rstd[:, :], minus_half[:, :], ALU.pow).then_inc(s["pow_done"], 1)

            def p_low(n, hp, mt):
                k = 8 * n + 2 * hp + mt
                pool.wait_ge(s["phi_done"], k + 1)
                pool.tensor_tensor(p_lo[:, hp % 2, mt, :], p32[:, mt, :], p_hi[:, hp % 2, mt, :],
                                   ALU.subtract).then_inc(s["plo_done"], 1)

            def pow2(n):
                pool.wait_ge(s["ln_in"], 2 + n)
                pool.tensor_tensor(rstd2[:, :], ve2[:, :], minus_half[:, 0:1], ALU.pow).then_inc(s["pow_done"], 1)

            def h_mul(gb, k):
                pool.wait_ge(s["up_used"], 1 + 4 + UNITS * gb + k + 1)
                pool.wait_ge(s["h_split"], 1 + UNITS * gb + k)
                pool.tensor_tensor(h32[:, :], ga[:, :], uw[:, :], ALU.mult).then_inc(s["h_mul"], 1)

            def attention_round(a, gb):
                for c in range(4):
                    n = 4 * a + c
                    for hp in range(4):
                        p_low(n, hp, 0)
                        p_low(n, hp, 1)
                        if gb is not None:
                            h_mul(gb, 4 * c + hp)
                    if c % 2 == 1:
                        pow2(2 * a + c // 2)

            with pool.Fori(0, 2) as a:
                attention_round(a, None)
            with pool.Fori(2, ROUNDS) as a:
                attention_round(a, a - 2)
            with pool.Fori(ROUNDS - 2, ROUNDS) as gb:
                for k in range(UNITS):
                    h_mul(gb, k)

            base_ln = 1 + NPAIR
            pool.wait_ge(s["yT_T"], 4 * ROUNDS)
            pool.wait_ge(s["down_done"], 2 + UNITS * ROUNDS)
            pool.memset(bd[:, :], 0.0).then_inc(s["consts_ready"], 1)
            pool.wait_ge(s["consts_ready"], 9)
            for q in range(2):
                pool.memset(bd[64 * q:64 * q + 64, 64 * q:64 * q + 64], 1.0).then_inc(s["consts_ready"], 1)
            with pool.Fori(0, ROUNDS) as j:
                for i in range(2):
                    pool.wait_ge(s["ln_in"], base_ln + 2 * j + i + 1)
                    pool.tensor_tensor(crs[:, :], cve[:, :], minus_half[:, 0:2], ALU.pow).then_inc(s["pow_done"], 1)
                pool.wait_ge(s["d_up"], 2 * j + 2)
                pool.tensor_tensor(h32[:, :], ga[:, :], uw[:, :], ALU.mult).then_inc(s["d_mul"], 1)

        @block.scalar
        def _(act):
            act.sem_inc(s["y_evac"], 1)
            act.wait_ge(s["small_loaded"], 16 * N_SMALL)
            act.activation(gates[:, :], gate_in[:, :], ACT.Tanh).then_inc(s["gates_ready"], 1)

            def w_hi(k, ps, dst):
                act.wait_ge(s["wgrp_T"], 1 + k + 1)
                act.activation(dst, ps, ACT.Copy, scale=W_SCALE).then_inc(s["w_hi"], 1)

            for w in range(3):
                act.wait_ge(s["wst_T"], 3)
                act.activation(w_bd[:, w, :], psM[:, w * P:w * P + P], ACT.Copy).then_inc(s["bias_ready"], 1)
            with act.Fori(0, NE) as e:
                for m in range(2):
                    for k in range(KT):
                        w_hi(6 * e + 2 * m + k, (psG, psU)[k][:, :], w_gu[:, 0, e, m, k, :])
                for k in range(2):
                    w_hi(6 * e + 4 + k, (psG, psU)[k][:, :].rearrange("p (t h) -> p t h", t=2),
                         w_dn[:, 0, e, 2 * k:2 * k + 2, :])

            def copy_qk(n):
                act.wait_ge(s["qk_projected"], n + 1)
                act.wait_ge(s["qk_split"], n)
                act.activation(qk32[:, 0, :], psM[:, 0:D], ACT.Identity, scale=DH ** -0.5,
                               bias=bias_qs[:, 0:1]).then_inc(s["qk_copied"], 1)
                act.activation(qk32[:, 1, :], psM[:, D:2 * D], ACT.Identity,
                               bias=bias_qk[:, 1:2]).then_inc(s["qk_copied"], 1)

            def copy_maskT(n, slot):
                act.wait_ge(s["maskT_ready"], n + 1)
                act.activation(maskT[:, slot, :, :], psM[:, :].rearrange("p (t n) -> p t n", t=2),
                               ACT.Copy).then_inc(s["maskT_copied"], 1)

            def copy_maxT(n):
                act.wait_ge(s["maxT_ready"], n + 1)
                act.wait_ge(s["max_rows_loaded"], 32 * n)
                act.activation(max_rows[:, :], psM[:, 0:64].bitcast(BF16)[0:48, :], ACT.Copy
                               ).then_inc(s["maxT_copied"], 1)

            def exps(n, hp, mt):
                k = 8 * n + 2 * hp + mt
                act.wait_ge(s["masked_done"], 1 + k + 1)
                act.activation(p32[:, mt, :], p32[:, mt, :], ACT.Exp, bias=lnscale[:, 0:1]).then_inc(s["exp_done"], 1)
                act.wait_ge(s["pv_done"], 4 * n + hp + 1)
                act.wait_ge(s["exp_done"], k + 1)
                act.activation(p_hi[:, hp % 2, mt, :], p32[:, mt, :], ACT.Copy).then_inc(s["phi_done"], 1)

            def x_high(a, u):
                act.wait_ge(s["xn2T_ready"], 2 * a + u + 1)
                act.activation(xT[:, (a // 2) % 2, 0, :, bass.ds((a % 2) * 256 + u * P, P)],
                               psM[:, 0:2 * P].rearrange("p (k t) -> p k t", k=KT), ACT.Copy,
                               scale=X_SCALE).then_inc(s["xt_hi"], 1)

            def route_exp(n):
                act.wait_ge(s["logits_done"], n + 1)
                act.activation(pe_[:, :], lg[:, :], ACT.Exp, scale=G_UNSCALE, bias=lmax[:, 0:1],
                               accum_out=lsum[:, 0:1]).then_inc(s["route_exp"], 1)

            def block_tanh(gb, k):
                act.wait_ge(s["gate_ready"], UNITS * gb + k + 1)
                act.activation(th[:, :], psG[:, :], ACT.Tanh, scale=0.5 * G_UNSCALE).then_inc(s["tanh_done"], 1)

            def block_high(gb, k):
                u = UNITS * gb + k
                act.wait_ge(s["h_mul"], 1 + u + 1)
                act.wait_ge(s["down_done"], u + 1)
                act.activation(hp_hi[:, k % 2, :], h32[:, :], ACT.Copy).then_inc(s["h_hi"], 1)

            def y_out(gb):
                act.wait_ge(s["down_done"], 2 + UNITS * (gb + 1))
                for hb in range(2):
                    act.activation(yT[:, hb, :], psY[:, hb, :], ACT.Copy, scale=1.0 / W_SCALE
                                   ).then_inc(s["y_evac"], 1)

            act.wait_ge(s["exp_bias_set"], 1)

            copy_maskT(0, 0)
            copy_qk(0)
            copy_maxT(0)

            def attention_round(a, gb):
                for c in range(4):
                    n = 4 * a + c
                    if c % 2 == 0:
                        copy_qk(2 * a + c // 2 + 1)
                    act.wait_ge(s["masked_done"], 1 + 8 * n)
                    copy_maskT(n + 1, (c + 1) % 2)
                    for hp in range(4):
                        if gb is not None:
                            block_tanh(gb, 4 * c + hp)
                        exps(n, hp, 0)
                        exps(n, hp, 1)
                        if gb is not None:
                            block_high(gb, 4 * c + hp)
                    copy_maxT(n + 1)
                    if c % 2 == 1:
                        x_high(a, c // 2)
                        route_exp(2 * a + c // 2)
                if gb is not None:
                    y_out(gb)

            with act.Fori(0, 2) as a:
                attention_round(a, None)
            with act.Fori(2, ROUNDS) as a:
                attention_round(a, a - 2)
            with act.Fori(ROUNDS - 2, ROUNDS) as gb:
                for k in range(UNITS):
                    block_tanh(gb, k)
                    block_high(gb, k)
                y_out(gb)

            act.wait_ge(s["yT_T"], 4 * ROUNDS)
            with act.Fori(0, ROUNDS) as j:
                for u in range(2):
                    act.wait_ge(s["cxT"], 2 * j + u + 1)
                    act.activation(ctxT[:, u, :, :], psM[:, 0:2 * P].rearrange("p (k t) -> p k t", k=KT),
                                   ACT.Copy).then_inc(s["ctxT_done"], 1)
                for u in range(2):
                    act.wait_ge(s["xn3T"], 2 * j + u + 1)
                    act.activation(x3T[:, u, :, :], psM[:, 0:2 * P].rearrange("p (k t) -> p k t", k=KT),
                                   ACT.Copy).then_inc(s["xt3_done"], 1)
                for u in range(2):
                    act.wait_ge(s["sc_masked"], 2 * j + u + 1)
                    act.activation(pc[:, u, :], sc[:, u, :], ACT.Exp, bias=cmax[:, u:u + 1],
                                   accum_out=csum[:, u:u + 1]).then_inc(s["c_exp"], 1)
                for u in range(2):
                    act.wait_ge(s["pT_ready"], 2 * j + u + 1)
                    act.activation(pT[:, u, :], psM[:, 0:P], ACT.Copy).then_inc(s["pT_done"], 1)
                for u in range(2):
                    act.wait_ge(s["xn4T"], 2 * j + u + 1)
                    for k in range(KT):
                        last = act.activation(x4T[:, 0, k, :, 32 * u:32 * u + 32],
                                              psM[:, k * P:k * P + P].rearrange("p (q e) -> p e q", e=NE1),
                                              ACT.Copy, scale=X_SCALE)
                    last.then_inc(s["xn4_hi"], 1)
                act.wait_ge(s["d_gate"], j + 1)
                act.activation(th[:, :], psG[:, :], ACT.Tanh, scale=0.5 * G_UNSCALE).then_inc(s["d_tanh"], 1)
                act.wait_ge(s["d_mul"], j + 1)
                act.activation(hp_hi[:, 0, :], h32[:, :], ACT.Copy).then_inc(s["d_hi"], 1)
                act.wait_ge(s["d_down"], j + 1)
                for hb in range(2):
                    act.activation(yT[:, hb, 0:256].rearrange("p (q e) -> p e q", e=NE1),
                                   psY[:, hb, 0:256].rearrange("p (e q) -> p e q", e=NE1),
                                   ACT.Copy, scale=dy_gate[:, 0:1]).then_inc(s["d_yevac"], 1)

        @block.tensor
        def _(pe):
            def mm(out_, lhsT, rhs, start=True, stop=True):
                return pe.matmul(out_, lhsT, rhs, start=start, stop=stop)

            def square(sl):
                return psM[:, sl * P:sl * P + P]

            pe.sem_inc(s["pv_done"], 2)
            pe.sem_inc(s["down_done"], 2)
            for name in ("wgrp_T", "scores2_done", "read_done"):
                pe.sem_inc(s[name], 1)
            pe.wait_ge(s["small_loaded"], 16 * N_SMALL)
            pe.wait_ge(s["consts_ready"], 2)
            for w in range(3):
                pe.transpose(square(w), stage_w[:, w, :], ident[:, :]).then_inc(s["wst_T"], 1)
            for k in range(KT):
                last = pe.transpose(psY[:, 0, k * NE:k * NE + NE], rt_in[:, k * P:k * P + P], ident[0:NE, 0:NE])
            last.then_inc(s["router_T"], 1)

            with pe.Fori(0, NE) as e:
                for m in range(3):
                    pe.wait_ge(s[f"stage{m}_loaded"], 16 * e + 16)
                    for k in range(2):
                        pe.wait_ge(s["w_split"], 6 * e + 2 * m + k + 1)
                        bank = (psG, psU)[k]
                        for i in range(4):
                            if m < 2:
                                src = stage[m].rearrange("p (t h) -> p t h", t=IB)[:, i, k * P:k * P + P]
                            else:
                                src = stage[2].rearrange("p (t i) -> p t i", t=2)[
                                    :, i % 2, (2 * k + i // 2) * P:(2 * k + i // 2) * P + P]
                            last = pe.transpose(bank[:, i * P:i * P + P], src, ident[:, :])
                        last.then_inc(s["wgrp_T"], 1)

            def project(par, n):
                pe.wait_ge(s["xn_ready"], n + 1)
                pe.wait_ge(s["bias_ready"], 4)
                pe.wait_ge(s[f"ctx{par}_loaded"], 16 * (n // 2 + 1))
                mm(psM[:, 0:D], w_bd[:, 0, :], xn[:, :])
                mm(psM[:, D:2 * D], w_bd[:, 1, :], ctx_in[:, par, :]).then_inc(s["qk_projected"], 1)
                pe.wait_ge(s["qk_copied"], 2 * n + 2)
                for t in range(2):
                    last = mm(psM[:, t * P:t * P + P], ctx_in[:, par, t * P:t * P + P], w_bd[:, 2, :])
                last.then_inc(s["v_projected"], 1)
                pe.wait_ge(s["v_copied"], n + 1)

            def mask_transposes(n, slot):
                pe.wait_ge(s[f"mask{slot}_loaded"], 16 * (n // 2 + 1))
                for mt in range(2):
                    for nt in range(2):
                        last = pe.transpose(psM[:, mt * 256 + nt * P:mt * 256 + nt * P + P],
                                            mask_in[:, slot, nt, mt * P:mt * P + P], ident[:, :])
                last.then_inc(s["maskT_ready"], 1)
                pe.wait_ge(s["maskT_copied"], n + 1)

            def first_pass(c, n, i):
                par, b2, hp, hh = c // 2, c % 2, i // 2, i % 2
                pe.wait_ge(s["max_done"], 16 * n + 2 * i)
                for nt in range(2):
                    last = mm(ps1[:, nt, :], q_stack[:, par, hh, b2, hp, nt * P:nt * P + P],
                              k_stack[:, par, b2, hp, :])
                last.then_inc(s["scores1_done"], 1)

            def second_pass(c, n, hp, mt):
                par, b2 = c // 2, c % 2
                pe.wait_ge(s["masked_done"], 1 + 8 * n + 2 * hp + mt)
                mm(ps2[:, :], k_stack[:, par, b2, hp, mt * P:mt * P + P],
                   q_stack[:, par, :, b2, hp, :]).then_inc(s["scores2_done"], 1)

            def times_v(c, n, hp):
                par, b2 = c // 2, c % 2
                pe.wait_ge(s["plo_done"], 2 + 8 * n + 2 * hp + 2)
                for hh in range(2):
                    for nt in range(2):
                        h = 2 * hp + hh
                        dst = psV[:, (nt * H + h) * VC:(nt * H + h + 1) * VC]
                        for i, (part, mt) in enumerate(((p_hi, 0), (p_hi, 1), (p_lo, 0), (p_lo, 1))):
                            at = hh * 256 + nt * P
                            last = mm(dst, part[:, hp % 2, mt, at:at + P], v_parts[:, par, mt, b2 * H + h, :],
                                      start=(i == 0), stop=(i == 3))
                last.then_inc(s["pv_done"], 1)

            def turn_maxima(n):
                pe.wait_ge(s["max_split"], n + 1)
                pe.sem_inc(s["pe_apart"], 1)
                pe.transpose(psM[:, 0:64].bitcast(BF16)[0:48, :],
                             max_parts[:, :, :, :].rearrange("p g c x -> p (g c x)"), ident_b[:, :]
                             ).then_inc(s["maxT_ready"], 1)
                pe.wait_ge(s["maxT_copied"], n + 1)

            def attention_end(a, u):
                pair = 2 * a + u
                pe.wait_ge(s["on_ready"], 2 * pair + 2)
                for nt in range(2):
                    last = pe.transpose(square(nt), on[:, nt, :], ident[:, :])
                last.then_inc(s["onT_ready"], 1)
                pe.wait_ge(s["x1_done"], pair + 1)
                pe.wait_ge(s["xn2_ready"], pair + 1)
                for k in range(KT):
                    last = pe.transpose(square(k), xn[:, k * P:k * P + P], ident[:, :])
                last.then_inc(s["xn2T_ready"], 1)
                pe.wait_ge(s["xt_split"], pair + 1)
                at = bass.ds((a % 2) * 256 + u * P, P)
                tp = (a // 2) % 2
                for k in range(KT):
                    mm(psM[:, 0:2 * NE], xT[:, tp, 0, k, at], w_rt[:, k, :], start=(k == 0), stop=False)
                for k in range(KT):
                    last = mm(psM[:, 0:NE], xT[:, tp, 1, k, at], w_rt[:, k, 0:NE], start=False, stop=(k == KT - 1))
                last.then_inc(s["router_done"], 1)
                pe.wait_ge(s["lg_done"], pair + 1)
                pe.wait_ge(s["w_ready"], pair + 1)
                pe.transpose(psM[0:NE, 0:P], tokw[:, :], ident[:, :]).then_inc(s["wT_ready"], 1)
                pe.wait_ge(s["wrow_ready"], pair + 1)

            def block_in(gb, k, bank, which, done):
                e = (gb % 2) * 4 + k // IB
                i0 = (k % IB) * P
                tp = (gb // 2) % 2
                n = 0
                for kt in range(KT):
                    for wp, xp in ((0, 0), (1, 0), (0, 1)):
                        last = mm(bank[:, :], w_gu[:, wp, e, which, kt, i0:i0 + P], xT[:, tp, xp, kt, :],
                                  start=(n == 0), stop=(n == 5))
                        n += 1
                last.then_inc(done, 1)

            def block_gate(gb, k):
                u = UNITS * gb + k
                pe.wait_ge(s["gate_used"], 1 + u)
                if k == 0:
                    pe.wait_ge(s["xt_split"], 4 * (gb // 2) + 4)
                block_in(gb, k, psG, 0, s["gate_ready"])

            def block_up(gb, k):
                pe.wait_ge(s["up_used"], 1 + 4 + UNITS * gb + k)
                block_in(gb, k, psU, 1, s["up_ready"])

            def block_down(gb, k):
                u = UNITS * gb + k
                e = (gb % 2) * 4 + k // IB
                pe.wait_ge(s["h_split"], 1 + u + 1)
                if k == 0:
                    pe.wait_ge(s["y_evac"], 1 + 2 * gb)
                for hb in range(2):
                    for i, (wp, hpart) in enumerate(((0, hp_hi), (1, hp_hi), (0, hp_lo))):
                        last = mm(psY[:, hb, :], w_dn[:, wp, e, k % IB, hb * P:hb * P + P], hpart[:, k % 2, :],
                                  start=(k == 0 and i == 0), stop=(k == UNITS - 1 and i == 2))
                last.then_inc(s["down_done"], 1)

            def turn_outputs(gb):
                pe.wait_ge(s["y_evac"], 1 + 2 * gb + 2)
                for q in range(4):
                    for hb in range(2):
                        last = pe.transpose(square(hb), yT[:, hb, q * P:q * P + P], ident[:, :])
                    last.then_inc(s["yT_T"], 1)
                    pe.wait_ge(s["y_added"], 4 * gb + q + 1)

            def attention_round(a, gb):
                for c in range(4):
                    n = 4 * a + c
                    if c % 2 == 0:
                        project(1 - c // 2, 2 * a + c // 2 + 1)
                    mask_transposes(n + 1, (c + 1) % 2)
                    if c % 2 == 1:
                        pe.wait_ge(s["stack_loaded"], STACK_DMAS * 16 * (2 * a + c // 2 + 2))
                    pe.wait_ge(s["max_rows_loaded"], 32 * (n + 1))
                    for hp in range(4):
                        if gb is not None:
                            block_gate(gb, 4 * c + hp)
                        first_pass((c + 1) % 4, n + 1, 2 * hp)
                        second_pass(c, n, hp, 0)
                        if gb is not None:
                            block_up(gb, 4 * c + hp)
                        first_pass((c + 1) % 4, n + 1, 2 * hp + 1)
                        second_pass(c, n, hp, 1)
                        if gb is not None and 4 * c + hp >= 1:
                            block_down(gb, 4 * c + hp - 1)
                        if hp == 0:
                            pe.wait_ge(s["pv_evac"], 1 + n)
                            pe.wait_ge(s["v_split"], 2 * a + c // 2 + 1)
                        else:
                            times_v(c, n, hp - 1)
                    times_v(c, n, 3)
                    turn_maxima(n + 1)
                    if c % 2 == 1:
                        attention_end(a, c // 2)
                if gb is not None:
                    block_down(gb, UNITS - 1)
                    turn_outputs(gb)

            pe.wait_ge(s["w_split"], 2 + 6 * NE)
            mask_transposes(0, 0)
            project(0, 0)
            pe.wait_ge(s["stack_loaded"], STACK_DMAS * 16)
            for i in range(H):
                first_pass(0, 0, i)
            turn_maxima(0)

            with pe.Fori(0, 2) as a:
                attention_round(a, None)
            with pe.Fori(2, ROUNDS) as a:
                attention_round(a, a - 2)
            with pe.Fori(ROUNDS - 2, ROUNDS) as gb:
                for k in range(UNITS):
                    block_gate(gb, k)
                    block_up(gb, k)
                    if k >= 1:
                        block_down(gb, k - 1)
                block_down(gb, UNITS - 1)
                turn_outputs(gb)

            pe.wait_ge(s["dw_split"], 4 * NE1)
            with pe.Fori(0, ROUNDS) as j:
                for u in range(2):
                    pe.wait_ge(s["cx_loaded"], 32 * (j + 1))
                    for k in range(KT):
                        last = pe.transpose(square(k), ctx2[:, u, k * P:k * P + P], ident[:, :])
                    last.then_inc(s["cxT"], 1)
                    pe.wait_ge(s["ctxT_done"], 2 * j + u + 1)
                pe.wait_ge(s["xn3_ready"], 4 * j + 2)
                for u in range(2):
                    for k in range(KT):
                        last = pe.transpose(square(k), xn3[:, u, k * P:k * P + P], ident[:, :])
                    last.then_inc(s["xn3T"], 1)
                    pe.wait_ge(s["xt3_done"], 2 * j + u + 1)
                for u in range(2):
                    for k in range(KT):
                        last = mm(psM[:, 0:P], x3T[:, u, k, :], ctxT[:, u, k, :], start=(k == 0), stop=(k == 1))
                    last.then_inc(s["sc_done"], 1)
                    pe.wait_ge(s["sc_read"], 2 * j + u + 1)
                for u in range(2):
                    pe.wait_ge(s["c_exp"], 2 * j + u + 1)
                    pe.transpose(psM[:, 0:P], pc[:, u, :], ident[:, :]).then_inc(s["pT_ready"], 1)
                    pe.wait_ge(s["pT_done"], 2 * j + u + 1)
                for u in range(2):
                    mm(psM[:, 0:D], pT[:, u, :], ctx2[:, u, :]).then_inc(s["read_done"], 1)
                    pe.wait_ge(s["x3_done"], 2 * j + u + 1)
                pe.wait_ge(s["xn3_ready"], 4 * j + 4)
                for u in range(2):
                    for k in range(KT):
                        last = pe.transpose(square(k), xn3[:, u, k * P:k * P + P], ident[:, :])
                    last.then_inc(s["xn4T"], 1)
                    pe.wait_ge(s["xn4_split"], 2 * j + u + 1)
                for which, bank, done in ((0, psG, "d_gate"), (1, psU, "d_upT")):
                    for ib in range(IB1):
                        for e in range(NE1):
                            n = 0
                            dst = bank[:, (ib * NE1 + e) * 64:(ib * NE1 + e) * 64 + 64]
                            i0 = which * NI1 + ib * P
                            for kt in range(KT):
                                for wp, xp in ((0, 0), (1, 0), (0, 1)):
                                    last = mm(dst, d_gu[:, wp, e, kt, i0:i0 + P], x4T[:, xp, kt, e, :],
                                              start=(n == 0), stop=(n == 5))
                                    n += 1
                    last.then_inc(s[done], 1)
                pe.wait_ge(s["d_split"], j + 1)
                for hb in range(2):
                    for e in range(NE1):
                        n = 0
                        for ib in range(IB1):
                            at = (ib * NE1 + e) * 64
                            for wp, hpart in ((0, hp_hi), (1, hp_hi), (0, hp_lo)):
                                last = mm(psY[:, hb, e * 64:e * 64 + 64], d_dn[:, wp, e, ib, hb * P:hb * P + P],
                                          hpart[:, 0, at:at + 64], start=(n == 0), stop=(n == 5))
                                n += 1
                last.then_inc(s["d_down"], 1)
                pe.wait_ge(s["d_yevac"], 2 * j + 2)
                for u in range(2):
                    for hb in range(2):
                        last = pe.transpose(square(hb), yT[:, hb, u * P:u * P + P], ident[:, :])
                    last.then_inc(s["d_yT"], 1)
                    pe.wait_ge(s["d_out"], 2 * j + u + 1)

        @block.vector
        def _(dve):
            st = Steps(dve, s["dve_step"], s["dve_apart"])
            dve.sem_inc(s["up_used"], 5)
            dve.sem_inc(s["w_split"], 2)
            for name in ("h_split", "masked_done", "pv_evac", "gate_used"):
                dve.sem_inc(s[name], 1)
            dve.memset(lnscale[:, :], LN_P_SCALE).then_inc(s["exp_bias_set"], 1)
            dve.wait_ge(s["exp_bias_set"], 1)
            dve.wait_ge(s["x_loaded"], 32)
            for p in range(NPAIR):
                st.link(dve.bn_stats(stats[:, :], x_res[:, p, :]))
                st.link(dve.bn_aggr(mean_var[:, p, :], stats[:, :]))
            dve.tensor_scalar(rstd[:, :], mean_var[:, :, 1], EPS, None, ALU.add).then_inc(s["ln_in"], 1)
            dve.wait_ge(s["small_loaded"], 16 * N_SMALL)
            dve.tensor_scalar(bias_qs[:, :], bias_qk[:, 0:1], DH ** -0.5, None, ALU.mult).then_inc(s["bias_ready"], 1)
            dve.wait_ge(s["router_T"], 1)
            for k in range(KT):
                st.link(dve.tensor_scalar(w_rt[:, k, 0:NE], psY[:, 0, k * NE:k * NE + NE], W_SCALE, None, ALU.mult))
                st.link(dve.scalar_tensor_tensor(out=w_rt[:, k, NE:2 * NE], in0=psY[:, 0, k * NE:k * NE + NE],
                                                 scalar=W_SCALE, in1=w_rt[:, k, 0:NE], op0=ALU.mult,
                                                 op1=ALU.subtract))

            def w_low(k, ps, hi, dst):
                dve.wait_ge(s["w_hi"], k + 1)
                dve.scalar_tensor_tensor(out=dst, in0=ps, scalar=W_SCALE, in1=hi, op0=ALU.mult,
                                         op1=ALU.subtract).then_inc(s["w_split"], 1)

            with dve.Fori(0, NE) as e:
                for m in range(2):
                    for k in range(KT):
                        w_low(6 * e + 2 * m + k, (psG, psU)[k][:, :], w_gu[:, 0, e, m, k, :], w_gu[:, 1, e, m, k, :])
                for k in range(2):
                    w_low(6 * e + 4 + k, (psG, psU)[k][:, :].rearrange("p (t h) -> p t h", t=2),
                          w_dn[:, 0, e, 2 * k:2 * k + 2, :], w_dn[:, 1, e, 2 * k:2 * k + 2, :])

            def norm1(pair, n):
                dve.wait_ge(s["qk_projected"], n)
                dve.wait_ge(s["pow_done"], 1)
                dve.tensor_scalar(xn[:, :], x_res[:, pair, :], mean_var[:, pair, 0:1],
                                  rstd[:, bass.ds(pair, 1)], ALU.subtract, ALU.mult).then_inc(s["xn_ready"], 1)

            def cut3(dst, src, remain, after):
                st.link(dve.tensor_copy(dst[0], src))
                st.link(dve.tensor_tensor(remain, src, dst[0], ALU.subtract))
                st.link(dve.tensor_copy(dst[1], remain))
                dve.tensor_tensor(dst[2], remain, dst[1], ALU.subtract).then_inc(after, 1)

            def project_evac(par, pair, n):
                norm1(pair, n)
                dve.wait_ge(s["qk_copied"], 2 * n + 2)
                dve.wait_ge(s["parts_stored"], 16 * n)
                dve.wait_ge(s["qk_split"], n)
                cut3([parts[:, :, c, :] for c in range(3)], qk32[:, :, :], rem[:, :, :], s["qk_split"])
                dve.wait_ge(s["v_projected"], n + 1)
                dve.wait_ge(s["qk_split"], n + 1)
                vps = psM[:, 0:2 * P].rearrange("p (t c) -> p t c", t=2)
                dve.tensor_tensor(rem[:, :, P:2 * P], vps, bias_v[:, :].unsqueeze(1).broadcast_to([P, 2, P]),
                                  ALU.add).then_inc(s["v_copied"], 1)
                dve.wait_ge(s["v_copied"], n + 1)
                v = rem[:, :, P:2 * P].rearrange("p t (g d) -> p t g d", d=DH)
                r = rem[:, :, 0:P].rearrange("p t (g d) -> p t g d", d=DH)
                dst = [v_parts[:, par, :, :, DH * c:DH * c + DH] for c in range(3)]
                dve.wait_ge(s["v_split"], n)
                cut3(dst, v, r, s["v_split"])

            def maxima(c, m, i):
                dve.wait_ge(s["scores1_done"], 8 * m + i + 1)
                st.apart()
                for nt in range(2):
                    hp, hh = i // 2, i % 2
                    col = hh * 8 + hp * 2 + nt
                    dve.tensor_tensor_reduce(out=ps1[:, nt, :], in0=ps1[:, nt, :], in1=mask_in[:, c % 2, nt, :],
                                             scale=1.0, scalar=LOW, op0=ALU.add, op1=ALU.max,
                                             accum_out=row_max[:, col:col + 1]).then_inc(s["max_done"], 1)

            def cut_max(m):
                dve.wait_ge(s["max_done"], 16 * m + 16)
                dve.wait_ge(s["maxT_ready"], m)
                rm = row_max[:, :].rearrange("p (g c) -> p g c", g=2)
                rr = max_rem[:, :].rearrange("p (g c) -> p g c", g=2)
                st.link(dve.tensor_scalar(max_parts[:, :, 0, :], rm, -1.0, None, ALU.mult))
                st.link(dve.scalar_tensor_tensor(out=rr, in0=rm, scalar=-1.0, in1=max_parts[:, :, 0, :],
                                                 op0=ALU.mult, op1=ALU.subtract))
                st.link(dve.tensor_copy(max_parts[:, :, 1, :], rr))
                dve.tensor_tensor(max_parts[:, :, 2, :], rr, max_parts[:, :, 1, :], ALU.subtract
                                  ).then_inc(s["max_split"], 1)

            def add_mask(c, n, hp, mt):
                k = 8 * n + 2 * hp + mt
                dve.wait_ge(s["scores2_done"], 1 + k + 1)
                dve.wait_ge(s["plo_done"], k + 1)
                dve.tensor_tensor(p32[:, mt, :].rearrange("p (g n) -> p g n", g=2),
                                  ps2[:, :].rearrange("p (g n) -> p g n", g=2),
                                  maskT[:, c % 2, mt, :].unsqueeze(1).broadcast_to([P, 2, 256]), ALU.add
                                  ).then_inc(s["masked_done"], 1)

            def pv_out(c, n):
                b2 = c % 2
                dve.wait_ge(s["pv_done"], 2 + 4 * n + 4)
                pv = psV[:, 0:2 * H * VC].rearrange("p (g c) -> p g c", c=VC)
                dve.tensor_reduce(o_sum[:, :, :, :].rearrange("p t h d -> p (t h) d"),
                                  pv[:, :, 0:3 * DH].rearrange("p g (c d) -> p g d c", c=3), AX.X, ALU.add)
                dve.reciprocal(o_rec[:, :, :].rearrange("p t h -> p (t h)"), pv[:, :, 3 * DH]
                               ).then_inc(s["pv_evac"], 1)
                dve.wait_ge(s["pv_evac"], 1 + n + 1)
                st.link(dve.tensor_scalar(o_rec[:, :, :], o_rec[:, :, :], gates[:, 0:1], None, ALU.mult))
                dve.tensor_tensor(on[:, :, 64 * b2:64 * b2 + 64].rearrange("p t (h d) -> p t h d", d=DH),
                                  o_sum[:, :, :, :], o_rec[:, :, :].unsqueeze(3).broadcast_to([P, 2, H, DH]),
                                  ALU.mult).then_inc(s["on_ready"], 1)

            def layer_norm2(pair):
                dve.wait_ge(s["onT_ready"], pair + 1)
                dve.tensor_tensor(x_res[:, pair, :], x_res[:, pair, :], psM[:, 0:D], ALU.add
                                  ).then_inc(s["x1_done"], 1)
                dve.wait_ge(s["x1_done"], pair + 1)
                st.apart()
                st.link(dve.bn_stats(stats[:, :], x_res[:, pair, :]))
                st.apart()
                st.link(dve.bn_aggr(mv2[:, :], stats[:, :]))
                dve.tensor_scalar(ve2[:, :], mv2[:, 1:2], EPS, None, ALU.add).then_inc(s["ln_in"], 1)
                dve.wait_ge(s["pow_done"], pair + 2)
                dve.wait_ge(s["qk_projected"], pair + 2)
                dve.tensor_scalar(xn[:, :], x_res[:, pair, :], mv2[:, 0:1], rstd2[:, 0:1],
                                  ALU.subtract, ALU.mult).then_inc(s["xn2_ready"], 1)

            def x_low(a, u):
                dve.wait_ge(s["xt_hi"], 2 * a + u + 1)
                at = bass.ds((a % 2) * 256 + u * P, P)
                dve.scalar_tensor_tensor(out=xT[:, (a // 2) % 2, 1, :, at],
                                         in0=psM[:, 0:2 * P].rearrange("p (k t) -> p k t", k=KT), scalar=X_SCALE,
                                         in1=xT[:, (a // 2) % 2, 0, :, at], op0=ALU.mult,
                                         op1=ALU.subtract).then_inc(s["xt_split"], 1)

            def route(pair):
                dve.wait_ge(s["router_done"], pair + 1)
                dve.tensor_reduce(lg[:, :], psM[:, 0:2 * NE].rearrange("p (c e) -> p e c", c=2), AX.X, ALU.add
                                  ).then_inc(s["lg_done"], 1)
                dve.wait_ge(s["lg_done"], pair + 1)
                st.link(dve.tensor_reduce(lmax[:, :], lg[:, :], AX.X, ALU.max, negate=True))
                dve.tensor_scalar(lmax[:, :], lmax[:, :], G_UNSCALE, None, ALU.mult).then_inc(s["logits_done"], 1)
                dve.wait_ge(s["route_exp"], pair + 1)
                st.link(dve.reciprocal(lsum[:, :], lsum[:, :]))
                st.link(dve.tensor_scalar(pe_[:, :], pe_[:, :], lsum[:, 0:1], None, ALU.mult))
                pj = pe_[:, :].unsqueeze(1).broadcast_to([P, NE, NE])
                pi = pe_[:, :].unsqueeze(2).broadcast_to([P, NE, NE])
                dve.tensor_tensor(gt[:, :, :], pj, pi, ALU.is_gt)
                st.link(dve.tensor_tensor(ge[:, :, :], pj, pi, ALU.is_equal))
                st.link(dve.tensor_tensor(ge[:, :, :], ge[:, :, :], tri[:, :, :], ALU.mult))
                st.link(dve.tensor_tensor(gt[:, :, :], gt[:, :, :], ge[:, :, :], ALU.add))
                st.link(dve.tensor_tensor(gt[:, :, :], gt[:, :, :], pj, ALU.mult))
                st.link(dve.tensor_reduce(excl[:, :], gt[:, :, :], AX.X, ALU.add))
                st.link(dve.tensor_scalar(keep[:, :], excl[:, :], 0.9, gates[:, 2:3], ALU.is_le, ALU.mult))
                dve.scalar_tensor_tensor(out=tokw[:, :], in0=pe_[:, :], scalar=0.5 * G_UNSCALE * G_UNSCALE,
                                         in1=keep[:, :], op0=ALU.mult, op1=ALU.mult).then_inc(s["w_ready"], 1)
                dve.wait_ge(s["wT_ready"], pair + 1)
                dve.wait_ge(s["tokw_stored"], 16 + 16 * pair)
                dve.tensor_copy(wrow[:, :], psM[0:NE, 0:P]).then_inc(s["wrow_ready"], 1)

            def gate_mul(gb, k):
                u = UNITS * gb + k
                dve.wait_ge(s["tanh_done"], u + 1)
                dve.wait_ge(s["h_mul"], 1 + u)
                dve.scalar_tensor_tensor(out=ga[:, :], in0=th[:, :], scalar=1.0, in1=psG[:, :], op0=ALU.add,
                                         op1=ALU.mult).then_inc(s["gate_used"], 1)

            def up_mul(gb, k):
                u = UNITS * gb + k
                if k % IB == 0:
                    dve.wait_ge(s[f"wb{k // IB % 2}_loaded"], 16 * (2 * gb + k // IB // 2 + 1))
                dve.wait_ge(s["up_ready"], u + 1)
                dve.wait_ge(s["gate_used"], 1 + u + 1)
                dve.tensor_tensor(uw[:, :], psU[:, :], wb[:, (k // IB) % 2, :], ALU.mult).then_inc(s["up_used"], 1)

            def block_low(gb, k):
                u = UNITS * gb + k
                dve.wait_ge(s["h_hi"], u + 1)
                dve.tensor_tensor(hp_lo[:, k % 2, :], h32[:, :], hp_hi[:, k % 2, :], ALU.subtract
                                  ).then_inc(s["h_split"], 1)

            def add_experts(gb):
                for q in range(4):
                    dve.wait_ge(s["yT_T"], 4 * gb + q + 1)
                    row = 4 * (gb // 2) + q
                    dve.tensor_tensor(x_res[:, row, :], x_res[:, row, :], psM[:, 0:D],
                                      ALU.add).then_inc(s["y_added"], 1)

            dve.wait_ge(s["consts_ready"], 8)
            project_evac(0, 0, 0)
            for i in range(H):
                maxima(0, 0, i)
            cut_max(0)
            base0 = st.n

            def attention_round(a, gb, base):
                st.at(base)
                for c in range(4):
                    n = 4 * a + c
                    if c % 2 == 0:
                        pair = 2 * a + c // 2
                        project_evac(1 - c // 2, (pair + 1) % NPAIR, pair + 1)
                    for hp in range(4):
                        if gb is not None:
                            gate_mul(gb, 4 * c + hp)
                        if hp == 0:
                            dve.wait_ge(s["maskT_copied"], n + 1)
                        maxima((c + 1) % 4, n + 1, 2 * hp)
                        add_mask(c, n, hp, 0)
                        maxima((c + 1) % 4, n + 1, 2 * hp + 1)
                        add_mask(c, n, hp, 1)
                        if gb is not None:
                            up_mul(gb, 4 * c + hp)
                            block_low(gb, 4 * c + hp)
                    cut_max(n + 1)
                    pv_out(c, n)
                    if c % 2 == 1:
                        layer_norm2(2 * a + c // 2)
                        x_low(a, c // 2)
                        route(2 * a + c // 2)
                if gb is not None:
                    add_experts(gb)
                return st.n

            STEPS = ROUND_STEPS
            with dve.Fori(0, 2) as a:
                n = attention_round(a, None, base0 + a * STEPS)
            assert n == STEPS, n
            with dve.Fori(2, ROUNDS) as a:
                n = attention_round(a, a - 2, base0 + a * STEPS)
            assert n == STEPS, n
            with dve.Fori(ROUNDS - 2, ROUNDS) as gb:
                for k in range(UNITS):
                    gate_mul(gb, k)
                    up_mul(gb, k)
                    block_low(gb, k)
                add_experts(gb)

            base1 = base0 + ROUNDS * STEPS
            st.at(base1)
            dve.wait_ge(s["y_added"], 4 * ROUNDS)
            st.link(dve.tensor_scalar(dy_gate[:, :], gates[:, 3:4], 1.0 / W_SCALE, None, ALU.mult))
            for e in range(NE1):
                dve.wait_ge(s["d_loaded"], 32 * (e + 1))
                g_in = d_st[:, e % 2, 0:1024].rearrange("p (t i) -> p t i", t=KT)
                d_in = d_st[:, e % 2, 1024:1536].rearrange("p (t i) -> p t i", t=IB1)
                for src, dst in ((g_in, d_gu), (d_in, d_dn)):
                    st.link(dve.tensor_scalar(dst[:, 0, e, :, :], src, W_SCALE, None, ALU.mult))
                    dve.scalar_tensor_tensor(out=dst[:, 1, e, :, :], in0=src, scalar=W_SCALE, in1=dst[:, 0, e, :, :],
                                             op0=ALU.mult, op1=ALU.subtract).then_inc(s["dw_split"], 2)
            base2 = base1 + st.n
            dve.wait_ge(s["mask_m_loaded"], 16)
            dve.wait_ge(s["consts_ready"], 11)

            def late_norm(j, i):
                for u in range(2):
                    st.apart()
                    st.link(dve.bn_stats(cstat[:, u, :], x_res[:, 2 * j + u, :]))
                for u in range(2):
                    st.apart()
                    st.link(dve.bn_aggr(cmv[:, u, :], cstat[:, u, :]))
                dve.tensor_scalar(cve[:, :], cmv[:, :, 1], EPS, None, ALU.add).then_inc(s["ln_in"], 1)
                dve.wait_ge(s["pow_done"], 1 + NPAIR + 2 * j + i + 1)
                for u in range(2):
                    dve.tensor_scalar(xn3[:, u, :], x_res[:, 2 * j + u, :], cmv[:, u, 0:1], crs[:, u:u + 1],
                                      ALU.subtract, ALU.mult).then_inc(s["xn3_ready"], 1)

            with dve.Fori(0, ROUNDS) as j:
                st.at(base2 + j * LATE_STEPS)
                for u in range(2):
                    dve.tensor_tensor(mm[:, u, :], m_u8[:, 2 * j + u, :], bd[:, :], ALU.mult
                                      ).then_inc(s["mask_m_ready"], 1)
                dve.wait_ge(s["mask_m_ready"], 2 * j + 2)
                st.link(dve.tensor_scalar(neg[:, :, :], mm[:, :, :], 1.0, 1.0e30, ALU.subtract, ALU.mult))
                st.link(dve.tensor_reduce(valid[:, :], mm[:, :, :], AX.X, ALU.max))
                st.link(dve.tensor_scalar(valid[:, :], valid[:, :], gates[:, 1:2], None, ALU.mult))
                late_norm(j, 0)
                for u in range(2):
                    dve.wait_ge(s["sc_done"], 2 * j + u + 1)
                    dve.scalar_tensor_tensor(out=sc[:, u, :], in0=psM[:, 0:P], scalar=D ** -0.5,
                                             in1=mm[:, u, :], op0=ALU.mult, op1=ALU.mult).then_inc(s["sc_read"], 1)
                    dve.wait_ge(s["sc_read"], 2 * j + u + 1)
                    st.link(dve.tensor_tensor(sc[:, u, :], sc[:, u, :], neg[:, u, :], ALU.add))
                    dve.tensor_reduce(cmax[:, u:u + 1], sc[:, u, :], AX.X, ALU.max, negate=True
                                      ).then_inc(s["sc_masked"], 1)
                dve.wait_ge(s["c_exp"], 2 * j + 2)
                st.link(dve.reciprocal(csum[:, :], csum[:, :]))
                st.link(dve.tensor_tensor(cr[:, :], csum[:, :], valid[:, :], ALU.mult))
                for u in range(2):
                    xv = x_res[:, 2 * j + u, :]
                    dve.wait_ge(s["read_done"], 1 + 2 * j + u + 1)
                    dve.scalar_tensor_tensor(out=xv, in0=psM[:, 0:D], scalar=cr[:, u:u + 1], in1=xv,
                                             op0=ALU.mult, op1=ALU.add).then_inc(s["x3_done"], 1)
                dve.wait_ge(s["x3_done"], 2 * j + 2)
                dve.wait_ge(s["xn3T"], 2 * j + 2)
                late_norm(j, 1)
                for u in range(2):
                    dve.wait_ge(s["xn4_hi"], 2 * j + u + 1)
                    for k in range(KT):
                        last = dve.scalar_tensor_tensor(out=x4T[:, 1, k, :, 32 * u:32 * u + 32],
                                                        in0=psM[:, k * P:k * P + P].rearrange("p (q e) -> p e q", e=NE1),
                                                        scalar=X_SCALE, in1=x4T[:, 0, k, :, 32 * u:32 * u + 32],
                                                        op0=ALU.mult, op1=ALU.subtract)
                    last.then_inc(s["xn4_split"], 1)
                dve.wait_ge(s["d_tanh"], j + 1)
                dve.scalar_tensor_tensor(out=ga[:, :], in0=th[:, :], scalar=1.0, in1=psG[:, :], op0=ALU.add,
                                         op1=ALU.mult).then_inc(s["d_up"], 1)
                dve.wait_ge(s["d_upT"], j + 1)
                dve.tensor_scalar(uw[:, :], psU[:, :], 0.5 * G_UNSCALE * G_UNSCALE, None, ALU.mult
                                  ).then_inc(s["d_up"], 1)
                dve.wait_ge(s["d_hi"], j + 1)
                dve.tensor_tensor(hp_lo[:, 0, :], h32[:, :], hp_hi[:, 0, :], ALU.subtract).then_inc(s["d_split"], 1)
                dve.wait_ge(s["out_stored"], 16 + 32 * j)
                for u in range(2):
                    dve.wait_ge(s["d_yT"], 2 * j + u + 1)
                    dve.tensor_tensor(xo[:, u, :], psM[:, 0:D], x_res[:, 2 * j + u, :],
                                      ALU.add).then_inc(s["d_out"], 1)
            assert st.n == LATE_STEPS, st.n


_INS = ["x", "ctx_2048", "mask_Bx2048x2048_ff0", "mask_BxS2_bk0", "g_xattn", "g_ffn", "L0_xattn_Wq",
        "L0_xattn_bq", "L0_xattn_Wk", "L0_xattn_bk", "L0_xattn_Wv", "L0_xattn_bv", "L0_ffn_router_w",
        "L0_ffn_gate_w", "L0_ffn_up_w", "L0_ffn_down_w", "L1_ffn_gate_up_proj", "L1_ffn_down_proj"]


def kernel(**inputs):
    import numpy as _np
    import concourse.bacc as _bacc
    from concourse import mybir as _mybir
    from concourse.bass_utils import run_bass_kernel_spmd as _run

    nc = _bacc.Bacc("TRN2", target_bir_lowering=False, num_devices=1)
    arrays, args = {}, {}
    for name in _INS:
        a = _np.ascontiguousarray(inputs[name])
        arrays[f"in_{name}"] = a
        args[name] = nc.dram_tensor(f"in_{name}", a.shape, _mybir.dt.from_np(a.dtype), kind="ExternalInput").ap()
    out = nc.dram_tensor("out_0", (B, S, D), F32, kind="ExternalOutput").ap()
    build(nc, args, out)
    r = _run(nc, [arrays], core_ids=[0])
    return r.results[0]["out_0"]
```

```python
from contextlib import ExitStack

import concourse.bass as bass
from concourse import mybir

F32 = mybir.dt.float32
BF16 = mybir.dt.bfloat16
F16 = mybir.dt.float16
U8 = mybir.dt.uint8
ALU = mybir.AluOpType
ACT = mybir.ActivationFunctionType
AX = mybir.AxisListType

B, S, D = 32, 64, 256
P = 128
NPAIR = B * S // P
H, DH = 8, 8
NE, NI = 8, 512
NE1, NI1 = 4, 256
ROUNDS = B // 4
TILE = 512
KT = D // P
IB = NI // P
IB1 = NI1 // P
UNITS = 4 * IB
VC = 3 * DH + 1
SROW = 7 * DH
EPS = 1e-5
ROUND_STEPS = 50
LATE_STEPS = 15
W_SCALE = 64.0
X_SCALE = 256.0
G_UNSCALE = 1.0 / (W_SCALE * X_SCALE)
LN_P_SCALE = 12 * 0.6931471805599453
LOW = -3.0e38


class Steps:

    def __init__(self, eng, sem, met):
        self.eng, self.sem, self.met, self.n, self.base = eng, sem, met, 0, 0

    def at(self, base):
        self.base, self.n = base, 0

    def enter_round(self, r):
        if not isinstance(r, int):
            self.loop_start = self.base + self.n
            self.at(self.loop_start + (r - 3) * ROUND_STEPS)
        elif r == ROUNDS:
            assert self.n == ROUND_STEPS, self.n
            self.at(self.loop_start + (ROUNDS - 3) * ROUND_STEPS)

    def apart(self):
        self.eng.sem_inc(self.met, 1)

    def link(self, instruction):
        self.n += 1
        instruction.then_inc(self.sem, 1)
        self.eng.wait_ge(self.sem, self.base + self.n)


def build(nc, A, out):
    ctx = ExitStack()

    def sb(name, shape, dt):
        return ctx.enter_context(nc.sbuf_tensor(name, shape, dt))

    def sem(name):
        return ctx.enter_context(nc.semaphore(name))

    x_d = A["x"].rearrange("(p b) s d -> (b s) p d", b=2)
    ctx_d = A["ctx_2048"].rearrange("(p b) s d -> p (b s) d", b=2)
    mask_d = A["mask_Bx2048x2048_ff0"].rearrange("b (t n) m -> b n t m", t=2)
    out_d = out.rearrange("(p b) s d -> p (b s) d", b=2)
    part_d = nc.dram_tensor("part_scratch", (2, 2, 3, P, D), BF16, kind="Internal").ap()
    tokw_d = nc.dram_tensor("tokw_scratch", (2, NE, TILE), F32, kind="Internal").ap()

    with ctx:
        ident = sb("ident", [P, P], F32)
        ident_b = sb("ident_b", [P, P], BF16)
        minus_half = sb("minus_half", [P, NPAIR], F32)
        gates = sb("gates", [P, 4], F32)
        gate_in = sb("gate_in", [P, 4], F32)
        x_res = sb("x_res", [P, NPAIR, D], F32)
        stats = sb("stats", [P, 6], F32)
        mean_var = sb("mean_var", [P, NPAIR, 2], F32)
        rstd = sb("rstd", [P, NPAIR], F32)
        mv2 = sb("mv2", [P, 2], F32)
        ve2 = sb("ve2", [P, 1], F32)
        rstd2 = sb("rstd2", [P, 1], F32)
        xn = sb("xn", [P, D], F32)
        th_ga_h = sb("th_ga_h", [P, 4, TILE], F32)
        th, ga, hb32 = th_ga_h[:, 0, :], th_ga_h[:, 1, :], th_ga_h[:, 2:4, :]
        hp_hi = sb("hp_hi", [P, 2, TILE], F16)
        hp_lo = sb("hp_lo", [P, 2, TILE], F16)
        yT = sb("yT", [P, 2, TILE], F32)

        psG = ctx.enter_context(nc.psum_tensor("psG", [P, 512], F32))
        psU = ctx.enter_context(nc.psum_tensor("psU", [P, 512], F32))
        psY = ctx.enter_context(nc.psum_tensor("psY", [P, 2, 512], F32))
        ps1 = ctx.enter_context(nc.psum_tensor("ps1", [P, 2, 256], F32))
        ps2 = ctx.enter_context(nc.psum_tensor("ps2", [P, 512], F32))
        psV = ctx.enter_context(nc.psum_tensor("psV", [P, 512], F32))
        psM = ctx.enter_context(nc.psum_tensor("psM", [P, 512], F32))

        lnscale = sb("lnscale", [P, 1], F32)

        names = """x_loaded small_loaded stage0_loaded stage1_loaded stage2_loaded
            ctx0_loaded ctx1_loaded mask0_loaded mask1_loaded parts_stored stack_loaded
            max_rows_loaded tokw_stored wb0_loaded wb1_loaded out_stored consts_ready stage_zeroed exp_bias_set
            gates_ready v_copied x1_done lg_done y_added sc_read x3_done d_upT wst_T router_T wgrp_T w_hi w_split bias_ready
            ln_in pow_done xn_ready qk_projected v_projected qk_copied qk_split v_split
            maskT_ready maskT_copied scores1_done max_done max_split maxT_ready maxT_copied
            scores2_done masked_done exp_done phi_done plo_done pv_done pv_evac on_ready onT_ready
            xn2_ready xn2T_ready xt_hi xt_split router_done logits_done route_exp w_ready
            wT_ready wrow_ready gate_ready up_ready tanh_done gate_used up_used h_mul h_hi h_split
            down_done y_evac yT_T dve_step dve_apart pe_apart sp_apart
            d_loaded dw_hi dw_split xt3_done ctxT_done sc_done sc_masked c_exp pT_ready pT_done
            read_done xn4T xn4_hi xn4_split cx_loaded d_gate d_up d_tanh d_mul d_hi d_split d_down d_yevac
            d_yT d_out xn3_ready xn3T cxT mask_m_loaded mask_m_ready xn4_ready""".split()
        s = {n: sem(n) for n in names}

        early = ExitStack()

        def eb(name, shape, dt):
            return early.enter_context(nc.sbuf_tensor(name, shape, dt))

        w_gu = eb("w_gu", [P, 2, NE, 2, KT, NI], F16)
        w_dn = eb("w_dn", [P, 2, NE, IB, D], F16)
        w_rt = eb("w_rt", [P, KT, 2 * NE], F16)
        xT = eb("xT", [P, 2, 2, KT, TILE], F16)
        wb = eb("wb", [P, 2, TILE], F32)
        wrow = eb("wrow", [NE, P], F32)
        w_bd = eb("w_bd", [P, 3, P], F32)
        bias_qk = eb("bias_qk", [P, 2], F32)
        bias_qs = eb("bias_qs", [P, 1], F32)
        bias_v = eb("bias_v", [P, P], F32)
        tri = eb("tri", [P, NE, NE], F32)
        ctx_in = eb("ctx_in", [P, 2, D], F32)
        qk32 = eb("qk32", [P, 2, D], F32)
        rem = eb("rem", [P, 2, D], F32)
        parts = eb("parts", [P, 2, 3, D], BF16)
        v_parts = eb("v_parts", [P, 2, 2, 2 * H, VC], BF16)
        mask_in = eb("mask_in", [P, 2, 2, 256], F32)
        maskT = eb("maskT", [P, 2, 2, 256], F32)
        q_stack = eb("q_stack", [P, 2, 2, 2, 4, D], BF16)
        k_stack = eb("k_stack", [P, 2, 2, 4, D], BF16)
        zero_rows = eb("zero_rows", [3, D], BF16)
        row_max = eb("row_max", [P, 16], F32)
        max_rem = eb("max_rem", [P, 16], F32)
        max_parts = eb("max_parts", [P, 2, 3, 8], BF16)
        max_rows = eb("max_rows", [48, P], BF16)
        p32 = eb("p32", [P, 2, 512], F32)
        p_hi = eb("p_hi", [P, 2, 2, 512], F16)
        p_lo = eb("p_lo", [P, 2, 2, 512], F16)
        o_sum = eb("o_sum", [P, 2, H, DH], F32)
        o_rec = eb("o_rec", [P, 2, H], F32)
        on = eb("on", [P, 2, P], F32)
        lg = eb("lg", [P, NE], F32)
        lmax = eb("lmax", [P, 1], F32)
        pe_ = eb("probs", [P, NE], F32)
        lsum = eb("lsum", [P, 1], F32)
        gt = eb("gt", [P, NE, NE], F32)
        ge = eb("ge", [P, NE, NE], F32)
        excl = eb("excl", [P, NE], F32)
        keep = eb("keep", [P, NE], F32)
        tokw = eb("tokw", [P, NE], F32)
        stage_w = maskT[:, :, :, :].rearrange("p a b n -> p (a b n)")[:, 0:3 * P].rearrange("p (w c) -> p w c", w=3)
        stage = [yT[:, :, :].rearrange("p a b -> p (a b)"),
                 th_ga_h[:, 0:2, :].rearrange("p a b -> p (a b)"),
                 th_ga_h[:, 2:4, :].rearrange("p a b -> p (a b)")]
        rt_in = xn[0:NE, :]
        early.close()

        late = ExitStack()

        def lb(name, shape, dt):
            return late.enter_context(nc.sbuf_tensor(name, shape, dt))

        d_gu = lb("d_gu", [P, 2, NE1, KT, 2 * NI1], F16)
        d_dn = lb("d_dn", [P, 2, NE1, IB1, D], F16)
        d_st = lb("d_st", [P, 2, 1536], F32)
        bd = lb("bd", [P, P], F32)
        m_u8 = lb("m_u8", [P, NPAIR, P], U8)
        mm = lb("mm", [P, 2, P], F32)
        neg = lb("neg", [P, 2, P], F32)
        sc = lb("sc", [P, 2, P], F32)
        pc = lb("pc", [P, 2, P], F32)
        pT = lb("pT", [P, 2, P], F32)
        ctx2 = lb("ctx2", [P, 2, D], F32)
        ctxT = lb("ctxT", [P, 2, KT, P], F32)
        x3T = lb("x3T", [P, 2, KT, P], F32)
        xn3 = lb("xn3", [P, 2, D], F32)
        cstat = lb("cstat", [P, 2, 6], F32)
        cmv = lb("cmv", [P, 2, 2], F32)
        cve = lb("cve", [P, 2], F32)
        crs = lb("crs", [P, 2], F32)
        cmax = lb("cmax", [P, 2], F32)
        csum = lb("csum", [P, 2], F32)
        valid = lb("valid", [P, 2], F32)
        cr = lb("cr", [P, 2], F32)
        x4T = lb("x4T", [P, 2, KT, NE1, 64], F16)
        dy_gate = lb("dy_gate", [P, 1], F32)
        xo = lb("xo", [P, 2, D], F32)
        uw, h32 = hb32[:, 0, :], hb32[:, 1, :]
        late.close()

        block = ctx.enter_context(nc.Block())

        w_in = [A["L0_xattn_Wq"], A["L0_xattn_Wk"], A["L0_xattn_Wv"]]
        b_in = [A["L0_xattn_bq"], A["L0_xattn_bk"]]
        N_SMALL = 2 * 8 * 2 + 2 * 2 + 1 + 2
        STACK_DMAS = 2 * 7

        def weight_group(e, m, k, part):
            bank = (psG, psU)[k][:, :]
            if m < 2:
                return bank, w_gu[:, part, e, m, k, :]
            return bank.rearrange("p (t h) -> p t h", t=2), w_dn[:, part, e, 2 * k:2 * k + 2, :]

        def expert_step(r, c):
            return (r - 2, c - 1) if c else (r - 3, 3)

        def turns_outputs(r, c):
            return c == 1 and not (isinstance(r, int) and r < 3)

        def schedule(eng, step):
            for r in range(2):
                for c in range(4):
                    step(r, c, attention=True, tail=r + c > 0, pair_tail=4 * r + c > 1, experts=False,
                         weights=True)
            for c in range(4):
                step(2, c, attention=True, tail=True, pair_tail=True, experts=c > 0, weights=False)
            with eng.Fori(3, ROUNDS) as r:
                for c in range(4):
                    step(r, c, attention=True, tail=True, pair_tail=True, experts=True, weights=False)
            for r in range(ROUNDS, ROUNDS + 3):
                for c in range(4 if r < ROUNDS + 2 else 2):
                    step(r, c, attention=False, tail=r == ROUNDS and c == 0, pair_tail=r == ROUNDS and c < 2,
                         experts=r < ROUNDS + 2 or c == 0, weights=False)

        @block.sync
        def _(sp):
            sp.sem_inc(s["tokw_stored"], 16)
            sp.sem_inc(s["max_rows_loaded"], 1)
            sp.sem_inc(s["out_stored"], 16)
            sp.dma_start(x_res[:, 0:8, :], x_d[:, 0:8, :]).then_inc(s["x_loaded"], 16)
            sp.dma_start(x_res[:, 8:16, :], x_d[:, 8:16, :]).then_inc(s["x_loaded"], 16)
            sp.dma_start(ctx_in[:, 0, :], ctx_d[0]).then_inc(s["ctx0_loaded"], 16)
            sp.wait_ge(s["stage_zeroed"], 3)
            for w in range(2):
                for b2 in range(2):
                    for hp in range(4):
                        r0 = b2 * 4 + hp
                        sp.dma_start(stage_w[r0:r0 + 121:8, w, 64 * b2:64 * b2 + 64],
                                     w_in[w][16 * hp:16 * hp + 16, :]).then_inc(s["small_loaded"], 16)
                        sp.dma_start(bias_qk[r0:r0 + 121:8, w:w + 1],
                                     b_in[w][16 * hp:16 * hp + 16].rearrange("(a b) -> a b", b=1)
                                     ).then_inc(s["small_loaded"], 16)
            for b2 in range(2):
                sp.dma_start(stage_w[64 * b2:64 * b2 + 64, 2, 64 * b2:64 * b2 + 64],
                             w_in[2]).then_inc(s["small_loaded"], 16)
                sp.dma_start(bias_v[:, 64 * b2:64 * b2 + 64],
                             A["L0_xattn_bv"].rearrange("(a n) -> a n", a=1).broadcast_to([P, 64])
                             ).then_inc(s["small_loaded"], 16)
            sp.dma_start(rt_in, A["L0_ffn_router_w"]).then_inc(s["small_loaded"], 16)
            for n, g in ((0, "g_xattn"), (2, "g_ffn")):
                sp.dma_start(gate_in[:, n:n + 2],
                             A[g].rearrange("(a n) -> a n", a=1).broadcast_to([P, 2])
                             ).then_inc(s["small_loaded"], 16)

            def load_weight_stage(e, m):
                if e == NE:
                    return
                if e:
                    sp.wait_ge(s["wgrp_T"], 6 * (e - 1) + 2 * (m + 1))
                if m < 2:
                    src = A[("L0_ffn_gate_w", "L0_ffn_up_w")[m]][e].rearrange("(t p) h -> p t h", p=P)
                    dst = stage[m].rearrange("p (t h) -> p t h", t=IB)
                else:
                    src = A["L0_ffn_down_w"][e].rearrange("(t p) i -> p t i", p=P)
                    dst = stage[m].rearrange("p (t i) -> p t i", t=2)
                sp.dma_start(dst, src).then_inc(s[f"stage{m}_loaded"], 16)

            def load_mask(b, slot):
                sp.dma_start(mask_in[:, slot, :, :], mask_d[b]).then_inc(s[f"mask{slot}_loaded"], 16)

            def store_parts(par, q):
                sp.wait_ge(s["qk_split"], q + 1)
                sp.dma_start(part_d[par].rearrange("w c r n -> r w c n"),
                             parts[:, :, :, :]).then_inc(s["parts_stored"], 16)

            def load_stacks(par, q):
                sp.wait_ge(s["parts_stored"], 16 * (q + 1))
                for hh in range(2):
                    lo, hi = 64 * hh, 64 * hh + 64
                    src = [[part_d[par, w, c].rearrange("(g d r) n -> g d (r n)", g=2, d=DH)[hh]
                            for c in range(3)] for w in range(2)]
                    for i in range(2):
                        sp.dma_start(
                            q_stack[lo + 24 * i:lo + 24 * i + 24, par, hh, :, :, :].rearrange("r b h n -> r (b h n)"),
                            src[0][i].unsqueeze(1).broadcast_to([DH, 3, 2048])
                        ).then_inc(s["stack_loaded"], 16)
                        sp.dma_start(
                            k_stack[lo + 24 * i:lo + 24 * i + 24, par, :, :, :].rearrange("r b h n -> r (b h n)"),
                            part_d[par, 1].rearrange("c (g d r) n -> g d c (r n)", g=2, d=DH)[hh]
                        ).then_inc(s["stack_loaded"], 16)
                    sp.dma_start(q_stack[lo + 48:lo + 56, par, hh, :, :, :].rearrange("r b h n -> r (b h n)"),
                                 src[0][2]).then_inc(s["stack_loaded"], 16)
                    sp.dma_start(k_stack[lo + 48:lo + 56, par, :, :, :].rearrange("r b h n -> r (b h n)"),
                                 src[1][0]).then_inc(s["stack_loaded"], 16)
                    sp.dma_start(q_stack[lo + 56:lo + 59, par, hh, :, :, :].rearrange("r b h n -> r (b h) n"),
                                 zero_rows[:, :].unsqueeze(1).broadcast_to([3, 8, D])).then_inc(s["stack_loaded"], 16)

            def load_max_rows(c, m):
                par, b2 = c // 2, c % 2
                sp.wait_ge(s["max_rows_loaded"], 1 + 32 * m)
                sp.sem_inc(s["sp_apart"], 1)
                sp.wait_ge(s["maxT_copied"], m + 1)
                for hh in range(2):
                    sp.dma_start(q_stack[64 * hh + 56:64 * hh + 59, par, hh, b2, :, :].rearrange("r h n -> r (h n)"),
                                 max_rows[24 * hh:24 * hh + 24, :]).then_inc(s["max_rows_loaded"], 16)

            def store_token_weights(a, u):
                sp.wait_ge(s["tokw_stored"], 16 + 16 * (2 * a + u))
                sp.sem_inc(s["sp_apart"], 1)
                sp.wait_ge(s["wrow_ready"], 2 * a + u + 1)
                sp.dma_start(tokw_d[(a // 2) % 2, :, bass.ds((a % 2) * 256 + u * P, P)],
                             wrow[:, :]).then_inc(s["tokw_stored"], 16)

            def load_expert_weights(gb, kq):
                sp.wait_ge(s["h_mul"], 1 + 16 * gb + 4 * kq)
                if kq == 0:
                    sp.wait_ge(s["tokw_stored"], 16 + 64 * (gb // 2) + 64)
                    sp.sem_inc(s["sp_apart"], 1)
                sp.dma_start(wb[:, kq % 2, :],
                             tokw_d[(gb // 2) % 2, (gb % 2) * 4 + kq].rearrange("(q t) -> q t", q=1).broadcast_to([P, TILE])
                             ).then_inc(s[f"wb{kq % 2}_loaded"], 16)

            def step(r, c, attention, tail, pair_tail, experts, weights):
                n, par = 4 * r + c, c // 2
                pair = 2 * r + par
                if c % 2 == 1 and pair_tail:
                    store_token_weights(r - 1 if c == 1 else r, 1 - par)
                if experts:
                    load_expert_weights(*expert_step(r, c))
                if attention:
                    if c % 2 == 0:
                        sp.wait_ge(s["scores2_done"], 1 + 8 * n)
                        sp.sem_inc(s["sp_apart"], 1)
                        load_stacks(1 - par, pair + 1)
                        sp.wait_ge(s["v_projected"], pair + 2)
                        sp.dma_start(ctx_in[:, 1 - par, :], ctx_d[(pair + 3) % NPAIR]
                                     ).then_inc(s[f"ctx{1 - par}_loaded"], 16)
                    else:
                        sp.wait_ge(s["stack_loaded"], STACK_DMAS * 16 * (pair + 2))
                        store_parts(par, pair + 2)
                    if weights:
                        for m in range(3):
                            load_weight_stage(n + 1, m)
                    sp.wait_ge(s["max_done"], 16 * n + 32)
                    sp.sem_inc(s["sp_apart"], 1)
                    sp.wait_ge(s["maskT_ready"], n + 2)
                    load_mask((n + 3) % B, (c + 1) % 2)
                    load_max_rows((c + 1) % 4, n + 1)

            sp.dma_start(ctx_in[:, 1, :], ctx_d[1]).then_inc(s["ctx1_loaded"], 16)
            for m in range(3):
                load_weight_stage(0, m)
            load_mask(0, 0)
            load_mask(1, 1)
            store_parts(0, 0)
            load_stacks(0, 0)
            store_parts(1, 1)
            sp.wait_ge(s["v_projected"], 1)
            sp.dma_start(ctx_in[:, 0, :], ctx_d[2]).then_inc(s["ctx0_loaded"], 16)
            sp.wait_ge(s["max_done"], 16)
            sp.wait_ge(s["maskT_ready"], 1)
            load_mask(2, 0)
            load_max_rows(0, 0)
            schedule(sp, step)

            sp.wait_ge(s["yT_T"], 4 * ROUNDS)
            sp.wait_ge(s["down_done"], 2 + UNITS * ROUNDS)
            sp.wait_ge(s["max_rows_loaded"], 1 + 32 * (B + 1))
            sp.wait_ge(s["ctx0_loaded"], 16 * (NPAIR // 2 + 1))
            sp.wait_ge(s["ctx1_loaded"], 16 * (NPAIR // 2 + 1))
            sp.wait_ge(s["parts_stored"], 16 * (NPAIR + 2))
            sp.dma_start(m_u8[:, :, :],
                         A["mask_BxS2_bk0"].rearrange("(q p b) s -> q p (b s)", q=1, b=2).broadcast_to([P, NPAIR, P])
                         ).then_inc(s["mask_m_loaded"], 16)
            for e in range(NE1):
                sp.wait_ge(s["dw_split"], 4 * max(0, e - 1))
                sp.dma_start(d_st[:, e % 2, 0:1024].rearrange("p (t i) -> p t i", t=KT),
                             A["L1_ffn_gate_up_proj"][e].rearrange("(t p) i -> p t i", p=P)
                             ).then_inc(s["d_loaded"], 16)
                sp.dma_start(d_st[:, e % 2, 1024:1536].rearrange("p (t h) -> p t h", t=IB1),
                             A["L1_ffn_down_proj"][e].rearrange("(t p) h -> p t h", p=P)
                             ).then_inc(s["d_loaded"], 16)
                sp.wait_ge(s["d_loaded"], 32 * (e + 1))
            with sp.Fori(0, ROUNDS) as j:
                for u in range(2):
                    sp.wait_ge(s["read_done"], 1 + 2 * j)
                    sp.dma_start(ctx2[:, u, :], ctx_d[2 * j + u]).then_inc(s["cx_loaded"], 16)
                for u in range(2):
                    sp.wait_ge(s["d_out"], 2 * j + u + 1)
                    sp.dma_start(out_d[2 * j + u], xo[:, u, :]).then_inc(s["out_stored"], 16)
                sp.wait_ge(s["out_stored"], 16 + 32 * (j + 1))
                sp.sem_inc(s["sp_apart"], 1)
            sp.wait_ge(s["out_stored"], 16 + 16 * NPAIR)

        @block.gpsimd
        def _(pool):
            pool.sem_inc(s["plo_done"], 2)
            pool.sem_inc(s["h_mul"], 5)
            pool.sem_inc(s["h_split"], 2)
            pool.memset(stage_w[:, :, :], 0.0).then_inc(s["stage_zeroed"], 1)
            pool.memset(zero_rows[:, :], 0.0).then_inc(s["stage_zeroed"], 1)
            pool.memset(ident[:, :], 0.0).then_inc(s["stage_zeroed"], 1)
            pool.wait_ge(s["stage_zeroed"], 3)
            pool.affine_select(out=ident[:, :], in_=ident[:, :], compare_op=ALU.not_equal, fill=1.0,
                               base=0, pattern=[[-1, P]], channel_multiplier=1).then_inc(s["consts_ready"], 1)
            pool.wait_ge(s["consts_ready"], 1)
            pool.tensor_copy(ident_b[:, :], ident[:, :]).then_inc(s["consts_ready"], 1)
            pool.memset(tri[:, :, :], 1.0).then_inc(s["consts_ready"], 1)
            pool.wait_ge(s["consts_ready"], 3)
            pool.affine_select(out=tri[:, :, :], in_=tri[:, :, :], compare_op=ALU.is_gt, fill=0.0,
                               base=0, pattern=[[1, NE], [-1, NE]], channel_multiplier=0).then_inc(s["consts_ready"], 1)
            pool.memset(minus_half[:, :], -0.5).then_inc(s["consts_ready"], 1)
            pool.memset(k_stack[:, :, :, :, :], 1.0).then_inc(s["consts_ready"], 1)
            pool.memset(q_stack[:, :, :, :, :, :], 0.0).then_inc(s["consts_ready"], 1)
            pool.memset(v_parts[:, :, :, :, :], 1.0).then_inc(s["consts_ready"], 1)
            pool.wait_ge(s["consts_ready"], 5)
            pool.wait_ge(s["ln_in"], 1)
            pool.tensor_tensor(rstd[:, :], rstd[:, :], minus_half[:, :], ALU.pow).then_inc(s["pow_done"], 1)

            def p_low(n, hp, mt):
                k = 8 * n + 2 * hp + mt
                pool.wait_ge(s["phi_done"], k + 1)
                pool.tensor_tensor(p_lo[:, hp % 2, mt, :], p32[:, mt, :], p_hi[:, hp % 2, mt, :],
                                   ALU.subtract).then_inc(s["plo_done"], 1)

            def pow2(pair):
                pool.wait_ge(s["ln_in"], 2 + pair)
                pool.tensor_tensor(rstd2[:, :], ve2[:, :], minus_half[:, 0:1], ALU.pow).then_inc(s["pow_done"], 1)

            def h_mul(gb, k):
                if k % IB == 0:
                    pool.wait_ge(s[f"wb{k // IB % 2}_loaded"], 16 * (2 * gb + k // IB // 2 + 1))
                pool.wait_ge(s["up_used"], 1 + UNITS * gb + k + 1)
                pool.tensor_tensor(hb32[:, k % 2, :], hb32[:, k % 2, :], wb[:, (k // IB) % 2, :],
                                   ALU.mult).then_inc(s["h_mul"], 1)

            def h_low(gb, k):
                pool.wait_ge(s["h_hi"], UNITS * gb + k + 1)
                pool.tensor_tensor(hp_lo[:, k % 2, :], hb32[:, k % 2, :], hp_hi[:, k % 2, :], ALU.subtract
                                   ).then_inc(s["h_split"], 1)

            def step(r, c, attention, tail, pair_tail, experts, weights):
                n = 4 * r + c
                for hp in range(4):
                    if experts:
                        gb, kq = expert_step(r, c)
                        h_mul(gb, 4 * kq + hp)
                    if attention:
                        p_low(n, hp, 0)
                    if pair_tail and c % 2 == 0 and hp == 1:
                        pow2(2 * r + c // 2 - 1)
                    if attention:
                        p_low(n, hp, 1)
                    if experts:
                        h_low(gb, 4 * kq + hp)

            schedule(pool, step)

            base_ln = 1 + NPAIR
            pool.wait_ge(s["yT_T"], 4 * ROUNDS)
            pool.wait_ge(s["down_done"], 2 + UNITS * ROUNDS)
            pool.memset(bd[:, :], 0.0).then_inc(s["consts_ready"], 1)
            pool.wait_ge(s["consts_ready"], 9)
            for q in range(2):
                pool.memset(bd[64 * q:64 * q + 64, 64 * q:64 * q + 64], 1.0).then_inc(s["consts_ready"], 1)
            with pool.Fori(0, ROUNDS) as j:
                for i in range(2):
                    pool.wait_ge(s["ln_in"], base_ln + 2 * j + i + 1)
                    pool.tensor_tensor(crs[:, :], cve[:, :], minus_half[:, 0:2], ALU.pow).then_inc(s["pow_done"], 1)
                pool.wait_ge(s["d_up"], 2 * j + 2)
                pool.tensor_tensor(h32, ga, uw, ALU.mult).then_inc(s["d_mul"], 1)

        @block.scalar
        def _(act):
            act.sem_inc(s["y_evac"], 1)
            act.wait_ge(s["small_loaded"], 16 * N_SMALL)
            act.activation(gates[:, :], gate_in[:, :], ACT.Tanh).then_inc(s["gates_ready"], 1)

            def w_high(e, m, k):
                act.wait_ge(s["wgrp_T"], 6 * e + 2 * m + k + 1)
                ps, dst = weight_group(e, m, k, 0)
                act.activation(dst, ps, ACT.Copy, scale=W_SCALE).then_inc(s["w_hi"], 1)

            for w in range(3):
                act.wait_ge(s["wst_T"], 3)
                act.activation(w_bd[:, w, :], psM[:, w * P:w * P + P], ACT.Copy).then_inc(s["bias_ready"], 1)
            def copy_qk(n):
                act.wait_ge(s["qk_projected"], n + 1)
                act.wait_ge(s["qk_split"], n)
                act.activation(qk32[:, 0, :], psM[:, 0:D], ACT.Identity, scale=DH ** -0.5,
                               bias=bias_qs[:, 0:1]).then_inc(s["qk_copied"], 1)
                act.activation(qk32[:, 1, :], psM[:, D:2 * D], ACT.Identity,
                               bias=bias_qk[:, 1:2]).then_inc(s["qk_copied"], 1)

            def copy_maskT(n, slot):
                act.wait_ge(s["maskT_ready"], n + 1)
                act.activation(maskT[:, slot, :, :], psM[:, :].rearrange("p (t n) -> p t n", t=2),
                               ACT.Copy).then_inc(s["maskT_copied"], 1)

            def copy_maxT(n):
                act.wait_ge(s["maxT_ready"], n + 1)
                act.wait_ge(s["max_rows_loaded"], 1 + 32 * n)
                act.activation(max_rows[:, :], psM[:, 0:64].bitcast(BF16)[0:48, :], ACT.Copy
                               ).then_inc(s["maxT_copied"], 1)

            def exps(n, hp, mt):
                k = 8 * n + 2 * hp + mt
                act.wait_ge(s["masked_done"], 1 + k + 1)
                act.activation(p32[:, mt, :], p32[:, mt, :], ACT.Exp, bias=lnscale[:, 0:1]).then_inc(s["exp_done"], 1)
                act.wait_ge(s["pv_done"], 4 * n + hp + 1)
                act.wait_ge(s["exp_done"], k + 1)
                act.activation(p_hi[:, hp % 2, mt, :], p32[:, mt, :], ACT.Copy).then_inc(s["phi_done"], 1)

            def x_high(a, u):
                act.wait_ge(s["xn2T_ready"], 2 * a + u + 1)
                act.activation(xT[:, (a // 2) % 2, 0, :, bass.ds((a % 2) * 256 + u * P, P)],
                               psM[:, 0:2 * P].rearrange("p (k t) -> p k t", k=KT), ACT.Copy,
                               scale=X_SCALE).then_inc(s["xt_hi"], 1)

            def route_exp(n):
                act.wait_ge(s["logits_done"], n + 1)
                act.activation(pe_[:, :], lg[:, :], ACT.Exp, scale=G_UNSCALE, bias=lmax[:, 0:1],
                               accum_out=lsum[:, 0:1]).then_inc(s["route_exp"], 1)

            def block_tanh(gb, k):
                act.wait_ge(s["gate_ready"], UNITS * gb + k + 1)
                act.activation(th, psG[:, :], ACT.Tanh, scale=0.5 * G_UNSCALE).then_inc(s["tanh_done"], 1)

            def block_high(gb, k):
                u = UNITS * gb + k
                act.wait_ge(s["h_mul"], 5 + u + 1)
                act.wait_ge(s["down_done"], u + 1)
                act.activation(hp_hi[:, k % 2, :], hb32[:, k % 2, :], ACT.Copy).then_inc(s["h_hi"], 1)

            def y_out(gb):
                act.wait_ge(s["down_done"], 2 + UNITS * (gb + 1))
                for hb in range(2):
                    act.activation(yT[:, hb, :], psY[:, hb, :], ACT.Copy, scale=1.0 / W_SCALE
                                   ).then_inc(s["y_evac"], 1)

            act.wait_ge(s["exp_bias_set"], 1)

            copy_qk(0)
            copy_maskT(0, 0)
            copy_qk(1)
            copy_maxT(0)

            def step(r, c, attention, tail, pair_tail, experts, weights):
                n, pair = 4 * r + c, 2 * r + c // 2
                for hp in range(4):
                    if experts:
                        gb, kq = expert_step(r, c)
                        block_tanh(gb, 4 * kq + hp)
                    if weights and hp < 3:
                        w_high(n, hp, 0)
                    if pair_tail and c % 2 == 0:
                        if hp == 2:
                            x_high(r - 1 if c == 0 else r, 1 - c // 2)
                        if hp == 3:
                            route_exp(pair - 1)
                    if attention:
                        exps(n, hp, 0)
                    if weights and hp < 3:
                        w_high(n, hp, 1)
                    if attention and hp == 3:
                        copy_maxT(n + 1)
                    if experts:
                        block_high(gb, 4 * kq + hp)
                    if attention:
                        exps(n, hp, 1)
                    if hp == 0 and turns_outputs(r, c):
                        y_out(r - 3)
                    if attention and hp == 0:
                        act.wait_ge(s["masked_done"], 1 + 8 * n)
                        copy_maskT(n + 1, (c + 1) % 2)
                    if attention and c % 2 == 1 and hp == 1:
                        copy_qk(pair + 2)

            schedule(act, step)

            act.wait_ge(s["yT_T"], 4 * ROUNDS)
            with act.Fori(0, ROUNDS) as j:
                for u in range(2):
                    act.wait_ge(s["cxT"], 2 * j + u + 1)
                    act.activation(ctxT[:, u, :, :], psM[:, 0:2 * P].rearrange("p (k t) -> p k t", k=KT),
                                   ACT.Copy).then_inc(s["ctxT_done"], 1)
                for u in range(2):
                    act.wait_ge(s["xn3T"], 2 * j + u + 1)
                    act.activation(x3T[:, u, :, :], psM[:, 0:2 * P].rearrange("p (k t) -> p k t", k=KT),
                                   ACT.Copy).then_inc(s["xt3_done"], 1)
                for u in range(2):
                    act.wait_ge(s["sc_masked"], 2 * j + u + 1)
                    act.activation(pc[:, u, :], sc[:, u, :], ACT.Exp, bias=cmax[:, u:u + 1],
                                   accum_out=csum[:, u:u + 1]).then_inc(s["c_exp"], 1)
                for u in range(2):
                    act.wait_ge(s["pT_ready"], 2 * j + u + 1)
                    act.activation(pT[:, u, :], psM[:, 0:P], ACT.Copy).then_inc(s["pT_done"], 1)
                for u in range(2):
                    act.wait_ge(s["xn4T"], 2 * j + u + 1)
                    for k in range(KT):
                        last = act.activation(x4T[:, 0, k, :, 32 * u:32 * u + 32],
                                              psM[:, k * P:k * P + P].rearrange("p (q e) -> p e q", e=NE1),
                                              ACT.Copy, scale=X_SCALE)
                    last.then_inc(s["xn4_hi"], 1)
                act.wait_ge(s["d_gate"], j + 1)
                act.activation(th, psG[:, :], ACT.Tanh, scale=0.5 * G_UNSCALE).then_inc(s["d_tanh"], 1)
                act.wait_ge(s["d_mul"], j + 1)
                act.activation(hp_hi[:, 0, :], h32, ACT.Copy).then_inc(s["d_hi"], 1)
                act.wait_ge(s["d_down"], j + 1)
                for hb in range(2):
                    act.activation(yT[:, hb, 0:256].rearrange("p (q e) -> p e q", e=NE1),
                                   psY[:, hb, 0:256].rearrange("p (e q) -> p e q", e=NE1),
                                   ACT.Copy, scale=dy_gate[:, 0:1]).then_inc(s["d_yevac"], 1)

        @block.tensor
        def _(pe):
            def mm(out_, lhsT, rhs, start=True, stop=True):
                return pe.matmul(out_, lhsT, rhs, start=start, stop=stop)

            def square(sl):
                return psM[:, sl * P:sl * P + P]

            pe.sem_inc(s["pv_done"], 2)
            pe.sem_inc(s["down_done"], 2)
            for name in ("scores2_done", "read_done"):
                pe.sem_inc(s[name], 1)
            pe.wait_ge(s["small_loaded"], 16 * N_SMALL)
            pe.wait_ge(s["consts_ready"], 2)
            for w in range(3):
                pe.transpose(square(w), stage_w[:, w, :], ident[:, :]).then_inc(s["wst_T"], 1)
            for k in range(KT):
                last = pe.transpose(psY[:, 0, k * NE:k * NE + NE], rt_in[:, k * P:k * P + P], ident[0:NE, 0:NE])
            last.then_inc(s["router_T"], 1)

            def weight_transposes(e, m, k):
                pe.wait_ge(s[f"stage{m}_loaded"], 16 * e + 16)
                pe.wait_ge(s["w_split"], 6 * e + 2 * m + k + 1)
                bank = (psG, psU)[k]
                for i in range(4):
                    if m < 2:
                        src = stage[m].rearrange("p (t h) -> p t h", t=IB)[:, i, k * P:k * P + P]
                    else:
                        src = stage[2].rearrange("p (t i) -> p t i", t=2)[
                            :, i % 2, (2 * k + i // 2) * P:(2 * k + i // 2) * P + P]
                    last = pe.transpose(bank[:, i * P:i * P + P], src, ident[:, :])
                last.then_inc(s["wgrp_T"], 1)

            def project_qk(par, q):
                pe.wait_ge(s["xn_ready"], q + 1)
                pe.wait_ge(s[f"ctx{par}_loaded"], 16 * (q // 2 + 1))
                mm(psM[:, 0:D], w_bd[:, 0, :], xn[:, :])
                mm(psM[:, D:2 * D], w_bd[:, 1, :], ctx_in[:, par, :]).then_inc(s["qk_projected"], 1)

            def project_v(par, q):
                for t in range(2):
                    last = mm(psM[:, t * P:t * P + P], ctx_in[:, par, t * P:t * P + P], w_bd[:, 2, :])
                last.then_inc(s["v_projected"], 1)

            def mask_transposes(n, slot):
                pe.wait_ge(s[f"mask{slot}_loaded"], 16 * (n // 2 + 1))
                for mt in range(2):
                    for nt in range(2):
                        last = pe.transpose(psM[:, mt * 256 + nt * P:mt * 256 + nt * P + P],
                                            mask_in[:, slot, nt, mt * P:mt * P + P], ident[:, :])
                last.then_inc(s["maskT_ready"], 1)

            def first_pass(c, n, i):
                par, b2, hp, hh = c // 2, c % 2, i // 2, i % 2
                pe.wait_ge(s["max_done"], 16 * n + 2 * i)
                for nt in range(2):
                    last = mm(ps1[:, nt, :], q_stack[:, par, hh, b2, hp, nt * P:nt * P + P],
                              k_stack[:, par, b2, hp, :])
                last.then_inc(s["scores1_done"], 1)

            def second_pass(c, n, hp, mt):
                par, b2 = c // 2, c % 2
                pe.wait_ge(s["masked_done"], 1 + 8 * n + 2 * hp + mt)
                mm(ps2[:, :], k_stack[:, par, b2, hp, mt * P:mt * P + P],
                   q_stack[:, par, :, b2, hp, :]).then_inc(s["scores2_done"], 1)

            def times_v(c, n, hp):
                par, b2 = c // 2, c % 2
                pe.wait_ge(s["plo_done"], 2 + 8 * n + 2 * hp + 2)
                for hh in range(2):
                    for nt in range(2):
                        h = 2 * hp + hh
                        dst = psV[:, (nt * H + h) * VC:(nt * H + h + 1) * VC]
                        for i, (part, mt) in enumerate(((p_hi, 0), (p_hi, 1), (p_lo, 0), (p_lo, 1))):
                            at = hh * 256 + nt * P
                            last = mm(dst, part[:, hp % 2, mt, at:at + P], v_parts[:, par, mt, b2 * H + h, :],
                                      start=(i == 0), stop=(i == 3))
                last.then_inc(s["pv_done"], 1)

            def turn_maxima(n):
                pe.wait_ge(s["max_split"], n + 1)
                pe.sem_inc(s["pe_apart"], 1)
                pe.transpose(psM[:, 0:64].bitcast(BF16)[0:48, :],
                             max_parts[:, :, :, :].rearrange("p g c x -> p (g c x)"), ident_b[:, :]
                             ).then_inc(s["maxT_ready"], 1)

            def turn_attention(pair):
                pe.wait_ge(s["on_ready"], 2 * pair + 2)
                for nt in range(2):
                    last = pe.transpose(square(nt), on[:, nt, :], ident[:, :])
                last.then_inc(s["onT_ready"], 1)

            def turn_xn2(pair):
                pe.wait_ge(s["xn2_ready"], pair + 1)
                for k in range(KT):
                    last = pe.transpose(square(k), xn[:, k * P:k * P + P], ident[:, :])
                last.then_inc(s["xn2T_ready"], 1)

            def router(a, u):
                at = bass.ds((a % 2) * 256 + u * P, P)
                tp = (a // 2) % 2
                for k in range(KT):
                    mm(psM[:, 0:2 * NE], xT[:, tp, 0, k, at], w_rt[:, k, :], start=(k == 0), stop=False)
                for k in range(KT):
                    last = mm(psM[:, 0:NE], xT[:, tp, 1, k, at], w_rt[:, k, 0:NE], start=False, stop=(k == KT - 1))
                last.then_inc(s["router_done"], 1)

            def turn_token_weights(pair):
                pe.wait_ge(s["w_ready"], pair + 1)
                pe.transpose(psM[0:NE, 0:P], tokw[:, :], ident[:, :]).then_inc(s["wT_ready"], 1)

            def block_in(gb, k, bank, which, done):
                e = (gb % 2) * 4 + k // IB
                i0 = (k % IB) * P
                tp = (gb // 2) % 2
                n = 0
                for kt in range(KT):
                    for wp, xp in ((0, 0), (1, 0), (0, 1)):
                        last = mm(bank[:, :], w_gu[:, wp, e, which, kt, i0:i0 + P], xT[:, tp, xp, kt, :],
                                  start=(n == 0), stop=(n == 5))
                        n += 1
                last.then_inc(done, 1)

            def block_gate(gb, k):
                u = UNITS * gb + k
                pe.wait_ge(s["gate_used"], 1 + u)
                if k == 0:
                    pe.wait_ge(s["xt_split"], 4 * (gb // 2) + 4)
                block_in(gb, k, psG, 0, s["gate_ready"])

            def block_up(gb, k):
                pe.wait_ge(s["up_used"], 1 + UNITS * gb + k)
                block_in(gb, k, psU, 1, s["up_ready"])

            def block_down(gb, k):
                u = UNITS * gb + k
                e = (gb % 2) * 4 + k // IB
                pe.wait_ge(s["h_split"], 2 + u + 1)
                if k == 0:
                    pe.wait_ge(s["y_evac"], 1 + 2 * gb)
                for hb in range(2):
                    for i, (wp, hpart) in enumerate(((0, hp_hi), (1, hp_hi), (0, hp_lo))):
                        last = mm(psY[:, hb, :], w_dn[:, wp, e, k % IB, hb * P:hb * P + P], hpart[:, k % 2, :],
                                  start=(k == 0 and i == 0), stop=(k == UNITS - 1 and i == 2))
                last.then_inc(s["down_done"], 1)

            def turn_outputs(gb, q):
                if q == 0:
                    pe.wait_ge(s["y_evac"], 1 + 2 * gb + 2)
                for hb in range(2):
                    last = pe.transpose(square(hb), yT[:, hb, q * P:q * P + P], ident[:, :])
                last.then_inc(s["yT_T"], 1)

            pe.wait_ge(s["bias_ready"], 4)
            project_qk(0, 0)
            pe.wait_ge(s["qk_copied"], 2)
            project_v(0, 0)
            pe.wait_ge(s["v_copied"], 1)
            mask_transposes(0, 0)
            pe.wait_ge(s["maskT_copied"], 1)
            project_qk(1, 1)
            pe.wait_ge(s["stack_loaded"], STACK_DMAS * 16)
            for i in range(H):
                first_pass(0, 0, i)
            for i in range(2):
                first_pass(1, 1, i)
            pe.wait_ge(s["qk_copied"], 4)
            turn_maxima(0)

            def step(r, c, attention, tail, pair_tail, experts, weights):
                n, par = 4 * r + c, c // 2
                pair = 2 * r + par
                outputs = turns_outputs(r, c)
                for hp in range(4):
                    k = None
                    if experts:
                        gb, kq = expert_step(r, c)
                        k = 4 * kq + hp
                        block_gate(gb, k)
                    if weights and hp < 3:
                        weight_transposes(n, hp, 0)
                    if attention:
                        i = (2 * hp + 2) % H
                        cm, m = ((c + 1) % 4, n + 1) if hp < 3 else ((c + 2) % 4, n + 2)
                        if hp == 3 and c % 2 == 0:
                            pe.wait_ge(s["stack_loaded"], STACK_DMAS * 16 * (pair + 2))
                        first_pass(cm, m, i)
                        if hp == 0:
                            pe.wait_ge(s["max_rows_loaded"], 1 + 32 * (n + 1))
                        second_pass(c, n, hp, 0)
                    if hp == 0 and attention and c % 2 == 0:
                        pe.wait_ge(s["maxT_copied"], n + 1)
                        if turns_outputs(r, 1) and c == 2:
                            pe.wait_ge(s["y_added"], 4 * (r - 3) + 4)
                        project_v(1 - par, pair + 1)
                    if hp == 1 and pair_tail and c % 2 == 0:
                        if attention:
                            pe.wait_ge(s["maskT_copied"], n + 2)
                        turn_attention(pair - 1)
                    if hp == 1 and outputs:
                        if attention:
                            pe.wait_ge(s["maskT_copied"], n + 2)
                        turn_outputs(r - 3, 0)
                    if hp == 2 and outputs:
                        if attention:
                            pe.wait_ge(s["qk_copied"], 2 * (pair + 2) + 2)
                        else:
                            pe.wait_ge(s["y_added"], 4 * (r - 3) + 1)
                        turn_outputs(r - 3, 1)
                    if hp == 3 and attention:
                        if outputs:
                            pe.wait_ge(s["y_added"], 4 * (r - 3) + 3)
                        elif c % 2 == 0 and pair_tail:
                            pe.wait_ge(s["lg_done"], pair)
                        elif c % 2 == 0:
                            pe.wait_ge(s["maskT_copied"], n + 2)
                        else:
                            pe.wait_ge(s["qk_copied"], 2 * (pair + 2) + 2)
                        turn_maxima(n + 1)

                    if experts:
                        block_up(gb, k)
                    if weights and hp < 3:
                        weight_transposes(n, hp, 1)
                    if attention:
                        first_pass(cm, m, i + 1)
                        second_pass(c, n, hp, 1)
                    if hp == 0 and attention:
                        if c % 2 == 0:
                            pe.wait_ge(s["v_copied"], pair + 2)
                        elif isinstance(r, int) and r == 0 and c == 1:
                            pe.wait_ge(s["maxT_copied"], n + 1)
                        else:
                            pe.wait_ge(s["wrow_ready"], pair)
                        mask_transposes(n + 1, (c + 1) % 2)
                    if hp == 1 and attention and c % 2 == 1:
                        if outputs:
                            pe.wait_ge(s["y_added"], 4 * (r - 3) + 1)
                        else:
                            pe.wait_ge(s["maskT_copied"], n + 2)
                        project_qk(par, pair + 2)
                    if hp == 2 and pair_tail and c % 2 == 0:
                        pe.wait_ge(s["xt_split"], pair)
                        router(r - 1 if c == 0 else r, 1 - par)

                    if k is not None and not (k == 0 and isinstance(r, int) and r == 2):
                        block_down(*((gb, k - 1) if k else (gb - 1, UNITS - 1)))
                    if k is None and hp == 0 and outputs:
                        block_down(r - 3, UNITS - 1)
                    if hp > 0 and attention:
                        if hp == 1:
                            pe.wait_ge(s["pv_evac"], 1 + n)
                            pe.wait_ge(s["v_split"], pair + 1)
                        times_v(c, n, hp - 1)
                    if hp == 0 and tail:
                        times_v((c + 3) % 4, n - 1, 3)
                    if hp == 1 and pair_tail and c % 2 == 0:
                        pe.wait_ge(s["x1_done"], pair)
                        turn_xn2(pair - 1)
                    if hp == 2 and outputs:
                        pe.wait_ge(s["y_added"], 4 * (r - 3) + 2)
                        turn_outputs(r - 3, 2)
                    if hp == 3 and outputs:
                        if attention:
                            pe.wait_ge(s["maxT_copied"], n + 2)
                        else:
                            pe.wait_ge(s["y_added"], 4 * (r - 3) + 3)
                        turn_outputs(r - 3, 3)
                    if hp == 3 and pair_tail and c % 2 == 0:
                        if attention:
                            pe.wait_ge(s["maxT_copied"], n + 2)
                        turn_token_weights(pair - 1)

            schedule(pe, step)

            pe.wait_ge(s["dw_split"], 4 * NE1)
            with pe.Fori(0, ROUNDS) as j:
                for u in range(2):
                    pe.wait_ge(s["cx_loaded"], 32 * (j + 1))
                    for k in range(KT):
                        last = pe.transpose(square(k), ctx2[:, u, k * P:k * P + P], ident[:, :])
                    last.then_inc(s["cxT"], 1)
                    pe.wait_ge(s["ctxT_done"], 2 * j + u + 1)
                pe.wait_ge(s["xn3_ready"], 4 * j + 2)
                for u in range(2):
                    for k in range(KT):
                        last = pe.transpose(square(k), xn3[:, u, k * P:k * P + P], ident[:, :])
                    last.then_inc(s["xn3T"], 1)
                    pe.wait_ge(s["xt3_done"], 2 * j + u + 1)
                for u in range(2):
                    for k in range(KT):
                        last = mm(psM[:, 0:P], x3T[:, u, k, :], ctxT[:, u, k, :], start=(k == 0), stop=(k == 1))
                    last.then_inc(s["sc_done"], 1)
                    pe.wait_ge(s["sc_read"], 2 * j + u + 1)
                for u in range(2):
                    pe.wait_ge(s["c_exp"], 2 * j + u + 1)
                    pe.transpose(psM[:, 0:P], pc[:, u, :], ident[:, :]).then_inc(s["pT_ready"], 1)
                    pe.wait_ge(s["pT_done"], 2 * j + u + 1)
                for u in range(2):
                    mm(psM[:, 0:D], pT[:, u, :], ctx2[:, u, :]).then_inc(s["read_done"], 1)
                    pe.wait_ge(s["x3_done"], 2 * j + u + 1)
                pe.wait_ge(s["xn3_ready"], 4 * j + 4)
                for u in range(2):
                    for k in range(KT):
                        last = pe.transpose(square(k), xn3[:, u, k * P:k * P + P], ident[:, :])
                    last.then_inc(s["xn4T"], 1)
                    pe.wait_ge(s["xn4_split"], 2 * j + u + 1)
                for which, bank, done in ((0, psG, "d_gate"), (1, psU, "d_upT")):
                    for ib in range(IB1):
                        for e in range(NE1):
                            n = 0
                            dst = bank[:, (ib * NE1 + e) * 64:(ib * NE1 + e) * 64 + 64]
                            i0 = which * NI1 + ib * P
                            for kt in range(KT):
                                for wp, xp in ((0, 0), (1, 0), (0, 1)):
                                    last = mm(dst, d_gu[:, wp, e, kt, i0:i0 + P], x4T[:, xp, kt, e, :],
                                              start=(n == 0), stop=(n == 5))
                                    n += 1
                    last.then_inc(s[done], 1)
                pe.wait_ge(s["d_split"], j + 1)
                for hb in range(2):
                    for e in range(NE1):
                        n = 0
                        for ib in range(IB1):
                            at = (ib * NE1 + e) * 64
                            for wp, hpart in ((0, hp_hi), (1, hp_hi), (0, hp_lo)):
                                last = mm(psY[:, hb, e * 64:e * 64 + 64], d_dn[:, wp, e, ib, hb * P:hb * P + P],
                                          hpart[:, 0, at:at + 64], start=(n == 0), stop=(n == 5))
                                n += 1
                last.then_inc(s["d_down"], 1)
                pe.wait_ge(s["d_yevac"], 2 * j + 2)
                for u in range(2):
                    for hb in range(2):
                        last = pe.transpose(square(hb), yT[:, hb, u * P:u * P + P], ident[:, :])
                    last.then_inc(s["d_yT"], 1)
                    pe.wait_ge(s["d_out"], 2 * j + u + 1)

        @block.vector
        def _(dve):
            st = Steps(dve, s["dve_step"], s["dve_apart"])
            dve.sem_inc(s["w_split"], 2)
            for name in ("up_used", "masked_done", "pv_evac", "gate_used"):
                dve.sem_inc(s[name], 1)
            dve.memset(lnscale[:, :], LN_P_SCALE).then_inc(s["exp_bias_set"], 1)
            dve.wait_ge(s["exp_bias_set"], 1)
            dve.wait_ge(s["x_loaded"], 32)
            for p in range(NPAIR):
                st.link(dve.bn_stats(stats[:, :], x_res[:, p, :]))
                st.link(dve.bn_aggr(mean_var[:, p, :], stats[:, :]))
            dve.tensor_scalar(rstd[:, :], mean_var[:, :, 1], EPS, None, ALU.add).then_inc(s["ln_in"], 1)
            dve.wait_ge(s["small_loaded"], 16 * N_SMALL)
            dve.tensor_scalar(bias_qs[:, :], bias_qk[:, 0:1], DH ** -0.5, None, ALU.mult).then_inc(s["bias_ready"], 1)
            dve.wait_ge(s["router_T"], 1)
            for k in range(KT):
                st.link(dve.tensor_scalar(w_rt[:, k, 0:NE], psY[:, 0, k * NE:k * NE + NE], W_SCALE, None, ALU.mult))
                st.link(dve.scalar_tensor_tensor(out=w_rt[:, k, NE:2 * NE], in0=psY[:, 0, k * NE:k * NE + NE],
                                                 scalar=W_SCALE, in1=w_rt[:, k, 0:NE], op0=ALU.mult,
                                                 op1=ALU.subtract))

            def w_low(e, m, k):
                dve.wait_ge(s["w_hi"], 6 * e + 2 * m + k + 1)
                ps, hi = weight_group(e, m, k, 0)
                dve.scalar_tensor_tensor(out=weight_group(e, m, k, 1)[1], in0=ps, scalar=W_SCALE, in1=hi,
                                         op0=ALU.mult, op1=ALU.subtract).then_inc(s["w_split"], 1)

            def norm1(pair, n):
                dve.wait_ge(s["qk_projected"], n)
                if isinstance(n, int) and n < 2:
                    dve.wait_ge(s["pow_done"], 1)
                dve.tensor_scalar(xn[:, :], x_res[:, pair, :], mean_var[:, pair, 0:1],
                                  rstd[:, bass.ds(pair, 1)], ALU.subtract, ALU.mult).then_inc(s["xn_ready"], 1)

            def cut3(dst, src, remain, after):
                st.link(dve.tensor_copy(dst[0], src))
                st.link(dve.tensor_tensor(remain, src, dst[0], ALU.subtract))
                st.link(dve.tensor_copy(dst[1], remain))
                dve.tensor_tensor(dst[2], remain, dst[1], ALU.subtract).then_inc(after, 1)

            def cut_qk(q):
                dve.wait_ge(s["qk_copied"], 2 * q + 2)
                dve.wait_ge(s["parts_stored"], 16 * q)
                dve.wait_ge(s["v_split"], q)
                cut3([parts[:, :, c, :] for c in range(3)], qk32[:, :, :], rem[:, :, :], s["qk_split"])

            def bias_to_v(q):
                dve.wait_ge(s["v_projected"], q + 1)
                dve.wait_ge(s["qk_split"], q + 1)
                vps = psM[:, 0:2 * P].rearrange("p (t c) -> p t c", t=2)
                dve.tensor_tensor(rem[:, :, P:2 * P], vps, bias_v[:, :].unsqueeze(1).broadcast_to([P, 2, P]),
                                  ALU.add).then_inc(s["v_copied"], 1)

            def cut_v(par, q):
                dve.wait_ge(s["v_copied"], q + 1)
                v = rem[:, :, P:2 * P].rearrange("p t (g d) -> p t g d", d=DH)
                r = rem[:, :, 0:P].rearrange("p t (g d) -> p t g d", d=DH)
                dst = [v_parts[:, par, :, :, DH * c:DH * c + DH] for c in range(3)]
                cut3(dst, v, r, s["v_split"])

            def maxima(c, m, i):
                dve.wait_ge(s["scores1_done"], 8 * m + i + 1)
                st.apart()
                for nt in range(2):
                    hp, hh = i // 2, i % 2
                    col = hh * 8 + hp * 2 + nt
                    dve.tensor_tensor_reduce(out=ps1[:, nt, :], in0=ps1[:, nt, :], in1=mask_in[:, c % 2, nt, :],
                                             scale=1.0, scalar=LOW, op0=ALU.add, op1=ALU.max,
                                             accum_out=row_max[:, col:col + 1]).then_inc(s["max_done"], 1)

            def cut_max(m):
                dve.wait_ge(s["max_done"], 16 * m + 16)
                dve.wait_ge(s["maxT_ready"], m)
                rm = row_max[:, :].rearrange("p (g c) -> p g c", g=2)
                rr = max_rem[:, :].rearrange("p (g c) -> p g c", g=2)
                st.link(dve.tensor_scalar(max_parts[:, :, 0, :], rm, -1.0, None, ALU.mult))
                st.link(dve.scalar_tensor_tensor(out=rr, in0=rm, scalar=-1.0, in1=max_parts[:, :, 0, :],
                                                 op0=ALU.mult, op1=ALU.subtract))
                st.link(dve.tensor_copy(max_parts[:, :, 1, :], rr))
                dve.tensor_tensor(max_parts[:, :, 2, :], rr, max_parts[:, :, 1, :], ALU.subtract
                                  ).then_inc(s["max_split"], 1)

            def add_mask(c, n, hp, mt):
                k = 8 * n + 2 * hp + mt
                dve.wait_ge(s["scores2_done"], 1 + k + 1)
                dve.wait_ge(s["plo_done"], k + 1)
                dve.tensor_tensor(p32[:, mt, :].rearrange("p (g n) -> p g n", g=2),
                                  ps2[:, :].rearrange("p (g n) -> p g n", g=2),
                                  maskT[:, c % 2, mt, :].unsqueeze(1).broadcast_to([P, 2, 256]), ALU.add
                                  ).then_inc(s["masked_done"], 1)

            def pv_out(c, n):
                b2 = c % 2
                dve.wait_ge(s["pv_done"], 2 + 4 * n + 4)
                pv = psV[:, 0:2 * H * VC].rearrange("p (g c) -> p g c", c=VC)
                dve.tensor_reduce(o_sum[:, :, :, :].rearrange("p t h d -> p (t h) d"),
                                  pv[:, :, 0:3 * DH].rearrange("p g (c d) -> p g d c", c=3), AX.X, ALU.add)
                dve.reciprocal(o_rec[:, :, :].rearrange("p t h -> p (t h)"), pv[:, :, 3 * DH]
                               ).then_inc(s["pv_evac"], 1)
                dve.wait_ge(s["pv_evac"], 1 + n + 1)
                st.link(dve.tensor_scalar(o_rec[:, :, :], o_rec[:, :, :], gates[:, 0:1], None, ALU.mult))
                dve.tensor_tensor(on[:, :, 64 * b2:64 * b2 + 64].rearrange("p t (h d) -> p t h d", d=DH),
                                  o_sum[:, :, :, :], o_rec[:, :, :].unsqueeze(3).broadcast_to([P, 2, H, DH]),
                                  ALU.mult).then_inc(s["on_ready"], 1)

            def attention_to_x(pair):
                dve.wait_ge(s["onT_ready"], pair + 1)
                dve.tensor_tensor(x_res[:, pair, :], x_res[:, pair, :], psM[:, 0:D], ALU.add
                                  ).then_inc(s["x1_done"], 1)
                dve.wait_ge(s["x1_done"], pair + 1)
                st.apart()
                st.link(dve.bn_stats(stats[:, :], x_res[:, pair, :]))
                st.apart()
                st.link(dve.bn_aggr(mv2[:, :], stats[:, :]))
                dve.tensor_scalar(ve2[:, :], mv2[:, 1:2], EPS, None, ALU.add).then_inc(s["ln_in"], 1)

            def norm2(pair):
                dve.wait_ge(s["pow_done"], pair + 2)
                dve.wait_ge(s["qk_projected"], pair + 3)
                dve.tensor_scalar(xn[:, :], x_res[:, pair, :], mv2[:, 0:1], rstd2[:, 0:1],
                                  ALU.subtract, ALU.mult).then_inc(s["xn2_ready"], 1)

            def x_low(a, u):
                dve.wait_ge(s["xt_hi"], 2 * a + u + 1)
                at = bass.ds((a % 2) * 256 + u * P, P)
                dve.scalar_tensor_tensor(out=xT[:, (a // 2) % 2, 1, :, at],
                                         in0=psM[:, 0:2 * P].rearrange("p (k t) -> p k t", k=KT), scalar=X_SCALE,
                                         in1=xT[:, (a // 2) % 2, 0, :, at], op0=ALU.mult,
                                         op1=ALU.subtract).then_inc(s["xt_split"], 1)

            def logits(pair):
                dve.wait_ge(s["router_done"], pair + 1)
                dve.tensor_reduce(lg[:, :], psM[:, 0:2 * NE].rearrange("p (c e) -> p e c", c=2), AX.X, ALU.add
                                  ).then_inc(s["lg_done"], 1)
                dve.wait_ge(s["lg_done"], pair + 1)
                st.link(dve.tensor_reduce(lmax[:, :], lg[:, :], AX.X, ALU.max, negate=True))
                dve.tensor_scalar(lmax[:, :], lmax[:, :], G_UNSCALE, None, ALU.mult).then_inc(s["logits_done"], 1)

            def route(pair):
                dve.wait_ge(s["route_exp"], pair + 1)
                st.link(dve.reciprocal(lsum[:, :], lsum[:, :]))
                st.link(dve.tensor_scalar(pe_[:, :], pe_[:, :], lsum[:, 0:1], None, ALU.mult))
                pj = pe_[:, :].unsqueeze(1).broadcast_to([P, NE, NE])
                pi = pe_[:, :].unsqueeze(2).broadcast_to([P, NE, NE])
                dve.tensor_tensor(gt[:, :, :], pj, pi, ALU.is_gt)
                st.link(dve.tensor_tensor(ge[:, :, :], pj, pi, ALU.is_equal))
                st.link(dve.tensor_tensor(ge[:, :, :], ge[:, :, :], tri[:, :, :], ALU.mult))
                st.link(dve.tensor_tensor(gt[:, :, :], gt[:, :, :], ge[:, :, :], ALU.add))
                st.link(dve.tensor_tensor(gt[:, :, :], gt[:, :, :], pj, ALU.mult))
                st.link(dve.tensor_reduce(excl[:, :], gt[:, :, :], AX.X, ALU.add))
                st.link(dve.tensor_scalar(keep[:, :], excl[:, :], 0.9, gates[:, 2:3], ALU.is_le, ALU.mult))
                dve.scalar_tensor_tensor(out=tokw[:, :], in0=pe_[:, :], scalar=0.5 * G_UNSCALE * G_UNSCALE,
                                         in1=keep[:, :], op0=ALU.mult, op1=ALU.mult).then_inc(s["w_ready"], 1)

            def token_weight_rows(pair):
                dve.wait_ge(s["wT_ready"], pair + 1)
                dve.wait_ge(s["tokw_stored"], 16 + 16 * pair)
                dve.tensor_copy(wrow[:, :], psM[0:NE, 0:P]).then_inc(s["wrow_ready"], 1)

            def gate_mul(gb, k):
                u = UNITS * gb + k
                dve.wait_ge(s["tanh_done"], u + 1)
                dve.wait_ge(s["up_used"], 1 + u)
                dve.scalar_tensor_tensor(out=ga, in0=th, scalar=1.0, in1=psG[:, :], op0=ALU.add,
                                         op1=ALU.mult).then_inc(s["gate_used"], 1)

            def up_mul(gb, k):
                u = UNITS * gb + k
                dve.wait_ge(s["up_ready"], u + 1)
                dve.wait_ge(s["gate_used"], 1 + u + 1)
                dve.wait_ge(s["h_split"], u + 1)
                dve.tensor_tensor(hb32[:, k % 2, :], psU[:, :], ga, ALU.mult).then_inc(s["up_used"], 1)

            def add_experts(gb, q):
                dve.wait_ge(s["yT_T"], 4 * gb + q + 1)
                row = 4 * (gb // 2) + q
                dve.tensor_tensor(x_res[:, row, :], x_res[:, row, :], psM[:, 0:D],
                                  ALU.add).then_inc(s["y_added"], 1)

            dve.wait_ge(s["consts_ready"], 8)
            norm1(0, 0)
            cut_qk(0)
            bias_to_v(0)
            cut_v(0, 0)
            norm1(1, 1)
            cut_qk(1)
            dve.wait_ge(s["mask0_loaded"], 16)
            for i in range(H):
                maxima(0, 0, i)
            cut_max(0)
            dve.wait_ge(s["mask1_loaded"], 16)
            for i in range(2):
                maxima(1, 1, i)

            def step(r, c, attention, tail, pair_tail, experts, weights):
                n, par = 4 * r + c, c // 2
                pair = 2 * r + par
                outputs = turns_outputs(r, c)
                if c == 0:
                    st.enter_round(r)
                for hp in range(4):
                    if hp == 3 and attention:
                        cut_max(n + 1)
                    if attention:
                        i = (2 * hp + 2) % H
                        cm, m = ((c + 1) % 4, n + 1) if hp < 3 else ((c + 2) % 4, n + 2)
                        if hp == 3:
                            dve.wait_ge(s[f"mask{c % 2}_loaded"], 16 * ((n + 2) // 2 + 1))
                        maxima(cm, m, i)
                        if hp == 0:
                            dve.wait_ge(s["maskT_copied"], n + 1)
                        add_mask(c, n, hp, 0)
                    if hp == 0 and c % 2 == 1 and pair_tail:
                        token_weight_rows(pair - 1)
                    if hp == 2 and c % 2 == 0 and pair_tail:
                        x_low(r - 1 if c == 0 else r, 1 - par)
                    if experts:
                        gb, kq = expert_step(r, c)
                        gate_mul(gb, 4 * kq + hp)
                    if weights and hp < 3:
                        w_low(n, hp, 0)
                    if hp == 0 and c % 2 == 0 and attention:
                        bias_to_v(pair + 1)
                    if hp == 0 and c % 2 == 1 and attention:
                        norm1((pair + 2) % NPAIR, pair + 2)
                    if hp == 1 and c % 2 == 0 and pair_tail:
                        attention_to_x(pair - 1)
                    if hp == 1 and outputs:
                        add_experts(r - 3, 0)
                    if hp == 2 and outputs:
                        add_experts(r - 3, 1)
                    if hp == 2 and c % 2 == 1 and attention:
                        cut_qk(pair + 2)
                    if hp == 3 and c % 2 == 0 and pair_tail:
                        route(pair - 1)
                    if experts:
                        up_mul(gb, 4 * kq + hp)
                    if weights and hp < 3:
                        w_low(n, hp, 1)
                    if attention:
                        maxima(cm, m, i + 1)
                        add_mask(c, n, hp, 1)
                    if hp == 0 and tail:
                        pv_out((c + 3) % 4, n - 1)
                    if hp == 0 and c % 2 == 0 and attention:
                        cut_v(1 - par, pair + 1)
                    if hp == 1 and c % 2 == 0 and pair_tail:
                        norm2(pair - 1)
                    if hp == 2 and c % 2 == 0 and pair_tail:
                        logits(pair - 1)
                    if hp == 2 and outputs:
                        add_experts(r - 3, 2)
                    if hp == 3 and outputs:
                        add_experts(r - 3, 3)

            schedule(dve, step)

            base1 = st.base + st.n
            st.at(base1)
            dve.wait_ge(s["y_added"], 4 * ROUNDS)
            st.link(dve.tensor_scalar(dy_gate[:, :], gates[:, 3:4], 1.0 / W_SCALE, None, ALU.mult))
            for e in range(NE1):
                dve.wait_ge(s["d_loaded"], 32 * (e + 1))
                g_in = d_st[:, e % 2, 0:1024].rearrange("p (t i) -> p t i", t=KT)
                d_in = d_st[:, e % 2, 1024:1536].rearrange("p (t i) -> p t i", t=IB1)
                for src, dst in ((g_in, d_gu), (d_in, d_dn)):
                    st.link(dve.tensor_scalar(dst[:, 0, e, :, :], src, W_SCALE, None, ALU.mult))
                    dve.scalar_tensor_tensor(out=dst[:, 1, e, :, :], in0=src, scalar=W_SCALE, in1=dst[:, 0, e, :, :],
                                             op0=ALU.mult, op1=ALU.subtract).then_inc(s["dw_split"], 2)
            base2 = base1 + st.n
            dve.wait_ge(s["mask_m_loaded"], 16)
            dve.wait_ge(s["consts_ready"], 11)

            def late_norm(j, i):
                for u in range(2):
                    st.apart()
                    st.link(dve.bn_stats(cstat[:, u, :], x_res[:, 2 * j + u, :]))
                for u in range(2):
                    st.apart()
                    st.link(dve.bn_aggr(cmv[:, u, :], cstat[:, u, :]))
                dve.tensor_scalar(cve[:, :], cmv[:, :, 1], EPS, None, ALU.add).then_inc(s["ln_in"], 1)
                dve.wait_ge(s["pow_done"], 1 + NPAIR + 2 * j + i + 1)
                for u in range(2):
                    dve.tensor_scalar(xn3[:, u, :], x_res[:, 2 * j + u, :], cmv[:, u, 0:1], crs[:, u:u + 1],
                                      ALU.subtract, ALU.mult).then_inc(s["xn3_ready"], 1)

            with dve.Fori(0, ROUNDS) as j:
                st.at(base2 + j * LATE_STEPS)
                for u in range(2):
                    dve.tensor_tensor(mm[:, u, :], m_u8[:, 2 * j + u, :], bd[:, :], ALU.mult
                                      ).then_inc(s["mask_m_ready"], 1)
                dve.wait_ge(s["mask_m_ready"], 2 * j + 2)
                st.link(dve.tensor_scalar(neg[:, :, :], mm[:, :, :], 1.0, 1.0e30, ALU.subtract, ALU.mult))
                st.link(dve.tensor_reduce(valid[:, :], mm[:, :, :], AX.X, ALU.max))
                st.link(dve.tensor_scalar(valid[:, :], valid[:, :], gates[:, 1:2], None, ALU.mult))
                late_norm(j, 0)
                for u in range(2):
                    dve.wait_ge(s["sc_done"], 2 * j + u + 1)
                    dve.scalar_tensor_tensor(out=sc[:, u, :], in0=psM[:, 0:P], scalar=D ** -0.5,
                                             in1=mm[:, u, :], op0=ALU.mult, op1=ALU.mult).then_inc(s["sc_read"], 1)
                    dve.wait_ge(s["sc_read"], 2 * j + u + 1)
                    st.link(dve.tensor_tensor(sc[:, u, :], sc[:, u, :], neg[:, u, :], ALU.add))
                    dve.tensor_reduce(cmax[:, u:u + 1], sc[:, u, :], AX.X, ALU.max, negate=True
                                      ).then_inc(s["sc_masked"], 1)
                dve.wait_ge(s["c_exp"], 2 * j + 2)
                st.link(dve.reciprocal(csum[:, :], csum[:, :]))
                st.link(dve.tensor_tensor(cr[:, :], csum[:, :], valid[:, :], ALU.mult))
                for u in range(2):
                    xv = x_res[:, 2 * j + u, :]
                    dve.wait_ge(s["read_done"], 1 + 2 * j + u + 1)
                    dve.scalar_tensor_tensor(out=xv, in0=psM[:, 0:D], scalar=cr[:, u:u + 1], in1=xv,
                                             op0=ALU.mult, op1=ALU.add).then_inc(s["x3_done"], 1)
                dve.wait_ge(s["x3_done"], 2 * j + 2)
                dve.wait_ge(s["xn3T"], 2 * j + 2)
                late_norm(j, 1)
                for u in range(2):
                    dve.wait_ge(s["xn4_hi"], 2 * j + u + 1)
                    for k in range(KT):
                        last = dve.scalar_tensor_tensor(out=x4T[:, 1, k, :, 32 * u:32 * u + 32],
                                                        in0=psM[:, k * P:k * P + P].rearrange("p (q e) -> p e q", e=NE1),
                                                        scalar=X_SCALE, in1=x4T[:, 0, k, :, 32 * u:32 * u + 32],
                                                        op0=ALU.mult, op1=ALU.subtract)
                    last.then_inc(s["xn4_split"], 1)
                dve.wait_ge(s["d_tanh"], j + 1)
                dve.scalar_tensor_tensor(out=ga, in0=th, scalar=1.0, in1=psG[:, :], op0=ALU.add,
                                         op1=ALU.mult).then_inc(s["d_up"], 1)
                dve.wait_ge(s["d_upT"], j + 1)
                dve.tensor_scalar(uw, psU[:, :], 0.5 * G_UNSCALE * G_UNSCALE, None, ALU.mult
                                  ).then_inc(s["d_up"], 1)
                dve.wait_ge(s["d_hi"], j + 1)
                dve.tensor_tensor(hp_lo[:, 0, :], h32, hp_hi[:, 0, :], ALU.subtract).then_inc(s["d_split"], 1)
                dve.wait_ge(s["out_stored"], 16 + 32 * j)
                for u in range(2):
                    dve.wait_ge(s["d_yT"], 2 * j + u + 1)
                    dve.tensor_tensor(xo[:, u, :], psM[:, 0:D], x_res[:, 2 * j + u, :],
                                      ALU.add).then_inc(s["d_out"], 1)
            assert st.n == LATE_STEPS, st.n


_INS = ["x", "ctx_2048", "mask_Bx2048x2048_ff0", "mask_BxS2_bk0", "g_xattn", "g_ffn", "L0_xattn_Wq",
        "L0_xattn_bq", "L0_xattn_Wk", "L0_xattn_bk", "L0_xattn_Wv", "L0_xattn_bv", "L0_ffn_router_w",
        "L0_ffn_gate_w", "L0_ffn_up_w", "L0_ffn_down_w", "L1_ffn_gate_up_proj", "L1_ffn_down_proj"]


def kernel(**inputs):
    import numpy as _np
    import concourse.bacc as _bacc
    from concourse import mybir as _mybir
    from concourse.bass_utils import run_bass_kernel_spmd as _run

    nc = _bacc.Bacc("TRN2", target_bir_lowering=False, num_devices=1)
    arrays, args = {}, {}
    for name in _INS:
        a = _np.ascontiguousarray(inputs[name])
        arrays[f"in_{name}"] = a
        args[name] = nc.dram_tensor(f"in_{name}", a.shape, _mybir.dt.from_np(a.dtype), kind="ExternalInput").ap()
    out = nc.dram_tensor("out_0", (B, S, D), F32, kind="ExternalOutput").ap()
    build(nc, args, out)
    r = _run(nc, [arrays], core_ids=[0])
    return r.results[0]["out_0"]
```

```python
from contextlib import ExitStack

import concourse.bass as bass
from concourse import mybir

F32 = mybir.dt.float32
BF16 = mybir.dt.bfloat16
F16 = mybir.dt.float16
U8 = mybir.dt.uint8
ALU = mybir.AluOpType
ACT = mybir.ActivationFunctionType
AX = mybir.AxisListType

B, S, D = 32, 64, 256
P = 128
NPAIR = B * S // P
H, DH = 8, 8
NE, NI = 8, 512
NE1, NI1 = 4, 256
ROUNDS = B // 4
TILE = 512
KT = D // P
IB = NI // P
IB1 = NI1 // P
UNITS = 4 * IB
VC = 3 * DH + 1
EPS = 1e-5
ROUND_STEPS = 50
LATE_START = 4 * ROUNDS + 3
LAST_OUTPUTS = 4 * ROUNDS + 9
CUT_STEP = {4 * ROUNDS + 1: {2: 0, 3: 1}, 4 * ROUNDS + 2: {0: 2, 1: 3}}
W_SCALE = 64.0
X_SCALE = 256.0
G_UNSCALE = 1.0 / (W_SCALE * X_SCALE)
LN_P_SCALE = 12 * 0.6931471805599453
LOW = -3.0e38


class Steps:

    def __init__(self, eng, sem, met):
        self.eng, self.sem, self.met, self.n, self.base = eng, sem, met, 0, 0

    def at(self, base):
        self.base, self.n = base, 0

    def enter_round(self, r):
        if not isinstance(r, int):
            self.loop_start = self.base + self.n
            self.at(self.loop_start + (r - 3) * ROUND_STEPS)
        elif r == ROUNDS:
            assert self.n == ROUND_STEPS, self.n
            self.at(self.loop_start + (ROUNDS - 3) * ROUND_STEPS)

    def apart(self):
        self.eng.sem_inc(self.met, 1)

    def link(self, instruction):
        self.n += 1
        instruction.then_inc(self.sem, 1)
        self.eng.wait_ge(self.sem, self.base + self.n)


def build(nc, A, out):
    ctx = ExitStack()

    def sb(name, shape, dt):
        return ctx.enter_context(nc.sbuf_tensor(name, shape, dt))

    def sem(name):
        return ctx.enter_context(nc.semaphore(name))

    x_d = A["x"].rearrange("(p b) s d -> (b s) p d", b=2)
    ctx_d = A["ctx_2048"].rearrange("(p b) s d -> p (b s) d", b=2)
    mask_d = A["mask_Bx2048x2048_ff0"].rearrange("b (t n) m -> b n t m", t=2)
    part_d = nc.dram_tensor("part_scratch", (2, 2, 3, P, D), BF16, kind="Internal").ap()
    tokw_d = nc.dram_tensor("tokw_scratch", (2, NE, TILE), F32, kind="Internal").ap()

    with ctx:
        ident = sb("ident", [P, P], F32)
        ident_b = sb("ident_b", [P, P], BF16)
        minus_half = sb("minus_half", [P, NPAIR], F32)
        gates = sb("gates", [P, 4], F32)
        gate_in = sb("gate_in", [P, 4], F32)
        x_res = sb("x_res", [P, NPAIR, D], F32)
        stats = sb("stats", [P, 6], F32)
        mean_var = sb("mean_var", [P, NPAIR, 2], F32)
        rstd = sb("rstd", [P, NPAIR], F32)
        mv2 = sb("mv2", [P, 2], F32)
        ve2 = sb("ve2", [P, 1], F32)
        rstd2 = sb("rstd2", [P, 1], F32)
        xn = sb("xn", [P, D], F32)
        th_ga_h = sb("th_ga_h", [P, 4, TILE], F32)
        th, ga, hb32 = th_ga_h[:, 0, :], th_ga_h[:, 1, :], th_ga_h[:, 2:4, :]
        hp_hi = sb("hp_hi", [P, 2, TILE], F16)
        hp_lo = sb("hp_lo", [P, 2, TILE], F16)
        yT = sb("yT", [P, 2, TILE], F32)

        psG = ctx.enter_context(nc.psum_tensor("psG", [P, 512], F32))
        psU = ctx.enter_context(nc.psum_tensor("psU", [P, 512], F32))
        psY = ctx.enter_context(nc.psum_tensor("psY", [P, 2, 512], F32))
        ps1 = ctx.enter_context(nc.psum_tensor("ps1", [P, 2, 256], F32))
        ps2 = ctx.enter_context(nc.psum_tensor("ps2", [P, 512], F32))
        psV = ctx.enter_context(nc.psum_tensor("psV", [P, 512], F32))
        psM = ctx.enter_context(nc.psum_tensor("psM", [P, 512], F32))

        lnscale = sb("lnscale", [P, 1], F32)
        bd = sb("bd", [P, P], F32)

        names = """x01_loaded ln01_in pow01_done stacks_set bias_set bias_turned biasT_ready x_loaded
            small_loaded stage0_loaded stage1_loaded stage2_loaded ctx0_loaded ctx1_loaded
            mask0_loaded mask1_loaded parts_stored stack_loaded max_rows_loaded tokw_stored
            wb0_loaded wb1_loaded out_stored consts_ready zeroed exp_bias_set gates_ready
            v_copied x1_done lg_done y_added x3_done d_upT wst_T router_T wgrp_T w_copied w_hi
            w_split bias_ready ln_in pow_done xn_ready qk_projected v_projected qk_copied
            qk_split v_split maskT_ready maskT_copied scores1_done max_done max_split
            maxT_ready maxT_copied scores2_done masked_done exp_done phi_done plo_done pv_done
            pv_evac on_ready onT_ready xn2_ready xn2T_ready xt_hi xt_split router_done
            logits_done route_exp w_ready wT_ready wrow_ready gate_ready up_ready tanh_done
            gate_used up_used h_mul h_hi h_split down_done y_evac yT_T dve_step dve_apart
            pe_apart sp_apart d0_loaded d1_loaded dw_split xt3_done ctxT_done sc_done sc_masked
            c_exp pT_ready pT_done read_done xn4T xn4_hi xn4_split cx0_loaded cx1_loaded d_gate
            d_tanh d_mul d_hi d_split d_down d_yevac d_yT d_out xn3_ready xn3T cxT
            mask_m_loaded bd_ready""".split()
        s = {n: sem(n) for n in names}

        w_gu = sb("w_gu", [P, 2, NE, 2, KT, NI], F16)
        w_dn = sb("w_dn", [P, 2, NE, IB, D], F16)
        w_rt = sb("w_rt", [P, KT, 2 * NE], F16)
        xT = sb("xT", [P, 2, 2, KT, TILE], F16)
        wb = sb("wb", [P, 2, TILE], F32)

        early = ExitStack()

        def eb(name, shape, dt):
            return early.enter_context(nc.sbuf_tensor(name, shape, dt))

        wrow = eb("wrow", [NE, P], F32)
        w_bd = eb("w_bd", [P, 3, P], F32)
        bias_qk = eb("bias_qk", [P, 2], F32)
        bias_qs = eb("bias_qs", [P, 1], F32)
        bias_row = eb("bias_row", [1, 2, S], F32)
        bias_turn = eb("bias_turn", [1, 2, P], F32)
        bias_v = eb("bias_v", [P, P], F32)
        tri = eb("tri", [P, NE, NE], F32)
        ctx_in = eb("ctx_in", [P, 2, D], F32)
        qk32 = eb("qk32", [P, 2, D], F32)
        rem = eb("rem", [P, 2, D], F32)
        parts = eb("parts", [P, 2, 3, D], BF16)
        v_parts = eb("v_parts", [P, 2, 2, 2 * H, VC], BF16)
        mask_in = eb("mask_in", [P, 2, 2, 256], F32)
        maskT = eb("maskT", [P, 2, 2, 256], F32)
        q_stack = eb("q_stack", [P, 2, 2, 2, 4, D], BF16)
        k_stack = eb("k_stack", [P, 2, 2, 4, D], BF16)
        zero_rows = eb("zero_rows", [3, D], BF16)
        row_max = eb("row_max", [P, 16], F32)
        max_rem = eb("max_rem", [P, 16], F32)
        max_parts = eb("max_parts", [P, 2, 3, 8], BF16)
        max_rows = eb("max_rows", [48, P], BF16)
        p32 = eb("p32", [P, 2, 512], F32)
        p_hi = eb("p_hi", [P, 2, 2, 512], F16)
        p_lo = eb("p_lo", [P, 2, 2, 512], F16)
        o_sum = eb("o_sum", [P, 2, H, DH], F32)
        o_rec = eb("o_rec", [P, 2, H], F32)
        on = eb("on", [P, 2, P], F32)
        lg = eb("lg", [P, NE], F32)
        lmax = eb("lmax", [P, 1], F32)
        pe_ = eb("probs", [P, NE], F32)
        lsum = eb("lsum", [P, 1], F32)
        gt = eb("gt", [P, NE, NE], F32)
        ge = eb("ge", [P, NE, NE], F32)
        excl = eb("excl", [P, NE], F32)
        keep = eb("keep", [P, NE], F32)
        tokw = eb("tokw", [P, NE], F32)
        stage_w = maskT[:, :, :, :].rearrange("p a b n -> p (a b n)")[:, 0:3 * P].rearrange("p (w c) -> p w c", w=3)
        stage = [yT[:, :, :].rearrange("p a b -> p (a b)"),
                 th_ga_h[:, 0:2, :].rearrange("p a b -> p (a b)"),
                 th_ga_h[:, 2:4, :].rearrange("p a b -> p (a b)")]
        rt_in = on[0:NE, :, :].rearrange("p t c -> p (t c)")
        early.close()

        late = ExitStack()

        def lb(name, shape, dt):
            return late.enter_context(nc.sbuf_tensor(name, shape, dt))

        d_gu = lb("d_gu", [P, 2, NE1, KT, 2 * NI1], F16)
        d_dn = lb("d_dn", [P, 2, NE1, IB1, D], F16)
        d_st = lb("d_st", [P, 2, 1536], F32)
        m_u8 = lb("m_u8", [P, NPAIR, P], U8)
        mm = lb("mm", [P, 2, P], F32)
        neg = lb("neg", [P, 2, P], F32)
        sc = lb("sc", [P, 2, P], F32)
        pc = lb("pc", [P, 2, P], F32)
        pT = lb("pT", [P, 2, P], F32)
        ctx2 = lb("ctx2", [P, 2, 2, D], F32)
        ctxT = lb("ctxT", [P, 2, KT, P], F32)
        x3T = lb("x3T", [P, 2, KT, P], F32)
        xn3 = lb("xn3", [P, 2, D], F32)
        cstat = lb("cstat", [P, 2, 6], F32)
        cmv = lb("cmv", [P, 2, 2], F32)
        cve = lb("cve", [P, 2], F32)
        crs = lb("crs", [P, 2], F32)
        cmax = lb("cmax", [P, 2], F32)
        csum = lb("csum", [P, 2], F32)
        valid = lb("valid", [P, 2], F32)
        cr = lb("cr", [P, 2], F32)
        x4T = lb("x4T", [P, 2, KT, NE1, 64], F16)
        dy_gate = lb("dy_gate", [P, 1], F32)
        xo = lb("xo", [P, 2, D], F32)
        d_th, d_ga, d_h = [d_st[:, 0, i * TILE:i * TILE + TILE] for i in range(3)]
        d_hp = lb("d_hp", [P, 2, TILE], F16)
        d_yT = d_st[:, 1, 0:4 * P].rearrange("p (h t) -> p h t", h=2)
        late.close()

        block = ctx.enter_context(nc.Block())

        w_in = [A["L0_xattn_Wq"], A["L0_xattn_Wk"], A["L0_xattn_Wv"]]
        b_in = [A["L0_xattn_bq"], A["L0_xattn_bk"]]
        N_SMALL = 3 + 2 + 1 + 1 + 2
        STACK_DMAS = 2 * 7

        def weight_part(e, m, k, part):
            if m < 2:
                return w_gu[:, part, e, m, k, :]
            return w_dn[:, part, e, 2 * k:2 * k + 2, :].rearrange("p t h -> p (t h)")

        def expert_step(r, c):
            return (r - 2, c - 1) if c else (r - 3, 3)

        def blocks(r, c, hp, experts):
            if not experts:
                return None, None, None
            gb, kq = expert_step(r, c)
            first = isinstance(r, int) and r == 2 and c == 1
            k = 4 * kq + hp
            block = [(gb, k - lag) if k >= lag else (gb - 1, UNITS + k - lag) for lag in range(3)]
            return [None if first and hp < lag else b for lag, b in enumerate(block)]

        def turns_outputs(r, c):
            return c == 1 and not (isinstance(r, int) and (r < 3 or r >= ROUNDS + 2))

        def schedule(eng, step, late_step):
            for r in range(2):
                for c in range(4):
                    step(r, c, tail=r + c > 0, pair_tail=4 * r + c > 1, experts=False, weights=True)
            for c in range(4):
                step(2, c, tail=True, pair_tail=True, experts=c > 0, weights=False)
            with eng.Fori(3, ROUNDS) as r:
                for c in range(4):
                    step(r, c, tail=True, pair_tail=True, experts=True, weights=False)
            for t in range(4 * ROUNDS, LATE_START + ROUNDS + 1):
                j = t - LATE_START
                late_step(t, experts=t < LAST_OUTPUTS, ja=j if 0 <= j < ROUNDS else None,
                          jb=j - 1 if j > 0 else None)

        @block.sync
        def _(sp):
            sp.sem_inc(s["tokw_stored"], 16)
            sp.sem_inc(s["max_rows_loaded"], 1)
            sp.dma_start(x_res[:, 0:2, :], x_d[:, 0:2, :]).then_inc(s["x01_loaded"], 16)
            for w in range(3):
                sp.dma_start(stage_w[0:S, w, :].rearrange("o (b c) -> o b c", b=2),
                             w_in[w].unsqueeze(1).broadcast_to([S, 2, S])).then_inc(s["small_loaded"], 16)
            for w in range(2):
                sp.dma_start(bias_row[:, w, :], b_in[w].rearrange("(a n) -> a n", a=1)
                             ).then_inc(s["small_loaded"], 16)
            sp.dma_start(bias_v[:, :].rearrange("p (b n) -> p b n", b=2),
                         A["L0_xattn_bv"].rearrange("(a b n) -> a b n", a=1, b=1).broadcast_to([P, 2, S])
                         ).then_inc(s["small_loaded"], 16)
            sp.dma_start(rt_in, A["L0_ffn_router_w"]).then_inc(s["small_loaded"], 16)
            for n, g in ((0, "g_xattn"), (2, "g_ffn")):
                sp.dma_start(gate_in[:, n:n + 2],
                             A[g].rearrange("(a n) -> a n", a=1).broadcast_to([P, 2])
                             ).then_inc(s["small_loaded"], 16)
            sp.dma_start(ctx_in[:, 0, :], ctx_d[0]).then_inc(s["ctx0_loaded"], 16)
            sp.dma_start(ctx_in[:, 1, :], ctx_d[1]).then_inc(s["ctx1_loaded"], 16)

            def load_weight_stage(e, m):
                if e == NE:
                    return
                if e:
                    sp.wait_ge(s["wgrp_T"], 6 * (e - 1) + 2 * (m + 1))
                if m < 2:
                    src = A[("L0_ffn_gate_w", "L0_ffn_up_w")[m]][e].rearrange("(t p) h -> p t h", p=P)
                    dst = stage[m].rearrange("p (t h) -> p t h", t=IB)
                else:
                    src = A["L0_ffn_down_w"][e].rearrange("(t p) i -> p t i", p=P)
                    dst = stage[m].rearrange("p (t i) -> p t i", t=2)
                sp.dma_start(dst, src).then_inc(s[f"stage{m}_loaded"], 16)

            def load_mask(b, slot):
                sp.dma_start(mask_in[:, slot, :, :], mask_d[b]).then_inc(s[f"mask{slot}_loaded"], 16)

            def store_parts(par, q):
                sp.wait_ge(s["qk_split"], q + 1)
                sp.dma_start(part_d[par].rearrange("w c r n -> r w c n"),
                             parts[:, :, :, :]).then_inc(s["parts_stored"], 16)

            def load_stacks(par, q):
                sp.wait_ge(s["parts_stored"], 16 * (q + 1))
                for hh in range(2):
                    lo, hi = 64 * hh, 64 * hh + 64
                    src = [[part_d[par, w, c].rearrange("(g d r) n -> g d (r n)", g=2, d=DH)[hh]
                            for c in range(3)] for w in range(2)]
                    for i in range(2):
                        sp.dma_start(
                            q_stack[lo + 24 * i:lo + 24 * i + 24, par, hh, :, :, :].rearrange("r b h n -> r (b h n)"),
                            src[0][i].unsqueeze(1).broadcast_to([DH, 3, 2048])
                        ).then_inc(s["stack_loaded"], 16)
                        sp.dma_start(
                            k_stack[lo + 24 * i:lo + 24 * i + 24, par, :, :, :].rearrange("r b h n -> r (b h n)"),
                            part_d[par, 1].rearrange("c (g d r) n -> g d c (r n)", g=2, d=DH)[hh]
                        ).then_inc(s["stack_loaded"], 16)
                    sp.dma_start(q_stack[lo + 48:lo + 56, par, hh, :, :, :].rearrange("r b h n -> r (b h n)"),
                                 src[0][2]).then_inc(s["stack_loaded"], 16)
                    sp.dma_start(k_stack[lo + 48:lo + 56, par, :, :, :].rearrange("r b h n -> r (b h n)"),
                                 src[1][0]).then_inc(s["stack_loaded"], 16)
                    sp.dma_start(q_stack[lo + 56:lo + 59, par, hh, :, :, :].rearrange("r b h n -> r (b h) n"),
                                 zero_rows[:, :].unsqueeze(1).broadcast_to([3, 8, D])).then_inc(s["stack_loaded"], 16)

            def load_max_rows(c, m):
                par, b2 = c // 2, c % 2
                sp.wait_ge(s["max_rows_loaded"], 1 + 32 * m)
                sp.sem_inc(s["sp_apart"], 1)
                sp.wait_ge(s["maxT_copied"], m + 1)
                for hh in range(2):
                    sp.dma_start(q_stack[64 * hh + 56:64 * hh + 59, par, hh, b2, :, :].rearrange("r h n -> r (h n)"),
                                 max_rows[24 * hh:24 * hh + 24, :]).then_inc(s["max_rows_loaded"], 16)

            def store_token_weights(a, u):
                sp.wait_ge(s["tokw_stored"], 16 + 16 * (2 * a + u))
                sp.sem_inc(s["sp_apart"], 1)
                sp.wait_ge(s["wrow_ready"], 2 * a + u + 1)
                sp.dma_start(tokw_d[(a // 2) % 2, :, bass.ds((a % 2) * 256 + u * P, P)],
                             wrow[:, :]).then_inc(s["tokw_stored"], 16)

            def load_expert_weights(gb, kq):
                sp.wait_ge(s["h_mul"], 1 + 16 * gb + 4 * kq)
                if isinstance(gb, int) and gb == 0:
                    sp.wait_ge(s["w_split"], 2 + 6 * NE)
                if kq == 0:
                    sp.wait_ge(s["tokw_stored"], 16 + 64 * (gb // 2) + 64)
                    sp.sem_inc(s["sp_apart"], 1)
                sp.dma_start(wb[:, kq % 2, :],
                             tokw_d[(gb // 2) % 2, (gb % 2) * 4 + kq].rearrange("(q t) -> q t", q=1).broadcast_to([P, TILE])
                             ).then_inc(s[f"wb{kq % 2}_loaded"], 16)

            def load_late_weights(e):
                if e >= 2:
                    sp.wait_ge(s["dw_split"], 4 * (e - 1))
                sp.dma_start(d_st[:, e % 2, 0:1024].rearrange("p (t i) -> p t i", t=KT),
                             A["L1_ffn_gate_up_proj"][e].rearrange("(t p) i -> p t i", p=P)
                             ).then_inc(s[f"d{e % 2}_loaded"], 16)
                sp.dma_start(d_st[:, e % 2, 1024:1536].rearrange("p (t h) -> p t h", t=IB1),
                             A["L1_ffn_down_proj"][e].rearrange("(t p) h -> p t h", p=P)
                             ).then_inc(s[f"d{e % 2}_loaded"], 16)

            def load_late_ctx(j):
                if j >= 2:
                    sp.wait_ge(s["read_done"], j - 1)
                sp.dma_start(ctx2[:, j % 2, :, :], A["ctx_2048"].rearrange("(j u b) s d -> j (b s) u d", u=2, b=2)[j]
                             ).then_inc(s[f"cx{j % 2}_loaded"], 16)

            def open_late():
                sp.wait_ge(s["wrow_ready"], NPAIR)
                sp.wait_ge(s["tokw_stored"], 16 + 16 * NPAIR)
                sp.wait_ge(s["max_rows_loaded"], 1 + 32 * (B + 1))
                sp.wait_ge(s["stack_loaded"], STACK_DMAS * 16 * (NPAIR + 1))
                sp.wait_ge(s["parts_stored"], 16 * (NPAIR + 2))
                for slot in range(2):
                    sp.wait_ge(s[f"ctx{slot}_loaded"], 16 * (NPAIR // 2 + 1))
                sp.wait_ge(s["mask0_loaded"], 16 * (B // 2 + 2))
                sp.wait_ge(s["mask1_loaded"], 16 * (B // 2 + 1))
                sp.dma_start(m_u8[:, :, :],
                             A["mask_BxS2_bk0"].rearrange("(q p b) s -> q p (b s)", q=1, b=2).broadcast_to([P, NPAIR, P])
                             ).then_inc(s["mask_m_loaded"], 16)

            def step(r, c, tail, pair_tail, experts, weights):
                n, par = 4 * r + c, c // 2
                pair = 2 * r + par
                if c % 2 == 1 and pair_tail:
                    store_token_weights(r - 1 if c == 1 else r, 1 - par)
                if experts:
                    load_expert_weights(*expert_step(r, c))
                if c % 2 == 0:
                    sp.wait_ge(s["scores2_done"], 1 + 8 * n)
                    sp.sem_inc(s["sp_apart"], 1)
                    load_stacks(1 - par, pair + 1)
                    sp.wait_ge(s["v_projected"], pair + 2)
                    sp.dma_start(ctx_in[:, 1 - par, :], ctx_d[(pair + 3) % NPAIR]
                                 ).then_inc(s[f"ctx{1 - par}_loaded"], 16)
                if weights:
                    load_weight_stage(n + 1, 0)
                    load_weight_stage(n + 1, 1)
                if c % 2 == 1:
                    sp.wait_ge(s["stack_loaded"], STACK_DMAS * 16 * (pair + 2))
                    store_parts(par, pair + 2)
                sp.wait_ge(s["max_done"], 16 * n + 32)
                sp.sem_inc(s["sp_apart"], 1)
                sp.wait_ge(s["maskT_ready"], n + 2)
                load_mask((n + 3) % B, (c + 1) % 2)
                load_max_rows((c + 1) % 4, n + 1)
                if weights:
                    load_weight_stage(n + 1, 2)

            def late_step(t, experts, ja, jb):
                if t == 4 * ROUNDS + 1:
                    store_token_weights(ROUNDS - 1, 1)
                if experts:
                    load_expert_weights(*expert_step(t // 4, t % 4))
                if t == 4 * ROUNDS + 1:
                    open_late()
                    load_late_ctx(0)
                    for e in range(3):
                        load_late_weights(e)
                if t == 4 * ROUNDS + 2:
                    load_late_weights(3)
                if ja is not None and ja + 1 < ROUNDS:
                    load_late_ctx(ja + 1)
                if jb is not None:
                    sp.wait_ge(s["d_out"], jb + 1)
                    sp.dma_start(out.rearrange("(j u b) s d -> j (b s) u d", u=2, b=2)[jb], xo[:, :, :]
                                 ).then_inc(s["out_stored"], 16)

            load_mask(0, 0)
            load_mask(1, 1)
            sp.dma_start(x_res[:, 2:16, :], x_d[:, 2:16, :]).then_inc(s["x_loaded"], 16)
            store_parts(0, 0)
            sp.wait_ge(s["stacks_set"], 2)
            sp.wait_ge(s["dve_step"], 2)
            load_stacks(0, 0)
            store_parts(1, 1)
            sp.wait_ge(s["v_projected"], 1)
            sp.dma_start(ctx_in[:, 0, :], ctx_d[2]).then_inc(s["ctx0_loaded"], 16)
            for m in range(3):
                load_weight_stage(0, m)
            sp.wait_ge(s["max_done"], 16)
            sp.wait_ge(s["maskT_ready"], 1)
            load_mask(2, 0)
            load_max_rows(0, 0)

            schedule(sp, step, late_step)

            sp.wait_ge(s["out_stored"], 16 * ROUNDS)

        @block.gpsimd
        def _(pool):
            pool.sem_inc(s["plo_done"], 2)
            pool.sem_inc(s["w_split"], 2)
            pool.sem_inc(s["h_mul"], 5)
            pool.sem_inc(s["h_split"], 2)
            pool.memset(ident[:, :], 0.0).then_inc(s["zeroed"], 1)
            pool.memset(minus_half[:, :], -0.5).then_inc(s["consts_ready"], 1)
            pool.memset(w_bd[:, :, :], 0.0).then_inc(s["consts_ready"], 1)
            pool.wait_ge(s["zeroed"], 1)
            pool.affine_select(out=ident[:, :], in_=ident[:, :], compare_op=ALU.not_equal, fill=1.0,
                               base=0, pattern=[[-1, P]], channel_multiplier=1).then_inc(s["consts_ready"], 1)
            pool.wait_ge(s["consts_ready"], 3)
            pool.tensor_copy(ident_b[:, :], ident[:, :]).then_inc(s["consts_ready"], 1)
            pool.wait_ge(s["ln01_in"], 1)
            pool.tensor_tensor(rstd[:, 0:2], rstd[:, 0:2], minus_half[:, 0:2], ALU.pow).then_inc(s["pow01_done"], 1)
            pool.memset(k_stack[:, :, :, :, :], 1.0).then_inc(s["stacks_set"], 1)
            pool.memset(v_parts[:, :, :, :, :], 1.0).then_inc(s["stacks_set"], 1)
            pool.memset(tri[:, :, :], 1.0).then_inc(s["consts_ready"], 1)
            pool.memset(bd[:, :], 0.0).then_inc(s["bd_ready"], 1)
            pool.wait_ge(s["consts_ready"], 5)
            pool.affine_select(out=tri[:, :, :], in_=tri[:, :, :], compare_op=ALU.is_gt, fill=0.0,
                               base=0, pattern=[[1, NE], [-1, NE]], channel_multiplier=0).then_inc(s["consts_ready"], 1)
            pool.wait_ge(s["bd_ready"], 1)
            pool.wait_ge(s["consts_ready"], 6)
            for q in range(2):
                pool.memset(bd[64 * q:64 * q + 64, 64 * q:64 * q + 64], 1.0).then_inc(s["bd_ready"], 1)
            pool.wait_ge(s["bd_ready"], 3)
            pool.wait_ge(s["ln_in"], 1)
            pool.tensor_tensor(rstd[:, 2:16], rstd[:, 2:16], minus_half[:, 2:16], ALU.pow).then_inc(s["pow_done"], 1)

            def p_low(n, hp, mt):
                k = 8 * n + 2 * hp + mt
                pool.wait_ge(s["phi_done"], k + 1)
                pool.tensor_tensor(p_lo[:, hp % 2, mt, :], p32[:, mt, :], p_hi[:, hp % 2, mt, :],
                                   ALU.subtract).then_inc(s["plo_done"], 1)

            def pow2(pair):
                pool.wait_ge(s["ln_in"], 2 + pair)
                pool.tensor_tensor(rstd2[:, :], ve2[:, :], minus_half[:, 0:1], ALU.pow).then_inc(s["pow_done"], 1)

            def w_low(e, m, k):
                pool.wait_ge(s["w_hi"], 6 * e + 2 * m + k + 1)
                pool.tensor_tensor(weight_part(e, m, k, 1), wb[:, k, :], weight_part(e, m, k, 0), ALU.subtract
                                   ).then_inc(s["w_split"], 1)

            def h_mul(gb, k):
                if k % IB == 0:
                    pool.wait_ge(s[f"wb{k // IB % 2}_loaded"], 16 * (2 * gb + k // IB // 2 + 1))
                pool.wait_ge(s["up_used"], 1 + UNITS * gb + k + 1)
                pool.tensor_tensor(hb32[:, k % 2, :], hb32[:, k % 2, :], wb[:, (k // IB) % 2, :],
                                   ALU.mult).then_inc(s["h_mul"], 1)

            def h_low(gb, k):
                pool.wait_ge(s["h_hi"], UNITS * gb + k + 1)
                pool.tensor_tensor(hp_lo[:, k % 2, :], hb32[:, k % 2, :], hp_hi[:, k % 2, :], ALU.subtract
                                   ).then_inc(s["h_split"], 1)

            def late_pow(j, i):
                pool.wait_ge(s["ln_in"], 1 + NPAIR + 2 * j + i + 1)
                pool.tensor_tensor(crs[:, :], cve[:, :], minus_half[:, 0:2], ALU.pow).then_inc(s["pow_done"], 1)

            def late_low(j):
                pool.wait_ge(s["d_hi"], j + 1)
                pool.tensor_tensor(d_hp[:, 1, :], d_h, d_hp[:, 0, :], ALU.subtract).then_inc(s["d_split"], 1)

            def step(r, c, tail, pair_tail, experts, weights):
                n = 4 * r + c
                for hp in range(4):
                    block, last, _ = blocks(r, c, hp, experts)
                    p_low(n, hp, 0)
                    if pair_tail and c % 2 == 0 and hp == 1:
                        pow2(2 * r + c // 2 - 1)
                    if last:
                        h_low(*last)
                    if weights and hp < 3:
                        w_low(n, hp, 0)
                    if block:
                        h_mul(*block)
                    p_low(n, hp, 1)
                    if weights and hp < 3:
                        w_low(n, hp, 1)

            def late_step(t, experts, ja, jb):
                if t == LAST_OUTPUTS:
                    h_low(ROUNDS - 1, UNITS - 1)
                for hp in range(4):
                    block, last, _ = blocks(t // 4, t % 4, hp, experts)
                    if ja is not None and hp == 0:
                        late_pow(ja, 0)
                    if jb is not None and hp == 2:
                        late_low(jb)
                    if ja is not None and hp == 3:
                        late_pow(ja, 1)
                    if last:
                        h_low(*last)
                    if t == 4 * ROUNDS and hp == 1:
                        pow2(NPAIR - 1)
                    if block:
                        h_mul(*block)

            schedule(pool, step, late_step)


        @block.scalar
        def _(act):
            act.sem_inc(s["y_evac"], 1)
            act.sem_inc(s["w_copied"], 2)
            act.wait_ge(s["small_loaded"], 16 * N_SMALL)
            act.activation(gates[:, :], gate_in[:, :], ACT.Tanh).then_inc(s["gates_ready"], 1)

            for w in range(2):
                act.activation(bias_turn[:, w, :].rearrange("p (i b h) -> p b h i", b=2, h=4),
                               bias_row[:, w, :].rearrange("p (b h i) -> p b h i", b=1, h=4).broadcast_to([1, 2, 4, 16]),
                               ACT.Copy).then_inc(s["bias_turned"], 1)
            act.wait_ge(s["wst_T"], 3)
            act.wait_ge(s["consts_ready"], 4)
            for w in range(3):
                for b2 in range(2):
                    rows = slice(S * b2, S * b2 + S)
                    src = psM[rows, w * S:w * S + S]
                    if w < 2:
                        src = src.rearrange("p (h i) -> p h i", h=4)
                        dst = w_bd[rows, w, :].rearrange("p (i b h) -> p b h i", b=2, h=4)[:, b2]
                    else:
                        dst = w_bd[rows, w, S * b2:S * b2 + S]
                    act.activation(dst, src, ACT.Copy).then_inc(s["bias_ready"], 1)

            def w_high(e, m, k):
                g = 6 * e + 2 * m + k
                act.wait_ge(s["wgrp_T"], g + 1)
                act.wait_ge(s["w_split"], g + 1)
                act.activation(wb[:, k, :], (psG, psU)[k][:, :], ACT.Copy, scale=W_SCALE).then_inc(s["w_copied"], 1)
                act.wait_ge(s["w_copied"], 2 + g + 1)
                act.activation(weight_part(e, m, k, 0), wb[:, k, :], ACT.Copy).then_inc(s["w_hi"], 1)

            def copy_qk(n):
                act.wait_ge(s["qk_projected"], n + 1)
                act.wait_ge(s["qk_split"], n)
                act.activation(qk32[:, 0, :], psM[:, 0:D], ACT.Identity, scale=DH ** -0.5,
                               bias=bias_qs[:, 0:1]).then_inc(s["qk_copied"], 1)
                act.activation(qk32[:, 1, :], psM[:, D:2 * D], ACT.Identity,
                               bias=bias_qk[:, 1:2]).then_inc(s["qk_copied"], 1)

            def copy_maskT(n, slot):
                act.wait_ge(s["maskT_ready"], n + 1)
                act.activation(maskT[:, slot, :, :], psM[:, :].rearrange("p (t n) -> p t n", t=2),
                               ACT.Copy).then_inc(s["maskT_copied"], 1)

            def copy_maxT(n):
                act.wait_ge(s["maxT_ready"], n + 1)
                act.wait_ge(s["max_rows_loaded"], 1 + 32 * n)
                act.activation(max_rows[:, :], psM[:, 0:64].bitcast(BF16)[0:48, :], ACT.Copy
                               ).then_inc(s["maxT_copied"], 1)

            def exps(n, hp, mt):
                k = 8 * n + 2 * hp + mt
                act.wait_ge(s["masked_done"], 1 + k + 1)
                act.activation(p32[:, mt, :], p32[:, mt, :], ACT.Exp, bias=lnscale[:, 0:1]).then_inc(s["exp_done"], 1)

            def exp_high(n, hp, mt):
                k = 8 * n + 2 * hp + mt
                act.wait_ge(s["pv_done"], 4 * n + hp + 1)
                act.wait_ge(s["exp_done"], k + 1)
                act.activation(p_hi[:, hp % 2, mt, :], p32[:, mt, :], ACT.Copy).then_inc(s["phi_done"], 1)

            def x_high(a, u):
                act.wait_ge(s["xn2T_ready"], 2 * a + u + 1)
                act.activation(xT[:, (a // 2) % 2, 0, :, bass.ds((a % 2) * 256 + u * P, P)],
                               psM[:, 0:2 * P].rearrange("p (k t) -> p k t", k=KT), ACT.Copy,
                               scale=X_SCALE).then_inc(s["xt_hi"], 1)

            def route_exp(n):
                act.wait_ge(s["logits_done"], n + 1)
                act.activation(pe_[:, :], lg[:, :], ACT.Exp, scale=G_UNSCALE, bias=lmax[:, 0:1],
                               accum_out=lsum[:, 0:1]).then_inc(s["route_exp"], 1)

            def block_tanh(gb, k):
                act.wait_ge(s["gate_ready"], UNITS * gb + k + 1)
                act.activation(th, psG[:, :], ACT.Tanh, scale=0.5 * G_UNSCALE).then_inc(s["tanh_done"], 1)

            def block_high(gb, k):
                u = UNITS * gb + k
                act.wait_ge(s["h_mul"], 5 + u + 1)
                act.wait_ge(s["down_done"], u + 1)
                act.activation(hp_hi[:, k % 2, :], hb32[:, k % 2, :], ACT.Copy).then_inc(s["h_hi"], 1)

            def y_out(gb):
                act.wait_ge(s["down_done"], 2 + UNITS * (gb + 1))
                for hb in range(2):
                    act.activation(yT[:, hb, :], psY[:, hb, :], ACT.Copy, scale=1.0 / W_SCALE
                                   ).then_inc(s["y_evac"], 1)

            act.wait_ge(s["exp_bias_set"], 1)
            act.wait_ge(s["bias_set"], 2)

            copy_qk(0)
            copy_maskT(0, 0)
            copy_qk(1)
            copy_maxT(0)

            def late_copy(sem_in, j, dst, ps, sem_out):
                act.wait_ge(s[sem_in], j + 1)
                act.activation(dst, ps, ACT.Copy).then_inc(s[sem_out], 1)

            def late_exps(j):
                act.wait_ge(s["sc_masked"], j + 1)
                for u in range(2):
                    act.activation(pc[:, u, :], sc[:, u, :], ACT.Exp, bias=cmax[:, u:u + 1],
                                   accum_out=csum[:, u:u + 1]).then_inc(s["c_exp"], 1)

            def late_tanh(j):
                act.wait_ge(s["d_gate"], j + 1)
                act.activation(d_th, ps1[:, :, :].rearrange("p a b -> p (a b)"), ACT.Tanh,
                               scale=0.5 * G_UNSCALE).then_inc(s["d_tanh"], 1)

            def late_x_high(j):
                act.wait_ge(s["xn4T"], j + 1)
                for u in range(2):
                    act.activation(x4T[:, 0, :, :, 32 * u:32 * u + 32],
                                   psV[:, u * D:u * D + D].rearrange("p (k q e) -> p k e q", k=KT, e=NE1),
                                   ACT.Copy, scale=X_SCALE).then_inc(s["xn4_hi"], 1)

            def late_y_out(j):
                act.wait_ge(s["d_down"], j + 1)
                act.activation(d_yT[:, :, :].rearrange("p h (q e) -> p h e q", e=NE1),
                               ps1[:, :, :].rearrange("p h (e q) -> p h e q", e=NE1),
                               ACT.Copy, scale=dy_gate[:, 0:1]).then_inc(s["d_yevac"], 1)

            def step(r, c, tail, pair_tail, experts, weights):
                n, pair = 4 * r + c, 2 * r + c // 2
                for hp in range(4):
                    block, last, _ = blocks(r, c, hp, experts)
                    if pair_tail and (c % 2, hp) == (0, 2):
                        x_high(r - 1 if c == 0 else r, 1 - c // 2)
                    if hp == 3:
                        copy_maxT(n + 1)
                    if block:
                        block_tanh(*block)
                    if last:
                        block_high(*last)
                    if weights and hp < 3:
                        w_high(n, hp, 0)
                    if pair_tail and (c % 2, hp) == (0, 3):
                        route_exp(pair - 1)
                    exps(n, hp, 0)
                    exp_high(n, hp, 0)
                    if weights and hp < 3:
                        w_high(n, hp, 1)
                    exps(n, hp, 1)
                    exp_high(n, hp, 1)
                    if hp == 1 and turns_outputs(r, c):
                        y_out(r - 3)
                    if hp == 0:
                        act.wait_ge(s["masked_done"], 1 + 8 * n)
                        copy_maskT(n + 1, (c + 1) % 2)
                    if (c % 2, hp) == (1, 1):
                        copy_qk(pair + 2)

            def late_step(t, experts, ja, jb):
                if t == LAST_OUTPUTS:
                    block_high(ROUNDS - 1, UNITS - 1)
                    y_out(ROUNDS - 1)
                for hp in range(4):
                    block, last, _ = blocks(t // 4, t % 4, hp, experts)
                    if block:
                        block_tanh(*block)
                    if ja is not None and hp == 0:
                        late_copy("cxT", ja, ctxT[:, :, :, :].rearrange("p u k t -> p (u k t)"), psV[:, :], "ctxT_done")
                    if ja is not None and hp == 1:
                        late_copy("xn3T", ja, x3T[:, :, :, :].rearrange("p u k t -> p (u k t)"), psV[:, :], "xt3_done")
                    if ja is not None and hp == 2:
                        late_exps(ja)
                    if jb is not None and hp == 3:
                        late_y_out(jb)
                    if (t, hp) == (4 * ROUNDS, 2):
                        x_high(ROUNDS - 1, 1)
                    if (t, hp) == (4 * ROUNDS, 3):
                        route_exp(NPAIR - 1)
                    if last:
                        block_high(*last)
                    if hp == 1 and turns_outputs(t // 4, t % 4):
                        y_out(t // 4 - 3)
                    if jb is not None and hp == 0:
                        late_tanh(jb)
                    if ja is not None and hp == 3:
                        late_x_high(ja)
                    if jb is not None and hp == 1:
                        late_copy("d_mul", jb, d_hp[:, 0, :], d_h, "d_hi")
                    if ja is not None and hp == 2:
                        late_copy("pT_ready", ja, pT[:, :, :].rearrange("p u t -> p (u t)"), psV[:, 0:2 * P], "pT_done")

            schedule(act, step, late_step)

        @block.tensor
        def _(pe):
            def mm(out_, lhsT, rhs, start=True, stop=True):
                return pe.matmul(out_, lhsT, rhs, start=start, stop=stop)

            def square(sl):
                return psM[:, sl * P:sl * P + P]

            pe.sem_inc(s["pv_done"], 2)
            pe.sem_inc(s["down_done"], 2)
            pe.sem_inc(s["scores2_done"], 1)
            pe.wait_ge(s["small_loaded"], 16 * N_SMALL)
            pe.wait_ge(s["consts_ready"], 4)
            for w in range(3):
                pe.transpose(psM[:, w * S:w * S + S], stage_w[0:S, w, :], ident[0:S, 0:S]).then_inc(s["wst_T"], 1)
            pe.wait_ge(s["bias_turned"], 2)
            for w in range(2):
                pe.transpose(psV[:, w:w + 1], bias_turn[:, w, :], ident[0:1, 0:1]).then_inc(s["biasT_ready"], 1)
            for k in range(KT):
                last = pe.transpose(psY[:, 0, k * NE:k * NE + NE], rt_in[:, k * P:k * P + P], ident[0:NE, 0:NE])
            last.then_inc(s["router_T"], 1)

            def weight_transposes(e, m, k):
                pe.wait_ge(s[f"stage{m}_loaded"], 16 * e + 16)
                pe.wait_ge(s["w_copied"], 6 * e + 2 * m + k + 1)
                bank = (psG, psU)[k]
                for i in range(4):
                    if m < 2:
                        src = stage[m].rearrange("p (t h) -> p t h", t=IB)[:, i, k * P:k * P + P]
                    else:
                        src = stage[2].rearrange("p (t i) -> p t i", t=2)[
                            :, i % 2, (2 * k + i // 2) * P:(2 * k + i // 2) * P + P]
                    last = pe.transpose(bank[:, i * P:i * P + P], src, ident[:, :])
                last.then_inc(s["wgrp_T"], 1)

            def project_qk(par, q):
                pe.wait_ge(s["xn_ready"], q + 1)
                pe.wait_ge(s[f"ctx{par}_loaded"], 16 * (q // 2 + 1))
                mm(psM[:, 0:D], w_bd[:, 0, :], xn[:, :])
                mm(psM[:, D:2 * D], w_bd[:, 1, :], ctx_in[:, par, :]).then_inc(s["qk_projected"], 1)

            def project_v(par, q):
                for t in range(2):
                    last = mm(psM[:, t * P:t * P + P], ctx_in[:, par, t * P:t * P + P], w_bd[:, 2, :])
                last.then_inc(s["v_projected"], 1)

            def mask_transposes(n, slot):
                pe.wait_ge(s[f"mask{slot}_loaded"], 16 * (n // 2 + 1))
                for mt in range(2):
                    for nt in range(2):
                        last = pe.transpose(psM[:, mt * 256 + nt * P:mt * 256 + nt * P + P],
                                            mask_in[:, slot, nt, mt * P:mt * P + P], ident[:, :])
                last.then_inc(s["maskT_ready"], 1)

            def first_pass(c, n, i):
                par, b2, hp, hh = c // 2, c % 2, i // 2, i % 2
                pe.wait_ge(s["max_done"], 16 * n + 2 * i)
                for nt in range(2):
                    last = mm(ps1[:, nt, :], q_stack[:, par, hh, b2, hp, nt * P:nt * P + P],
                              k_stack[:, par, b2, hp, :])
                last.then_inc(s["scores1_done"], 1)

            def second_pass(c, n, hp, mt):
                par, b2 = c // 2, c % 2
                pe.wait_ge(s["masked_done"], 1 + 8 * n + 2 * hp + mt)
                mm(ps2[:, :], k_stack[:, par, b2, hp, mt * P:mt * P + P],
                   q_stack[:, par, :, b2, hp, :]).then_inc(s["scores2_done"], 1)

            def times_v(c, n, hp):
                par, b2 = c // 2, c % 2
                pe.wait_ge(s["plo_done"], 2 + 8 * n + 2 * hp + 2)
                for hh in range(2):
                    for nt in range(2):
                        h = 2 * hp + hh
                        dst = psV[:, (nt * H + h) * VC:(nt * H + h + 1) * VC]
                        for i, (part, mt) in enumerate(((p_hi, 0), (p_hi, 1), (p_lo, 0), (p_lo, 1))):
                            at = hh * 256 + nt * P
                            last = mm(dst, part[:, hp % 2, mt, at:at + P], v_parts[:, par, mt, b2 * H + h, :],
                                      start=(i == 0), stop=(i == 3))
                last.then_inc(s["pv_done"], 1)

            def turn_maxima(n):
                pe.wait_ge(s["max_split"], n + 1)
                pe.sem_inc(s["pe_apart"], 1)
                pe.transpose(psM[:, 0:64].bitcast(BF16)[0:48, :],
                             max_parts[:, :, :, :].rearrange("p g c x -> p (g c x)"), ident_b[:, :]
                             ).then_inc(s["maxT_ready"], 1)

            def turn_attention(pair):
                pe.wait_ge(s["on_ready"], 2 * pair + 2)
                for nt in range(2):
                    last = pe.transpose(square(nt), on[:, nt, :], ident[:, :])
                last.then_inc(s["onT_ready"], 1)

            def turn_xn2(pair):
                pe.wait_ge(s["xn2_ready"], pair + 1)
                for k in range(KT):
                    last = pe.transpose(square(k), xn[:, k * P:k * P + P], ident[:, :])
                last.then_inc(s["xn2T_ready"], 1)

            def router(a, u):
                at = bass.ds((a % 2) * 256 + u * P, P)
                tp = (a // 2) % 2
                for k in range(KT):
                    mm(psM[:, 0:2 * NE], xT[:, tp, 0, k, at], w_rt[:, k, :], start=(k == 0), stop=False)
                for k in range(KT):
                    last = mm(psM[:, 0:NE], xT[:, tp, 1, k, at], w_rt[:, k, 0:NE], start=False, stop=(k == KT - 1))
                last.then_inc(s["router_done"], 1)

            def turn_token_weights(pair):
                pe.wait_ge(s["w_ready"], pair + 1)
                pe.transpose(psM[0:NE, 0:P], tokw[:, :], ident[:, :]).then_inc(s["wT_ready"], 1)

            def block_in(gb, k, bank, which, done):
                e = (gb % 2) * 4 + k // IB
                i0 = (k % IB) * P
                tp = (gb // 2) % 2
                n = 0
                for kt in range(KT):
                    for wp, xp in ((0, 0), (1, 0), (0, 1)):
                        last = mm(bank[:, :], w_gu[:, wp, e, which, kt, i0:i0 + P], xT[:, tp, xp, kt, :],
                                  start=(n == 0), stop=(n == 5))
                        n += 1
                last.then_inc(done, 1)

            def block_gate(gb, k):
                u = UNITS * gb + k
                pe.wait_ge(s["gate_used"], 1 + u)
                if k == 0:
                    pe.wait_ge(s["xt_split"], 4 * (gb // 2) + 4)
                block_in(gb, k, psG, 0, s["gate_ready"])

            def block_up(gb, k):
                pe.wait_ge(s["up_used"], 1 + UNITS * gb + k)
                block_in(gb, k, psU, 1, s["up_ready"])

            def block_down(gb, k):
                u = UNITS * gb + k
                e = (gb % 2) * 4 + k // IB
                pe.wait_ge(s["h_split"], 2 + u + 1)
                if k == 0:
                    pe.wait_ge(s["y_evac"], 1 + 2 * gb)
                for hb in range(2):
                    for i, (wp, hpart) in enumerate(((0, hp_hi), (1, hp_hi), (0, hp_lo))):
                        last = mm(psY[:, hb, :], w_dn[:, wp, e, k % IB, hb * P:hb * P + P], hpart[:, k % 2, :],
                                  start=(k == 0 and i == 0), stop=(k == UNITS - 1 and i == 2))
                last.then_inc(s["down_done"], 1)

            def turn_outputs(gb, q):
                if q == 0:
                    pe.wait_ge(s["y_evac"], 1 + 2 * gb + 2)
                for hb in range(2):
                    last = pe.transpose(square(hb), yT[:, hb, q * P:q * P + P], ident[:, :])
                last.then_inc(s["yT_T"], 1)

            pe.wait_ge(s["bias_ready"], 6)
            project_qk(0, 0)
            pe.wait_ge(s["qk_copied"], 2)
            project_v(0, 0)
            pe.wait_ge(s["v_copied"], 1)
            mask_transposes(0, 0)
            pe.wait_ge(s["maskT_copied"], 1)
            project_qk(1, 1)
            pe.wait_ge(s["stack_loaded"], STACK_DMAS * 16)
            for i in range(H):
                first_pass(0, 0, i)
            for i in range(2):
                first_pass(1, 1, i)
            pe.wait_ge(s["qk_copied"], 4)
            turn_maxima(0)

            def late_turn(src, done):
                for u in range(2):
                    for k in range(KT):
                        at = (u * KT + k) * P
                        last = pe.transpose(psV[:, at:at + P], src[:, u, k * P:k * P + P], ident[:, :])
                last.then_inc(s[done], 1)

            def late_block_in(j, bank, which, done):
                for ib in range(IB1):
                    for e in range(NE1):
                        n = 0
                        dst = bank[:, (ib * NE1 + e) * 64:(ib * NE1 + e) * 64 + 64]
                        i0 = which * NI1 + ib * P
                        for kt in range(KT):
                            for wp, xp in ((0, 0), (1, 0), (0, 1)):
                                last = mm(dst, d_gu[:, wp, e, kt, i0:i0 + P], x4T[:, xp, kt, e, :],
                                          start=(n == 0), stop=(n == 5))
                                n += 1
                last.then_inc(s[done], 1)

            def late_down(j):
                pe.wait_ge(s["d_split"], j + 1)
                pe.wait_ge(s["d_mul"], j + 1)
                for hb in range(2):
                    for e in range(NE1):
                        n = 0
                        for ib in range(IB1):
                            at = (ib * NE1 + e) * 64
                            for wp, hpart in ((0, 0), (1, 0), (0, 1)):
                                last = mm(ps1[:, hb, e * 64:e * 64 + 64], d_dn[:, wp, e, ib, hb * P:hb * P + P],
                                          d_hp[:, hpart, at:at + 64], start=(n == 0), stop=(n == 5))
                                n += 1
                last.then_inc(s["d_down"], 1)

            def late_scores(j):
                pe.wait_ge(s["xt3_done"], j + 1)
                for u in range(2):
                    for k in range(KT):
                        last = mm(psV[:, u * P:u * P + P], x3T[:, u, k, :], ctxT[:, u, k, :], start=(k == 0), stop=(k == 1))
                last.then_inc(s["sc_done"], 1)

            def late_place(ja, jb, hp, place):
                at = (hp, place)
                if ja is not None:
                    if at == (0, 0):
                        if ja:
                            pe.wait_ge(s["xn4_split"], 4 * ja)
                        pe.wait_ge(s[f"cx{ja % 2}_loaded"], 16 * (ja // 2 + 1))
                        late_turn(ctx2[:, ja % 2, :, :], "cxT")
                    elif at == (1, 0):
                        pe.wait_ge(s["ctxT_done"], ja + 1)
                        pe.wait_ge(s["xn3_ready"], 4 * ja + 2)
                        late_turn(xn3, "xn3T")
                    elif at == (1, 2):
                        late_scores(ja)
                    elif at == (2, 1):
                        pe.wait_ge(s["c_exp"], 2 * ja + 2)
                        for u in range(2):
                            last = pe.transpose(psV[:, u * P:u * P + P], pc[:, u, :], ident[:, :])
                        last.then_inc(s["pT_ready"], 1)
                    elif at == (3, 0):
                        pe.wait_ge(s["pT_done"], ja + 1)
                        for u in range(2):
                            last = mm(psV[:, u * D:u * D + D], pT[:, u, :], ctx2[:, ja % 2, u, :])
                        last.then_inc(s["read_done"], 1)
                    elif at == (3, 2):
                        pe.wait_ge(s["x3_done"], 2 * ja + 2)
                        pe.wait_ge(s["xn3_ready"], 4 * ja + 4)
                        late_turn(xn3, "xn4T")
                if jb is not None:
                    if at == (0, 1):
                        pe.wait_ge(s["xn4_split"], 4 * jb + 4)
                        if jb == 0:
                            pe.wait_ge(s["dw_split"], 4 * NE1)
                        else:
                            pe.wait_ge(s["d_yevac"], jb)
                        late_block_in(jb, ps1[:, :, :].rearrange("p a b -> p (a b)"), 0, "d_gate")
                    elif at == (0, 2):
                        if jb:
                            pe.wait_ge(s["d_out"], jb)
                        late_block_in(jb, ps2, 1, "d_upT")
                    elif at == (2, 0):
                        late_down(jb)
                    elif at == (3, 1):
                        pe.wait_ge(s["d_yevac"], jb + 1)
                        for u in range(2):
                            for hb in range(2):
                                at2 = (u * 2 + hb) * P
                                last = pe.transpose(ps2[:, at2:at2 + P], d_yT[:, hb, u * P:u * P + P], ident[:, :])
                        last.then_inc(s["d_yT"], 1)

            def step(r, c, tail, pair_tail, experts, weights):
                n, par = 4 * r + c, c // 2
                pair = 2 * r + par
                outputs = turns_outputs(r, c)
                for hp in range(4):
                    block, _, before = blocks(r, c, hp, experts)
                    if block:
                        block_gate(*block)
                    if weights and hp < 3:
                        weight_transposes(n, hp, 0)
                    i = (2 * hp + 2) % H
                    cm, m = ((c + 1) % 4, n + 1) if hp < 3 else ((c + 2) % 4, n + 2)
                    if hp == 3 and c % 2 == 0:
                        pe.wait_ge(s["stack_loaded"], STACK_DMAS * 16 * (pair + 2))
                    first_pass(cm, m, i)
                    if hp == 0:
                        pe.wait_ge(s["max_rows_loaded"], 1 + 32 * (n + 1))
                    second_pass(c, n, hp, 0)
                    if hp == 0 and c % 2 == 0:
                        pe.wait_ge(s["maxT_copied"], n + 1)
                        if turns_outputs(r, 1) and c == 2:
                            pe.wait_ge(s["y_added"], 4 * (r - 3) + 4)
                        project_v(1 - par, pair + 1)
                    if hp == 0 and pair_tail and c % 2 == 1:
                        pe.wait_ge(s["maxT_copied"], n + 1)
                        turn_token_weights(pair - 1)
                    if hp == 1 and pair_tail and c % 2 == 0:
                        pe.wait_ge(s["maskT_copied"], n + 2)
                        turn_attention(pair - 1)
                    if hp == 2 and pair_tail and c % 2 == 0:
                        pe.wait_ge(s["x1_done"], pair)
                        turn_xn2(pair - 1)
                    if hp == 2 and outputs:
                        pe.wait_ge(s["qk_copied"], 2 * (pair + 2) + 2)
                        turn_outputs(r - 3, 0)
                    if hp == 3:
                        if outputs:
                            pe.wait_ge(s["y_added"], 4 * (r - 3) + 2)
                        elif c % 2 == 1:
                            pe.wait_ge(s["qk_copied"], 2 * (pair + 2) + 2)
                        elif pair_tail:
                            pe.wait_ge(s["lg_done"], pair)
                        else:
                            pe.wait_ge(s["maskT_copied"], n + 2)
                        turn_maxima(n + 1)
                    if block:
                        block_up(*block)
                    if weights and hp < 3:
                        weight_transposes(n, hp, 1)
                    first_pass(cm, m, i + 1)
                    second_pass(c, n, hp, 1)
                    if before:
                        block_down(*before)
                    if hp > 0:
                        if hp == 1:
                            pe.wait_ge(s["pv_evac"], 1 + n)
                            pe.wait_ge(s["v_split"], pair + 1)
                        times_v(c, n, hp - 1)
                    elif tail:
                        times_v((c + 3) % 4, n - 1, 3)
                    if hp == 0:
                        if c % 2 == 0:
                            pe.wait_ge(s["v_copied"], pair + 2)
                        elif pair_tail:
                            pe.wait_ge(s["wrow_ready"], pair)
                        else:
                            pe.wait_ge(s["maxT_copied"], n + 1)
                        mask_transposes(n + 1, (c + 1) % 2)
                    if hp == 1 and c % 2 == 1:
                        pe.wait_ge(s["maskT_copied"], n + 2)
                        project_qk(par, pair + 2)
                    if hp == 3 and outputs:
                        pe.wait_ge(s["maxT_copied"], n + 2)
                        turn_outputs(r - 3, 2)
                    if hp == 2 and pair_tail and c % 2 == 0:
                        pe.wait_ge(s["xt_split"], pair)
                        router(r - 1 if c == 0 else r, 1 - par)
                    if hp == 2 and outputs:
                        pe.wait_ge(s["y_added"], 4 * (r - 3) + 1)
                        turn_outputs(r - 3, 1)
                    if hp == 3 and outputs:
                        pe.wait_ge(s["y_added"], 4 * (r - 3) + 3)
                        turn_outputs(r - 3, 3)

            def late_step(t, experts, ja, jb):
                tail = t == 4 * ROUNDS
                outputs = turns_outputs(t // 4, t % 4)
                if t == LAST_OUTPUTS:
                    gb = ROUNDS - 1
                    block_down(gb, UNITS - 2)
                    block_down(gb, UNITS - 1)
                    pe.wait_ge(s["y_evac"], 1 + 2 * gb + 2)
                    for half in range(2):
                        if half:
                            pe.wait_ge(s["y_added"], 4 * gb + 2)
                        for q in range(2):
                            for hb in range(2):
                                at = (2 * half + q) * P
                                last = pe.transpose(square(2 * q + hb), yT[:, hb, at:at + P], ident[:, :])
                        last.then_inc(s["yT_T"], 2)
                gb = t // 4 - 3
                for hp in range(4):
                    block, _, before = blocks(t // 4, t % 4, hp, experts)
                    if block:
                        block_gate(*block)
                    if tail and hp == 1:
                        pe.wait_ge(s["y_added"], 4 * (ROUNDS - 4) + 4)
                        turn_attention(NPAIR - 1)
                    if tail and hp == 2:
                        pe.wait_ge(s["x1_done"], NPAIR)
                        turn_xn2(NPAIR - 1)
                    if (t, hp) == (4 * ROUNDS + 1, 0):
                        pe.wait_ge(s["lg_done"], NPAIR)
                        turn_token_weights(NPAIR - 1)
                    if hp == 2 and outputs:
                        pe.wait_ge(s["wrow_ready"], NPAIR)
                        turn_outputs(gb, 0)
                    late_place(ja, jb, hp, 0)
                    if block:
                        block_up(*block)
                    if before:
                        block_down(*before)
                    if tail and hp == 0:
                        times_v(3, B - 1, 3)
                    if hp == 3 and outputs:
                        pe.wait_ge(s["y_added"], 4 * gb + 2)
                        turn_outputs(gb, 2)
                    late_place(ja, jb, hp, 1)
                    if tail and hp == 2:
                        pe.wait_ge(s["xt_split"], NPAIR)
                        router(ROUNDS - 1, 1)
                    if hp == 2 and outputs:
                        pe.wait_ge(s["y_added"], 4 * gb + 1)
                        turn_outputs(gb, 1)
                    if hp == 3 and outputs:
                        pe.wait_ge(s["y_added"], 4 * gb + 3)
                        turn_outputs(gb, 3)
                    late_place(ja, jb, hp, 2)

            schedule(pe, step, late_step)


        @block.vector
        def _(dve):
            st = Steps(dve, s["dve_step"], s["dve_apart"])
            for name in ("up_used", "masked_done", "pv_evac", "gate_used"):
                dve.sem_inc(s[name], 1)
            dve.memset(lnscale[:, :], LN_P_SCALE).then_inc(s["exp_bias_set"], 1)
            dve.wait_ge(s["exp_bias_set"], 1)
            st.link(dve.memset(zero_rows[:, :], 0.0))
            st.link(dve.memset(q_stack[:, :, :, :, :, :], 0.0))

            def norm1_stats(first, last):
                for p in range(first, last):
                    st.link(dve.bn_stats(stats[:, :], x_res[:, p, :]))
                    st.link(dve.bn_aggr(mean_var[:, p, :], stats[:, :]))

            def norm1_var(first, last, done):
                dve.tensor_scalar(rstd[:, first:last], mean_var[:, first:last, 1], EPS, None, ALU.add).then_inc(done, 1)

            dve.wait_ge(s["x01_loaded"], 16)
            norm1_stats(0, 2)
            norm1_var(0, 2, s["ln01_in"])
            dve.wait_ge(s["biasT_ready"], 2)
            dve.tensor_scalar(bias_qs[:, :], psV[:, 0:1], DH ** -0.5, None, ALU.mult).then_inc(s["bias_set"], 1)
            dve.tensor_copy(bias_qk[:, :], psV[:, 0:2]).then_inc(s["bias_set"], 1)
            def norm1(pair, n):
                dve.wait_ge(s["qk_projected"], n)
                if isinstance(n, int) and n < 2:
                    dve.wait_ge(s["pow01_done"], 1)
                if isinstance(n, int) and n == 2:
                    dve.wait_ge(s["pow_done"], 1)
                dve.tensor_scalar(xn[:, :], x_res[:, pair, :], mean_var[:, pair, 0:1],
                                  rstd[:, bass.ds(pair, 1)], ALU.subtract, ALU.mult).then_inc(s["xn_ready"], 1)

            def cut3(dst, src, remain, after):
                st.link(dve.tensor_copy(dst[0], src))
                st.link(dve.tensor_tensor(remain, src, dst[0], ALU.subtract))
                st.link(dve.tensor_copy(dst[1], remain))
                dve.tensor_tensor(dst[2], remain, dst[1], ALU.subtract).then_inc(after, 1)

            def cut_qk(q):
                dve.wait_ge(s["qk_copied"], 2 * q + 2)
                dve.wait_ge(s["parts_stored"], 16 * q)
                dve.wait_ge(s["v_split"], q)
                cut3([parts[:, :, c, :] for c in range(3)], qk32[:, :, :], rem[:, :, :], s["qk_split"])

            def bias_to_v(q):
                dve.wait_ge(s["v_projected"], q + 1)
                dve.wait_ge(s["qk_split"], q + 1)
                vps = psM[:, 0:2 * P].rearrange("p (t c) -> p t c", t=2)
                dve.tensor_tensor(rem[:, :, P:2 * P], vps, bias_v[:, :].unsqueeze(1).broadcast_to([P, 2, P]),
                                  ALU.add).then_inc(s["v_copied"], 1)

            def cut_v(par, q):
                dve.wait_ge(s["v_copied"], q + 1)
                v = rem[:, :, P:2 * P].rearrange("p t (g d) -> p t g d", d=DH)
                r = rem[:, :, 0:P].rearrange("p t (g d) -> p t g d", d=DH)
                dst = [v_parts[:, par, :, :, DH * c:DH * c + DH] for c in range(3)]
                cut3(dst, v, r, s["v_split"])

            def maxima(c, m, i):
                dve.wait_ge(s["scores1_done"], 8 * m + i + 1)
                st.apart()
                for nt in range(2):
                    hp, hh = i // 2, i % 2
                    col = hh * 8 + hp * 2 + nt
                    dve.tensor_tensor_reduce(out=ps1[:, nt, :], in0=ps1[:, nt, :], in1=mask_in[:, c % 2, nt, :],
                                             scale=1.0, scalar=LOW, op0=ALU.add, op1=ALU.max,
                                             accum_out=row_max[:, col:col + 1]).then_inc(s["max_done"], 1)

            def cut_max(m):
                dve.wait_ge(s["max_done"], 16 * m + 16)
                dve.wait_ge(s["maxT_ready"], m)
                rm = row_max[:, :].rearrange("p (g c) -> p g c", g=2)
                rr = max_rem[:, :].rearrange("p (g c) -> p g c", g=2)
                st.link(dve.tensor_scalar(max_parts[:, :, 0, :], rm, -1.0, None, ALU.mult))
                st.link(dve.scalar_tensor_tensor(out=rr, in0=rm, scalar=-1.0, in1=max_parts[:, :, 0, :],
                                                 op0=ALU.mult, op1=ALU.subtract))
                st.link(dve.tensor_copy(max_parts[:, :, 1, :], rr))
                dve.tensor_tensor(max_parts[:, :, 2, :], rr, max_parts[:, :, 1, :], ALU.subtract
                                  ).then_inc(s["max_split"], 1)

            def add_mask(c, n, hp, mt):
                k = 8 * n + 2 * hp + mt
                dve.wait_ge(s["scores2_done"], 1 + k + 1)
                dve.wait_ge(s["plo_done"], k + 1)
                dve.tensor_tensor(p32[:, mt, :].rearrange("p (g n) -> p g n", g=2),
                                  ps2[:, :].rearrange("p (g n) -> p g n", g=2),
                                  maskT[:, c % 2, mt, :].unsqueeze(1).broadcast_to([P, 2, 256]), ALU.add
                                  ).then_inc(s["masked_done"], 1)

            def pv_out(c, n):
                b2 = c % 2
                dve.wait_ge(s["pv_done"], 2 + 4 * n + 4)
                pv = psV[:, 0:2 * H * VC].rearrange("p (g c) -> p g c", c=VC)
                dve.tensor_reduce(o_sum[:, :, :, :].rearrange("p t h d -> p (t h) d"),
                                  pv[:, :, 0:3 * DH].rearrange("p g (c d) -> p g d c", c=3), AX.X, ALU.add)
                dve.reciprocal(o_rec[:, :, :].rearrange("p t h -> p (t h)"), pv[:, :, 3 * DH]
                               ).then_inc(s["pv_evac"], 1)
                dve.wait_ge(s["pv_evac"], 1 + n + 1)
                st.link(dve.tensor_scalar(o_rec[:, :, :], o_rec[:, :, :], gates[:, 0:1], None, ALU.mult))
                dve.tensor_tensor(on[:, :, 64 * b2:64 * b2 + 64].rearrange("p t (h d) -> p t h d", d=DH),
                                  o_sum[:, :, :, :], o_rec[:, :, :].unsqueeze(3).broadcast_to([P, 2, H, DH]),
                                  ALU.mult).then_inc(s["on_ready"], 1)

            def attention_to_x(pair):
                dve.wait_ge(s["onT_ready"], pair + 1)
                dve.tensor_tensor(x_res[:, pair, :], x_res[:, pair, :], psM[:, 0:D], ALU.add
                                  ).then_inc(s["x1_done"], 1)
                dve.wait_ge(s["x1_done"], pair + 1)
                st.apart()
                st.link(dve.bn_stats(stats[:, :], x_res[:, pair, :]))
                st.apart()
                st.link(dve.bn_aggr(mv2[:, :], stats[:, :]))
                dve.tensor_scalar(ve2[:, :], mv2[:, 1:2], EPS, None, ALU.add).then_inc(s["ln_in"], 1)

            def norm2(pair):
                dve.wait_ge(s["pow_done"], pair + 2)
                dve.wait_ge(s["qk_projected"], pair + 3)
                dve.tensor_scalar(xn[:, :], x_res[:, pair, :], mv2[:, 0:1], rstd2[:, 0:1],
                                  ALU.subtract, ALU.mult).then_inc(s["xn2_ready"], 1)

            def x_low(a, u):
                dve.wait_ge(s["xt_hi"], 2 * a + u + 1)
                at = bass.ds((a % 2) * 256 + u * P, P)
                dve.scalar_tensor_tensor(out=xT[:, (a // 2) % 2, 1, :, at],
                                         in0=psM[:, 0:2 * P].rearrange("p (k t) -> p k t", k=KT), scalar=X_SCALE,
                                         in1=xT[:, (a // 2) % 2, 0, :, at], op0=ALU.mult,
                                         op1=ALU.subtract).then_inc(s["xt_split"], 1)

            def logits(pair):
                dve.wait_ge(s["router_done"], pair + 1)
                dve.tensor_reduce(lg[:, :], psM[:, 0:2 * NE].rearrange("p (c e) -> p e c", c=2), AX.X, ALU.add
                                  ).then_inc(s["lg_done"], 1)
                dve.wait_ge(s["lg_done"], pair + 1)
                st.link(dve.tensor_reduce(lmax[:, :], lg[:, :], AX.X, ALU.max, negate=True))
                dve.tensor_scalar(lmax[:, :], lmax[:, :], G_UNSCALE, None, ALU.mult).then_inc(s["logits_done"], 1)

            def route(pair):
                dve.wait_ge(s["route_exp"], pair + 1)
                st.link(dve.reciprocal(lsum[:, :], lsum[:, :]))
                st.link(dve.tensor_scalar(pe_[:, :], pe_[:, :], lsum[:, 0:1], None, ALU.mult))
                pj = pe_[:, :].unsqueeze(1).broadcast_to([P, NE, NE])
                pi = pe_[:, :].unsqueeze(2).broadcast_to([P, NE, NE])
                dve.tensor_tensor(gt[:, :, :], pj, pi, ALU.is_gt)
                st.link(dve.tensor_tensor(ge[:, :, :], pj, pi, ALU.is_equal))
                st.link(dve.tensor_tensor(ge[:, :, :], ge[:, :, :], tri[:, :, :], ALU.mult))
                st.link(dve.tensor_tensor(gt[:, :, :], gt[:, :, :], ge[:, :, :], ALU.add))
                st.link(dve.tensor_tensor(gt[:, :, :], gt[:, :, :], pj, ALU.mult))
                st.link(dve.tensor_reduce(excl[:, :], gt[:, :, :], AX.X, ALU.add))
                st.link(dve.tensor_scalar(keep[:, :], excl[:, :], 0.9, gates[:, 2:3], ALU.is_le, ALU.mult))
                dve.scalar_tensor_tensor(out=tokw[:, :], in0=pe_[:, :], scalar=0.5 * G_UNSCALE * G_UNSCALE,
                                         in1=keep[:, :], op0=ALU.mult, op1=ALU.mult).then_inc(s["w_ready"], 1)

            def token_weight_rows(pair):
                dve.wait_ge(s["wT_ready"], pair + 1)
                dve.wait_ge(s["tokw_stored"], 16 + 16 * pair)
                dve.tensor_copy(wrow[:, :], psM[0:NE, 0:P]).then_inc(s["wrow_ready"], 1)

            def gate_mul(gb, k):
                u = UNITS * gb + k
                dve.wait_ge(s["tanh_done"], u + 1)
                dve.wait_ge(s["up_used"], 1 + u)
                dve.scalar_tensor_tensor(out=ga, in0=th, scalar=1.0, in1=psG[:, :], op0=ALU.add,
                                         op1=ALU.mult).then_inc(s["gate_used"], 1)

            def up_mul(gb, k):
                u = UNITS * gb + k
                dve.wait_ge(s["up_ready"], u + 1)
                dve.wait_ge(s["gate_used"], 1 + u + 1)
                dve.wait_ge(s["h_split"], u + 1)
                dve.tensor_tensor(hb32[:, k % 2, :], psU[:, :], ga, ALU.mult).then_inc(s["up_used"], 1)

            def add_experts(gb, q):
                dve.wait_ge(s["yT_T"], 4 * gb + q + 1)
                row = 4 * (gb // 2) + q
                dve.tensor_tensor(x_res[:, row, :], x_res[:, row, :], psM[:, 0:D],
                                  ALU.add).then_inc(s["y_added"], 1)

            norm1(0, 0)
            cut_qk(0)
            dve.wait_ge(s["small_loaded"], 16 * N_SMALL)
            bias_to_v(0)
            dve.wait_ge(s["stacks_set"], 2)
            cut_v(0, 0)
            norm1(1, 1)
            dve.wait_ge(s["x_loaded"], 16)
            norm1_stats(2, 6)
            cut_qk(1)
            norm1_stats(6, 12)
            dve.wait_ge(s["consts_ready"], 6)
            dve.wait_ge(s["router_T"], 1)
            for k in range(KT):
                st.link(dve.tensor_scalar(w_rt[:, k, 0:NE], psY[:, 0, k * NE:k * NE + NE], W_SCALE, None, ALU.mult))
                st.link(dve.scalar_tensor_tensor(out=w_rt[:, k, NE:2 * NE], in0=psY[:, 0, k * NE:k * NE + NE],
                                                 scalar=W_SCALE, in1=w_rt[:, k, 0:NE], op0=ALU.mult,
                                                 op1=ALU.subtract))
            dve.wait_ge(s["mask0_loaded"], 16)
            for i in range(H):
                maxima(0, 0, i)
                if 1 <= i < 5:
                    norm1_stats(11 + i, 12 + i)
            norm1_var(2, NPAIR, s["ln_in"])
            cut_max(0)
            dve.wait_ge(s["mask1_loaded"], 16)
            for i in range(2):
                maxima(1, 1, i)

            def late_cut(e):
                dve.wait_ge(s[f"d{e % 2}_loaded"], 32 * (e // 2 + 1))
                g_in = d_st[:, e % 2, 0:1024].rearrange("p (t i) -> p t i", t=KT)
                d_in = d_st[:, e % 2, 1024:1536].rearrange("p (t i) -> p t i", t=IB1)
                for src, dst in ((g_in, d_gu), (d_in, d_dn)):
                    st.link(dve.tensor_scalar(dst[:, 0, e, :, :], src, W_SCALE, None, ALU.mult))
                    dve.scalar_tensor_tensor(out=dst[:, 1, e, :, :], in0=src, scalar=W_SCALE, in1=dst[:, 0, e, :, :],
                                             op0=ALU.mult, op1=ALU.subtract).then_inc(s["dw_split"], 2)

            def late_stats(j):
                for u in range(2):
                    st.link(dve.bn_stats(cstat[:, u, :], x_res[:, 2 * j + u, :]))
                for u in range(2):
                    st.link(dve.bn_aggr(cmv[:, u, :], cstat[:, u, :]))
                dve.tensor_scalar(cve[:, :], cmv[:, :, 1], EPS, None, ALU.add).then_inc(s["ln_in"], 1)

            def late_norm(j, i):
                dve.wait_ge(s["pow_done"], 1 + NPAIR + 2 * j + i + 1)
                if i:
                    dve.wait_ge(s["xn3T"], j + 1)
                elif j:
                    dve.wait_ge(s["xn4T"], j)
                for u in range(2):
                    dve.tensor_scalar(xn3[:, u, :], x_res[:, 2 * j + u, :], cmv[:, u, 0:1], crs[:, u:u + 1],
                                      ALU.subtract, ALU.mult).then_inc(s["xn3_ready"], 1)

            def late_masks(j):
                st.link(dve.tensor_tensor(mm[:, :, :], m_u8[:, 2 * j:2 * j + 2, :],
                                          bd[:, :].unsqueeze(1).broadcast_to([P, 2, P]), ALU.mult))
                st.link(dve.tensor_scalar(neg[:, :, :], mm[:, :, :], 1.0, 1.0e30, ALU.subtract, ALU.mult))
                st.link(dve.tensor_reduce(valid[:, :], mm[:, :, :], AX.X, ALU.max))
                st.link(dve.tensor_scalar(valid[:, :], valid[:, :], gates[:, 1:2], None, ALU.mult))

            def late_masked(j):
                dve.wait_ge(s["sc_done"], j + 1)
                st.link(dve.scalar_tensor_tensor(out=sc[:, :, :], in0=psV[:, 0:2 * P].rearrange("p (u t) -> p u t", u=2),
                                                 scalar=D ** -0.5, in1=mm[:, :, :], op0=ALU.mult, op1=ALU.mult))
                st.link(dve.tensor_tensor(sc[:, :, :], sc[:, :, :], neg[:, :, :], ALU.add))
                dve.tensor_reduce(cmax[:, :], sc[:, :, :], AX.X, ALU.max, negate=True).then_inc(s["sc_masked"], 1)

            def late_attend(j):
                dve.wait_ge(s["c_exp"], 2 * j + 2)
                st.link(dve.reciprocal(csum[:, :], csum[:, :]))
                st.link(dve.tensor_tensor(cr[:, :], csum[:, :], valid[:, :], ALU.mult))
                dve.wait_ge(s["read_done"], j + 1)
                for u in range(2):
                    xv = x_res[:, 2 * j + u, :]
                    dve.scalar_tensor_tensor(out=xv, in0=psV[:, u * D:u * D + D], scalar=cr[:, u:u + 1], in1=xv,
                                             op0=ALU.mult, op1=ALU.add).then_inc(s["x3_done"], 1)
                dve.wait_ge(s["x3_done"], 2 * j + 2)

            def late_x_low(j):
                dve.wait_ge(s["xn4_hi"], 2 * j + 2)
                for u in range(2):
                    for k in range(KT):
                        at = (u * KT + k) * P
                        dve.scalar_tensor_tensor(out=x4T[:, 1, k, :, 32 * u:32 * u + 32],
                                                 in0=psV[:, at:at + P].rearrange("p (q e) -> p e q", e=NE1),
                                                 scalar=X_SCALE, in1=x4T[:, 0, k, :, 32 * u:32 * u + 32],
                                                 op0=ALU.mult, op1=ALU.subtract).then_inc(s["xn4_split"], 1)

            def late_mul(j):
                dve.wait_ge(s["d_tanh"], j + 1)
                st.link(dve.scalar_tensor_tensor(out=d_ga, in0=d_th, scalar=1.0,
                                                 in1=ps1[:, :, :].rearrange("p a b -> p (a b)"), op0=ALU.add,
                                                 op1=ALU.mult))
                dve.wait_ge(s["d_upT"], j + 1)
                dve.scalar_tensor_tensor(out=d_h, in0=ps2[:, :], scalar=0.5 * G_UNSCALE * G_UNSCALE,
                                         in1=d_ga, op0=ALU.mult, op1=ALU.mult).then_inc(s["d_mul"], 1)

            def late_out(j):
                if j:
                    dve.wait_ge(s["out_stored"], 16 * j)
                dve.wait_ge(s["d_yT"], j + 1)
                dve.tensor_tensor(xo[:, :, :], ps2[:, :].rearrange("p (u h) -> p u h", u=2), x_res[:, 2 * j:2 * j + 2, :],
                                  ALU.add).then_inc(s["d_out"], 1)

            def step(r, c, tail, pair_tail, experts, weights):
                n, par = 4 * r + c, c // 2
                pair = 2 * r + par
                outputs = turns_outputs(r, c)
                if c == 0:
                    st.enter_round(r)
                for hp in range(4):
                    block, _, _ = blocks(r, c, hp, experts)
                    if pair_tail and (c % 2, hp) == (0, 3):
                        logits(pair - 1)
                    i = (2 * hp + 2) % H
                    cm, m = ((c + 1) % 4, n + 1) if hp < 3 else ((c + 2) % 4, n + 2)
                    if hp == 3:
                        cut_max(n + 1)
                        dve.wait_ge(s[f"mask{c % 2}_loaded"], 16 * ((n + 2) // 2 + 1))
                    maxima(cm, m, i)
                    if hp == 0:
                        dve.wait_ge(s["maskT_copied"], n + 1)
                    add_mask(c, n, hp, 0)
                    if block:
                        gate_mul(*block)
                    if pair_tail and (c % 2, hp) == (1, 0):
                        token_weight_rows(pair - 1)
                    if pair_tail and (c % 2, hp) == (0, 2):
                        x_low(r - 1 if c == 0 else r, 1 - par)
                    if (c % 2, hp) == (0, 0):
                        bias_to_v(pair + 1)
                    if (c % 2, hp) == (1, 0):
                        norm1((pair + 2) % NPAIR, pair + 2)
                    if pair_tail and (c % 2, hp) == (0, 1):
                        attention_to_x(pair - 1)
                    if hp == 2 and outputs:
                        add_experts(r - 3, 0)
                    if (c % 2, hp) == (1, 2):
                        cut_qk(pair + 2)
                    maxima(cm, m, i + 1)
                    add_mask(c, n, hp, 1)
                    if hp == 0 and tail:
                        pv_out((c + 3) % 4, n - 1)
                    if pair_tail and (c % 2, hp) == (0, 1):
                        norm2(pair - 1)
                    if hp == 2 and outputs:
                        add_experts(r - 3, 1)
                    if hp == 3 and outputs:
                        add_experts(r - 3, 2)
                        add_experts(r - 3, 3)
                    if block:
                        up_mul(*block)
                    if (c % 2, hp) == (0, 0):
                        cut_v(1 - par, pair + 1)
                    if pair_tail and (c % 2, hp) == (0, 3):
                        route(pair - 1)

            def late_step(t, experts, ja, jb):
                tail = t == 4 * ROUNDS
                outputs, gb = turns_outputs(t // 4, t % 4), t // 4 - 3
                if tail:
                    st.enter_round(ROUNDS)
                if t == LAST_OUTPUTS:
                    gb = ROUNDS - 1
                    for half in range(2):
                        dve.wait_ge(s["yT_T"], 4 * gb + 2 * half + 2)
                        rows = slice(4 * (gb // 2) + 2 * half, 4 * (gb // 2) + 2 * half + 2)
                        dve.tensor_tensor(x_res[:, rows, :], x_res[:, rows, :],
                                          psM[:, :].rearrange("p (q h) -> p q h", q=2), ALU.add
                                          ).then_inc(s["y_added"], 2)
                        dve.wait_ge(s["y_added"], 4 * gb + 2 * half + 2)
                for hp in range(4):
                    block, _, _ = blocks(t // 4, t % 4, hp, experts)
                    e = CUT_STEP.get(t, {}).get(hp)
                    if e == 0:
                        dve.wait_ge(s["mask_m_loaded"], 16)
                        st.link(dve.tensor_scalar(dy_gate[:, :], gates[:, 3:4], 1.0 / W_SCALE, None, ALU.mult))
                    if e is not None:
                        late_cut(e)
                    if ja is not None and hp == 0:
                        late_stats(ja)
                        late_masks(ja)
                    if jb is not None and hp == 1:
                        late_mul(jb)
                    if ja is not None and hp == 2:
                        late_masked(ja)
                    if tail and hp == 3:
                        logits(NPAIR - 1)
                    if block:
                        gate_mul(*block)
                    if (t, hp) == (4 * ROUNDS + 1, 0):
                        token_weight_rows(NPAIR - 1)
                    if tail and hp == 2:
                        x_low(ROUNDS - 1, 1)
                    if tail and hp == 1:
                        attention_to_x(NPAIR - 1)
                    if hp == 2 and outputs:
                        add_experts(gb, 0)
                    if tail and hp == 3:
                        route(NPAIR - 1)
                    if ja is not None and hp == 0:
                        late_norm(ja, 0)
                    if ja is not None and hp == 3:
                        late_attend(ja)
                        late_stats(ja)
                    if block:
                        up_mul(*block)
                    if tail and hp == 0:
                        pv_out(3, B - 1)
                    if tail and hp == 1:
                        norm2(NPAIR - 1)
                    if ja is not None and hp == 3:
                        late_norm(ja, 1)
                    if hp == 2 and outputs:
                        add_experts(gb, 1)
                    if hp == 3 and outputs:
                        add_experts(gb, 2)
                        add_experts(gb, 3)
                    if jb is not None and hp == 3:
                        late_out(jb)
                    if ja is not None and hp == 3:
                        late_x_low(ja)

            schedule(dve, step, late_step)


_INS = ["x", "ctx_2048", "mask_Bx2048x2048_ff0", "mask_BxS2_bk0", "g_xattn", "g_ffn", "L0_xattn_Wq",
        "L0_xattn_bq", "L0_xattn_Wk", "L0_xattn_bk", "L0_xattn_Wv", "L0_xattn_bv", "L0_ffn_router_w",
        "L0_ffn_gate_w", "L0_ffn_up_w", "L0_ffn_down_w", "L1_ffn_gate_up_proj", "L1_ffn_down_proj"]


def kernel(**inputs):
    import numpy as _np
    import concourse.bacc as _bacc
    from concourse import mybir as _mybir
    from concourse.bass_utils import run_bass_kernel_spmd as _run

    nc = _bacc.Bacc("TRN2", target_bir_lowering=False, num_devices=1)
    arrays, args = {}, {}
    for name in _INS:
        a = _np.ascontiguousarray(inputs[name])
        arrays[f"in_{name}"] = a
        args[name] = nc.dram_tensor(f"in_{name}", a.shape, _mybir.dt.from_np(a.dtype), kind="ExternalInput").ap()
    out = nc.dram_tensor("out_0", (B, S, D), F32, kind="ExternalOutput").ap()
    build(nc, args, out)
    r = _run(nc, [arrays], core_ids=[0])
    return r.results[0]["out_0"]
```
